# Optimizing a Trainium2 kernel written in Bass

```python
import numpy as np
import jax
import jax.numpy as jnp

def _softmax(x, axis=-1):
    return jax.nn.softmax(x, axis=axis)

def _gelu(x):
    return jax.nn.gelu(x, approximate=True)

def _silu(x):
    return jax.nn.silu(x)

def _sigmoid(x):
    return jax.nn.sigmoid(x)

def _layernorm(x, axis=-1, eps=1e-05):
    m = jnp.mean(x, axis=axis, keepdims=True)
    v = jnp.var(x, axis=axis, keepdims=True)
    return (x - m) / jnp.sqrt(v + eps)

def _scatter_add(tgt, idx, src, axis=0):
    return tgt.at[idx].add(src)

def _segment_sum(src, seg, n):
    return jax.ops.segment_sum(src, seg, n)
kernel_name = 'mk_lm_tower_d1_tok_ids512_r4_37d9fa'

def setup_inputs(seed: int=0):
    np.random.seed(seed)
    _w = jnp.asarray

    def _rec_inputs():
        import jax
        import jax.numpy as jnp
        _rk = jax.random.key(seed)
        x = jax.random.randint(jax.random.fold_in(_rk, 1), (8, 1024), 0, 64, jnp.int32)
        return x
    x = _rec_inputs()

    def _L0_tok_setup():
        import jax, jax.numpy as jnp
        import numpy as np
        NGRAM_SIZES = (2, 3, 4)
        HASH_VOCAB = 25000
        EMBED_DIM = 128
        BATCH, SEQ = (8, 1024)

        def _ngram_hash_ids(byte_sequence, n):
            L = byte_sequence.shape[1] - n + 1
            h = jnp.zeros((byte_sequence.shape[0], L), dtype=jnp.int64)
            for j in range(n):
                h = (h * 64 + byte_sequence[:, j:j + L]) % HASH_VOCAB
            return h

        def _ngram_embed(byte_sequence, table, n):
            B, S = byte_sequence.shape
            ids = _ngram_hash_ids(byte_sequence, n)
            emb = table[ids]
            out = jnp.zeros((B, S, table.shape[1]), dtype=table.dtype)
            c = n // 2
            return out.at[:, c:c + emb.shape[1]].set(emb)
        key = jax.random.key(seed)
        ks = jax.random.split(key, 6)
        return {'byte_sequence': jax.random.randint(ks[0], (BATCH, SEQ), 0, 64, dtype=jnp.int64), 'emb_2': jax.random.normal(ks[1], (HASH_VOCAB, EMBED_DIM), dtype=jnp.float32), 'emb_3': jax.random.normal(ks[2], (HASH_VOCAB, EMBED_DIM), dtype=jnp.float32), 'emb_4': jax.random.normal(ks[3], (HASH_VOCAB, EMBED_DIM), dtype=jnp.float32), 'proj_w': jax.random.normal(ks[4], (EMBED_DIM, len(NGRAM_SIZES) * EMBED_DIM), dtype=jnp.float32) * 0.02, 'proj_b': jax.random.normal(ks[5], (EMBED_DIM,), dtype=jnp.float32) * 0.02}
    _L0_tok_all = _L0_tok_setup()
    _L0_tok_in = {k: v for k, v in _L0_tok_all.items() if k in ('emb_2', 'emb_3', 'emb_4', 'proj_w', 'proj_b')}
    del _L0_tok_all

    def _L0_attn_setup():
        import jax, jax.numpy as jnp
        import numpy as np
        import math
        C = 128
        B, T = (8, 512)
        STRIDE = 2
        LN_EPS = 1e-05
        EPS = 1e-08

        def _ln(x, g, b):
            mu = jnp.mean(x, axis=-1, keepdims=True)
            var = jnp.mean(jnp.square(x - mu), axis=-1, keepdims=True)
            return (x - mu) * jax.lax.rsqrt(var + LN_EPS) * g + b

        def _lin(x, w, b):
            return jnp.einsum('btc,oc->bto', x, w) + b

        def _forward(x, dw, db, wq_cr, bq_cr, wk_cr, bk_cr, wv_cr, bv_cr, ln_cr_g, ln_cr_b, wq_d, bq_d, wk_d, bk_d, wv_d, bv_d, ln_d_g, ln_d_b, wq_c, bq_c, wk_c, bk_c, wv_c, bv_c, ln_c_g, ln_c_b, temp, gw, gb):
            scale = 1.0 / math.sqrt(C)
            xc = jnp.transpose(x, (0, 2, 1))
            xd = jax.lax.conv_general_dilated(xc, dw, window_strides=(STRIDE,), padding=[(1, 1)], dimension_numbers=('NCH', 'OIH', 'NCH')) + db[None, :, None]
            x_down = jnp.transpose(xd, (0, 2, 1))
            q = _lin(x, wq_cr, bq_cr)
            k = _lin(x_down, wk_cr, bk_cr)
            v = _lin(x_down, wv_cr, bv_cr)
            a = jax.nn.softmax(jnp.einsum('btc,bsc->bts', q, k) * scale, axis=-1)
            out_cross = _ln(jnp.einsum('bts,bsc->btc', a, v), ln_cr_g, ln_cr_b)
            q = _lin(x, wq_d, bq_d)
            k = _lin(x, wk_d, bk_d)
            v = _lin(x, wv_d, bv_d)
            a = jax.nn.softmax(jnp.einsum('btc,bsc->bts', q, k) * scale, axis=-1)
            out_dot = _ln(jnp.einsum('bts,bsc->btc', a, v), ln_d_g, ln_d_b)
            q = _lin(x, wq_c, bq_c)
            k = _lin(x, wk_c, bk_c)
            qn = q / (jnp.linalg.norm(q, axis=2, keepdims=True) + EPS)
            kn = k / (jnp.linalg.norm(k, axis=2, keepdims=True) + EPS)
            t = jnp.maximum(temp, 0.01)
            a = jax.nn.softmax(jnp.einsum('btc,bsc->bts', qn, kn) / t, axis=-1)
            v = _lin(x, wv_c, bv_c)
            out_cos = _ln(jnp.einsum('bts,bsc->btc', a, v), ln_c_g, ln_c_b)
            fused = jnp.concatenate([out_cross, out_dot, out_cos], axis=-1)
            gate = jax.nn.softmax(jnp.einsum('btc,gc->btg', fused, gw) + gb, axis=-1)
            z = gate[..., 0:1] * out_cross + gate[..., 1:2] * out_dot + gate[..., 2:3] * out_cos
            return z
        key = jax.random.key(seed)
        ks = iter(jax.random.split(key, 40))
        s = 0.02
        d = {'x': jax.random.normal(next(ks), (B, T, C), jnp.float32)}
        d['dw'] = jax.random.normal(next(ks), (C, C, 3), jnp.float32) * s
        d['db'] = jnp.zeros((C,), jnp.float32)
        for br in ('cr', 'd', 'c'):
            for p in ('q', 'k', 'v'):
                d[f'w{p}_{br}'] = jax.random.normal(next(ks), (C, C), jnp.float32) * s
                d[f'b{p}_{br}'] = jnp.zeros((C,), jnp.float32)
            d[f'ln_{br}_g'] = jnp.ones((C,), jnp.float32)
            d[f'ln_{br}_b'] = jnp.zeros((C,), jnp.float32)
        d['temp'] = jnp.asarray(0.1, jnp.float32)
        d['gw'] = jax.random.normal(next(ks), (3, 3 * C), jnp.float32) * s
        d['gb'] = jnp.zeros((3,), jnp.float32)
        return d
    _L0_attn_all = _L0_attn_setup()
    _L0_attn_in = {k: v for k, v in _L0_attn_all.items() if k in ('dw', 'db', 'wq_cr', 'bq_cr', 'wk_cr', 'bk_cr', 'wv_cr', 'bv_cr', 'ln_cr_g', 'ln_cr_b', 'wq_d', 'bq_d', 'wk_d', 'bk_d', 'wv_d', 'bv_d', 'ln_d_g', 'ln_d_b', 'wq_c', 'bq_c', 'wk_c', 'bk_c', 'wv_c', 'bv_c', 'ln_c_g', 'ln_c_b', 'temp', 'gw', 'gb')}
    del _L0_attn_all

    def _L0_ffn_setup():
        import jax, jax.numpy as jnp
        import numpy as np
        NUM_EXPERTS = 32
        GROUP_SIZE = 4
        NUM_GROUPS = NUM_EXPERTS // GROUP_SIZE
        C_CAP = 1.0
        key = jax.random.key(seed)
        ks = jax.random.split(key, 5)
        B, S, H = (16, 512, 128)
        D_FF = int(H * 4 * (2.0 / 3.0))
        x = jax.random.normal(ks[0], (B, S, H), dtype=jnp.float32)
        W_router = jax.random.normal(ks[1], (H, NUM_EXPERTS), dtype=jnp.float32) * (1.0 / np.sqrt(H))
        b_router = jnp.zeros((NUM_EXPERTS,), dtype=jnp.float32)
        W_up = jax.random.normal(ks[2], (NUM_GROUPS, H, D_FF), dtype=jnp.float32) * (1.0 / np.sqrt(H))
        b_up = jnp.zeros((NUM_GROUPS, D_FF), dtype=jnp.float32)
        W_down = jax.random.normal(ks[3], (NUM_EXPERTS, D_FF, H), dtype=jnp.float32) * (1.0 / np.sqrt(D_FF))
        b_down = jnp.zeros((NUM_EXPERTS, H), dtype=jnp.float32)
        return {'x': x, 'W_router': W_router, 'b_router': b_router, 'W_up': W_up, 'b_up': b_up, 'W_down': W_down, 'b_down': b_down}
    _L0_ffn_all = _L0_ffn_setup()
    _L0_ffn_in = {k: v for k, v in _L0_ffn_all.items() if k in ('W_router', 'b_router', 'W_up', 'b_up', 'W_down', 'b_down')}
    del _L0_ffn_all
    return {'x': x, 'L0_tok_emb_2': _L0_tok_in['emb_2'], 'L0_tok_emb_3': _L0_tok_in['emb_3'], 'L0_tok_emb_4': _L0_tok_in['emb_4'], 'L0_tok_proj_w': _L0_tok_in['proj_w'], 'L0_tok_proj_b': _L0_tok_in['proj_b'], 'L0_attn_dw': _L0_attn_in['dw'], 'L0_attn_db': _L0_attn_in['db'], 'L0_attn_wq_cr': _L0_attn_in['wq_cr'], 'L0_attn_bq_cr': _L0_attn_in['bq_cr'], 'L0_attn_wk_cr': _L0_attn_in['wk_cr'], 'L0_attn_bk_cr': _L0_attn_in['bk_cr'], 'L0_attn_wv_cr': _L0_attn_in['wv_cr'], 'L0_attn_bv_cr': _L0_attn_in['bv_cr'], 'L0_attn_ln_cr_g': _L0_attn_in['ln_cr_g'], 'L0_attn_ln_cr_b': _L0_attn_in['ln_cr_b'], 'L0_attn_wq_d': _L0_attn_in['wq_d'], 'L0_attn_bq_d': _L0_attn_in['bq_d'], 'L0_attn_wk_d': _L0_attn_in['wk_d'], 'L0_attn_bk_d': _L0_attn_in['bk_d'], 'L0_attn_wv_d': _L0_attn_in['wv_d'], 'L0_attn_bv_d': _L0_attn_in['bv_d'], 'L0_attn_ln_d_g': _L0_attn_in['ln_d_g'], 'L0_attn_ln_d_b': _L0_attn_in['ln_d_b'], 'L0_attn_wq_c': _L0_attn_in['wq_c'], 'L0_attn_bq_c': _L0_attn_in['bq_c'], 'L0_attn_wk_c': _L0_attn_in['wk_c'], 'L0_attn_bk_c': _L0_attn_in['bk_c'], 'L0_attn_wv_c': _L0_attn_in['wv_c'], 'L0_attn_bv_c': _L0_attn_in['bv_c'], 'L0_attn_ln_c_g': _L0_attn_in['ln_c_g'], 'L0_attn_ln_c_b': _L0_attn_in['ln_c_b'], 'L0_attn_temp': _L0_attn_in['temp'], 'L0_attn_gw': _L0_attn_in['gw'], 'L0_attn_gb': _L0_attn_in['gb'], 'L0_ffn_W_router': _L0_ffn_in['W_router'], 'L0_ffn_b_router': _L0_ffn_in['b_router'], 'L0_ffn_W_up': _L0_ffn_in['W_up'], 'L0_ffn_b_up': _L0_ffn_in['b_up'], 'L0_ffn_W_down': _L0_ffn_in['W_down'], 'L0_ffn_b_down': _L0_ffn_in['b_down']}

def reference(x, L0_tok_emb_2, L0_tok_emb_3, L0_tok_emb_4, L0_tok_proj_w, L0_tok_proj_b, L0_attn_dw, L0_attn_db, L0_attn_wq_cr, L0_attn_bq_cr, L0_attn_wk_cr, L0_attn_bk_cr, L0_attn_wv_cr, L0_attn_bv_cr, L0_attn_ln_cr_g, L0_attn_ln_cr_b, L0_attn_wq_d, L0_attn_bq_d, L0_attn_wk_d, L0_attn_bk_d, L0_attn_wv_d, L0_attn_bv_d, L0_attn_ln_d_g, L0_attn_ln_d_b, L0_attn_wq_c, L0_attn_bq_c, L0_attn_wk_c, L0_attn_bk_c, L0_attn_wv_c, L0_attn_bv_c, L0_attn_ln_c_g, L0_attn_ln_c_b, L0_attn_temp, L0_attn_gw, L0_attn_gb, L0_ffn_W_router, L0_ffn_b_router, L0_ffn_W_up, L0_ffn_b_up, L0_ffn_W_down, L0_ffn_b_down):
    import jax
    import jax.numpy as jnp

    def _L0_tok_ref(byte_sequence, emb_2, emb_3, emb_4, proj_w, proj_b):
        import jax, jax.numpy as jnp
        import numpy as np
        NGRAM_SIZES = (2, 3, 4)
        HASH_VOCAB = 25000
        EMBED_DIM = 128
        BATCH, SEQ = (8, 1024)

        def _ngram_hash_ids(byte_sequence, n):
            L = byte_sequence.shape[1] - n + 1
            h = jnp.zeros((byte_sequence.shape[0], L), dtype=jnp.int64)
            for j in range(n):
                h = (h * 64 + byte_sequence[:, j:j + L]) % HASH_VOCAB
            return h

        def _ngram_embed(byte_sequence, table, n):
            B, S = byte_sequence.shape
            ids = _ngram_hash_ids(byte_sequence, n)
            emb = table[ids]
            out = jnp.zeros((B, S, table.shape[1]), dtype=table.dtype)
            c = n // 2
            return out.at[:, c:c + emb.shape[1]].set(emb)
        tables = (emb_2, emb_3, emb_4)
        combined = jnp.concatenate([_ngram_embed(byte_sequence, t, n) for t, n in zip(tables, NGRAM_SIZES)], axis=-1)
        return jnp.einsum('bsk,dk->bsd', combined, proj_w) + proj_b

    def _L0_attn_ref(x, dw, db, wq_cr, bq_cr, wk_cr, bk_cr, wv_cr, bv_cr, ln_cr_g, ln_cr_b, wq_d, bq_d, wk_d, bk_d, wv_d, bv_d, ln_d_g, ln_d_b, wq_c, bq_c, wk_c, bk_c, wv_c, bv_c, ln_c_g, ln_c_b, temp, gw, gb):
        import jax, jax.numpy as jnp
        import numpy as np
        import math
        C = 128
        B, T = (8, 512)
        STRIDE = 2
        LN_EPS = 1e-05
        EPS = 1e-08

        def _ln(x, g, b):
            mu = jnp.mean(x, axis=-1, keepdims=True)
            var = jnp.mean(jnp.square(x - mu), axis=-1, keepdims=True)
            return (x - mu) * jax.lax.rsqrt(var + LN_EPS) * g + b

        def _lin(x, w, b):
            return jnp.einsum('btc,oc->bto', x, w) + b

        def _forward(x, dw, db, wq_cr, bq_cr, wk_cr, bk_cr, wv_cr, bv_cr, ln_cr_g, ln_cr_b, wq_d, bq_d, wk_d, bk_d, wv_d, bv_d, ln_d_g, ln_d_b, wq_c, bq_c, wk_c, bk_c, wv_c, bv_c, ln_c_g, ln_c_b, temp, gw, gb):
            scale = 1.0 / math.sqrt(C)
            xc = jnp.transpose(x, (0, 2, 1))
            xd = jax.lax.conv_general_dilated(xc, dw, window_strides=(STRIDE,), padding=[(1, 1)], dimension_numbers=('NCH', 'OIH', 'NCH')) + db[None, :, None]
            x_down = jnp.transpose(xd, (0, 2, 1))
            q = _lin(x, wq_cr, bq_cr)
            k = _lin(x_down, wk_cr, bk_cr)
            v = _lin(x_down, wv_cr, bv_cr)
            a = jax.nn.softmax(jnp.einsum('btc,bsc->bts', q, k) * scale, axis=-1)
            out_cross = _ln(jnp.einsum('bts,bsc->btc', a, v), ln_cr_g, ln_cr_b)
            q = _lin(x, wq_d, bq_d)
            k = _lin(x, wk_d, bk_d)
            v = _lin(x, wv_d, bv_d)
            a = jax.nn.softmax(jnp.einsum('btc,bsc->bts', q, k) * scale, axis=-1)
            out_dot = _ln(jnp.einsum('bts,bsc->btc', a, v), ln_d_g, ln_d_b)
            q = _lin(x, wq_c, bq_c)
            k = _lin(x, wk_c, bk_c)
            qn = q / (jnp.linalg.norm(q, axis=2, keepdims=True) + EPS)
            kn = k / (jnp.linalg.norm(k, axis=2, keepdims=True) + EPS)
            t = jnp.maximum(temp, 0.01)
            a = jax.nn.softmax(jnp.einsum('btc,bsc->bts', qn, kn) / t, axis=-1)
            v = _lin(x, wv_c, bv_c)
            out_cos = _ln(jnp.einsum('bts,bsc->btc', a, v), ln_c_g, ln_c_b)
            fused = jnp.concatenate([out_cross, out_dot, out_cos], axis=-1)
            gate = jax.nn.softmax(jnp.einsum('btc,gc->btg', fused, gw) + gb, axis=-1)
            z = gate[..., 0:1] * out_cross + gate[..., 1:2] * out_dot + gate[..., 2:3] * out_cos
            return z
        return _forward(x, dw, db, wq_cr, bq_cr, wk_cr, bk_cr, wv_cr, bv_cr, ln_cr_g, ln_cr_b, wq_d, bq_d, wk_d, bk_d, wv_d, bv_d, ln_d_g, ln_d_b, wq_c, bq_c, wk_c, bk_c, wv_c, bv_c, ln_c_g, ln_c_b, temp, gw, gb)

    def _L0_ffn_ref(x, W_router, b_router, W_up, b_up, W_down, b_down):
        import jax, jax.numpy as jnp
        import numpy as np
        NUM_EXPERTS = 32
        GROUP_SIZE = 4
        NUM_GROUPS = NUM_EXPERTS // GROUP_SIZE
        C_CAP = 1.0
        B, S, H = x.shape
        bs = B * S
        E = NUM_EXPERTS
        k = min(int(bs * C_CAP) // E, bs)
        xf = x.reshape(bs, H)
        h = xf @ W_router + b_router
        Sm = jax.nn.softmax(h, axis=-1)
        G_ek, idx_ek = jax.lax.top_k(Sm.T, k)
        tokens = xf[idx_ek]
        D_FF = W_up.shape[-1]
        tok_g = tokens.reshape(NUM_GROUPS, GROUP_SIZE, k, H)
        up = jnp.einsum('gjkh,ghf->gjkf', tok_g, W_up) + b_up[:, None, None, :]
        act = jax.nn.silu(up).reshape(E, k, D_FF)
        Eout = jnp.einsum('ekf,efh->ekh', act, W_down) + b_down[:, None, :]
        weighted = G_ek[..., None] * Eout
        y = jnp.zeros((bs, H), dtype=x.dtype).at[idx_ek.reshape(-1)].add(weighted.reshape(-1, H))
        return y.reshape(B, S, H)
    h = _L0_tok_ref(x, L0_tok_emb_2, L0_tok_emb_3, L0_tok_emb_4, L0_tok_proj_w, L0_tok_proj_b)
    h = h + _L0_attn_ref(_layernorm(h, axis=-1), L0_attn_dw, L0_attn_db, L0_attn_wq_cr, L0_attn_bq_cr, L0_attn_wk_cr, L0_attn_bk_cr, L0_attn_wv_cr, L0_attn_bv_cr, L0_attn_ln_cr_g, L0_attn_ln_cr_b, L0_attn_wq_d, L0_attn_bq_d, L0_attn_wk_d, L0_attn_bk_d, L0_attn_wv_d, L0_attn_bv_d, L0_attn_ln_d_g, L0_attn_ln_d_b, L0_attn_wq_c, L0_attn_bq_c, L0_attn_wk_c, L0_attn_bk_c, L0_attn_wv_c, L0_attn_bv_c, L0_attn_ln_c_g, L0_attn_ln_c_b, L0_attn_temp, L0_attn_gw, L0_attn_gb)
    h = h + _L0_ffn_ref(_layernorm(h, axis=-1), L0_ffn_W_router, L0_ffn_b_router, L0_ffn_W_up, L0_ffn_b_up, L0_ffn_W_down, L0_ffn_b_down)
    return h

_drawn_inputs = setup_inputs


def setup_inputs(seed=0):
    import zlib

    import numpy as np

    out = dict(_drawn_inputs(seed))
    spreads = {'L0_attn_db': (0.0, 0.1),
     'L0_attn_bq_cr': (0.0, 0.8),
     'L0_attn_bk_cr': (0.0, 2.0),
     'L0_attn_bv_cr': (0.0, 0.1),
     'L0_attn_ln_cr_g': (1.0, 0.2),
     'L0_attn_ln_cr_b': (0.0, 0.1),
     'L0_attn_bq_d': (0.0, 0.8),
     'L0_attn_bk_d': (0.0, 2.0),
     'L0_attn_bv_d': (0.0, 0.1),
     'L0_attn_ln_d_g': (1.0, 0.2),
     'L0_attn_ln_d_b': (0.0, 0.1),
     'L0_attn_bq_c': (0.0, 0.339),
     'L0_attn_bk_c': (0.0, 0.598),
     'L0_attn_bv_c': (0.0, 0.1),
     'L0_attn_ln_c_g': (1.0, 0.2),
     'L0_attn_ln_c_b': (0.0, 0.1),
     'L0_attn_gb': (0.0, 0.1),
     'L0_ffn_b_router': (0.0, 0.5),
     'L0_ffn_b_up': (0.0, 0.8),
     'L0_ffn_b_down': (0.0, 0.525)}
    factors = {'L0_attn_wq_cr': 8.0, 'L0_attn_wk_cr': 8.0, 'L0_attn_wq_d': 5.693, 'L0_attn_wk_d': 5.929}
    for name, (base, spread) in spreads.items():
        noise = np.random.default_rng([zlib.crc32(name.encode()), seed]).standard_normal(out[name].shape)
        drawn = base * np.exp(spread * noise) if base else spread * noise
        out[name] = jnp.asarray(drawn.astype(out[name].dtype))
    for name, factor in factors.items():
        out[name] = (out[name] * factor).astype(out[name].dtype)
    return out
```

```python
from contextlib import ExitStack

import concourse.bass as bass
from concourse import mybir

ALU = mybir.AluOpType
ACT = mybir.ActivationFunctionType
AX_X = mybir.AxisListType.X
F32 = mybir.dt.float32
F32R = mybir.dt.float32r
BF16 = mybir.dt.bfloat16
I32 = mybir.dt.int32

B, S, C = 8, 1024, 128
P = 128
NT = S // P
TOK = B * S
TT = TOK // P
VOCAB = 25000
SD = S // 2
NE, GROUP = 32, 4
NG = NE // GROUP
DFF = 341
FC = 3
FP = (DFF + 1) // FC
TOPK = TOK // NE
HALVES = TOPK // P
LN_EPS = 1e-5
NORM_EPS = 1e-8
SCALE = 1.0 / float(C) ** 0.5
VW = 132
XW = C + NE
BR = 3
UNITS = NT * BR
CHUNKS = P // NE
SEQ_OF_CHUNK = B // CHUNKS
BITS = 30

WCOL, _at = {}, 0
for _name, _width in (("conv", 3 * C), ("q_cr", C), ("k_cr", C), ("q_d", C), ("k_d", C), ("qk_c", 2 * C),
                      ("v_cr", VW), ("v_d", VW), ("v_c", VW)):
    WCOL[_name] = (_at, _at + _width)
    _at += _width
WSPLIT = _at
for _name, _width in (("proj", 3 * C), ("v_nat", 3 * C), ("router", NE)):
    WCOL[_name] = (_at, _at + _width)
    _at += _width
WALL = _at

COL = dict(db=0, bq_cr=1, bk_cr=2, bq_d=3, bk_d=4, ln_g=5, ln_b=8, bv=11, gw=14)
NCOL = 23
ROW, _at = {}, 0
for _name, _width in (("proj_b", C), ("bqk_c", 2 * C), ("bv", 3 * C), ("ln_g", 3 * C), ("ln_b", 3 * C),
                      ("b_router", NE), ("gb", 3), ("temp", 1)):
    ROW[_name] = (_at, _at + _width)
    _at += _width
NROW = _at
CON, _at = {}, 0
for _name, _width in (("ident", P), ("upto", P), ("after", P), ("below", P), ("same", P), ("slot", TOPK),
                      ("slotcol", HALVES)):
    CON[_name] = (_at, _at + _width)
    _at += _width
NCON = _at

USES = ([("gram", "a")] * 6 + [("token", "v")] * 2 + [("xT", "av")] * 2 + [("qk_raw", "v")] * 4 + [("down", "av")]
        + [("q_d", "av")] * 2 + [("k_d", "av")] * 2 + [("q_cr", "av")] * 2 + [("k_cr", "av")]
        + [("v_cr", "av")] * 2 + [("v_dc", "av")] * 8 + [("q_c", "av")] * 2 + [("k_c", "av")] * 2)
NUSE = len(USES)


def first(name):
    return [n for n, _ in USES].index(name)


def reads(engine, k):
    return sum(engine in who for _, who in USES[:k + 1])


A_READS, V_READS = reads("a", NUSE - 1), reads("v", NUSE - 1)


def build_program(nc, x_tok, emb, weights, cols, rows, consts, cand_bits, w_up, b_up, w_down, out):
    table = nc.dram_tensor("token_table", (TOK, XW), F32, kind="Internal").ap()
    with ExitStack() as ctx:
        def sb(name, shape, dt=F32):
            return ctx.enter_context(nc.sbuf_tensor(name, shape, dt))

        def sem(name):
            return ctx.enter_context(nc.semaphore(name))

        attn = ExitStack()

        def asb(name, shape, dt=F32):
            return attn.enter_context(nc.sbuf_tensor(name, shape, dt))

        scores = ctx.enter_context(nc.psum_tensor("scores", [P, 4 * 512], F32))
        turned = ctx.enter_context(nc.psum_tensor("turned", [P, 2 * 512], F32))
        mixed = ctx.enter_context(nc.psum_tensor("mixed", [P, 2 * 512], F32))

        con = sb("con", [P, NCON])
        prob = sb("prob", [P, TT, NE])
        ones_row = sb("ones_row", [1, P])

        w = asb("w", [P, WALL])
        w_hi = asb("w_hi", [P, WSPLIT], F32R)
        w_lo = asb("w_lo", [P, WSPLIT], F32R)
        col = asb("col", [P, NCOL])
        row = asb("row", [P, NROW])
        gate_w = asb("gate_w", [P, 9])
        gate_mean = asb("gate_mean", [P, 9])
        gate_const = asb("gate_const", [P, 3])
        wide = asb("wide", [P, 6, C])
        mean_w = asb("mean_w", [P, P])
        bv_ext = asb("bv_ext", [P, 3 * VW])
        bv_hi = asb("bv_hi", [1, 3 * VW], F32R)
        bv_lo = asb("bv_lo", [1, 3 * VW], F32R)
        one_row = asb("one_row", [1, P], F32R)
        inv_temp = asb("inv_temp", [P, 1])
        m_half = asb("m_half", [P, 16])
        p_half = asb("p_half", [P, 16])

        xw = asb("xw", [TT, P + 3])
        xwi = asb("xwi", [TT, P + 3], I32)
        hashed = asb("hashed", [TT, 3, P])
        quot = asb("quot", [TT, P])
        quot_i = asb("quot_i", [TT, P], I32)
        ids = asb("ids", [P, B, NT, 3], I32)
        ids_now = asb("ids_now", [P, NT * 3], I32)

        gram = asb("gram", [P, NT, 3, C])
        gramT = asb("gramT", [P, 3, S])
        h = asb("h", [P, 2 * NT, C])
        st1 = asb("st1", [P, NT, 6])
        mv1 = asb("mv1", [P, NT, 2])
        rstd1 = asb("rstd1", [P, NT])
        xn = asb("xn", [P, NT, C])
        xT_hi = asb("xT_hi", [P, S + 2], F32R)
        xT_lo = asb("xT_lo", [P, S + 2], F32R)
        square = xn[:].bitcast(BF16)
        norm = asb("norm", [P, NT * 2])
        inv_norm = asb("inv_norm", [P, NT * 2])
        down_hi = asb("down_hi", [P, SD], F32R)
        down_lo = asb("down_lo", [P, SD], F32R)
        q_hi = [asb(f"q_hi{i}", [P, S], F32R) for i in range(BR)]
        q_lo = [asb(f"q_lo{i}", [P, S], F32R) for i in range(BR)]
        k_hi = [asb(f"k_hi{i}", [P, S if i else SD], F32R) for i in range(BR)]
        k_lo = [asb(f"k_lo{i}", [P, S if i else SD], F32R) for i in range(BR)]
        v0_hi = asb("v0_hi", [P, SD // P, VW], F32R)
        v0_lo = asb("v0_lo", [P, SD // P, VW], F32R)
        v12_hi = asb("v12_hi", [P, NT, 2 * VW], F32R)
        v12_lo = asb("v12_lo", [P, NT, 2 * VW], F32R)

        neg_max = asb("neg_max", [P, 4])
        exp_sum = asb("exp_sum", [P, 4, BR])
        probs = asb("probs", [P, 2, S])
        qk_raw = probs[:].rearrange("p a (t c) -> p (a t) c", c=2 * C)
        pT_hi = asb("pT_hi", [P, 2, S], F32R)
        pT_lo = asb("pT_lo", [P, 2, S], F32R)

        st = asb("st", [P, 2, BR, 6])
        mv = asb("mv", [P, 2, BR, 2])
        og = asb("og", [P, 2, BR, 3])
        sum_sq = asb("sum_sq", [P, 2, BR])
        var_eps = asb("var_eps", [P, 2, BR])
        rstd = asb("rstd", [P, 2, BR])
        logit9 = asb("logit9", [P, 2, 3, BR])
        logit_s = asb("logit_s", [P, 2, 3])
        logit = asb("logit", [P, 2, 3])
        logit_nm = asb("logit_nm", [P, 2])
        gate_e = asb("gate_e", [P, 2, 3])
        gate_sum = asb("gate_sum", [P, 2])
        gate_inv = asb("gate_inv", [P, 2])
        gate = asb("gate", [P, 2, 3])
        gate_r = asb("gate_r", [P, 2, 3])
        gate_b = asb("gate_b", [P, 2, 3])
        u = asb("u", [P, 2, BR, C])
        zb = asb("zb", [P, 2, BR, C])
        h1 = asb("h1", [P, NT, C])
        st2 = asb("st2", [P, 2, 6])
        mv2 = asb("mv2", [P, 2, 2])
        ve2 = asb("ve2", [P, 2])
        rstd2 = asb("rstd2", [P, 2])
        trow = asb("trow", [P, NT, XW])
        x2T = w[:, 0:S]
        r_log, r_sub, r_exp = (wide[:, 2 * i:2 * i + 2, :].rearrange("p a (t e) -> p (a t) e", e=NE) for i in range(3))
        r_nm = asb("r_nm", [P, NT])
        r_sum = asb("r_sum", [P, NT])
        r_inv = asb("r_inv", [P, NT])

        loaded = sem("loaded")
        tok_loaded = sem("tok_loaded")
        setup_v = sem("setup_v")
        setup_t = sem("setup_t")
        setup_g = sem("setup_g")
        ids_ready = sem("ids_ready")
        ids_turned = sem("ids_turned")
        weights_ready = sem("weights_ready")
        staged = sem("staged")
        gathered = sem("gathered")
        bank_full = sem("bank_full")
        bank_a = sem("bank_a")
        bank_v = sem("bank_v")
        edges = sem("edges")
        ln1_stats = sem("ln1_stats")
        ln1_mv = sem("ln1_mv")
        ln1_g = sem("ln1_g")
        ln1_rstd = sem("ln1_rstd")
        x_ready = sem("x_ready")
        sq_ready = sem("sq_ready")
        norm_g = sem("norm_g")
        norm_v = sem("norm_v")
        qk_ready = sem("qk_ready")
        scored = sem("scored")
        maxed = sem("maxed")
        exped = sem("exped")
        turn_done = sem("turn_done")
        hi_done = sem("hi_done")
        lo_done = sem("lo_done")
        pv_done = sem("pv_done")
        o_stats = sem("o_stats")
        o_mv = sem("o_mv")
        rstd_g = sem("rstd_g")
        rstd_ok = sem("rstd_ok")
        logit_c = sem("logit_c")
        logit_ok = sem("logit_ok")
        gate_ok = sem("gate_ok")
        gate_c = sem("gate_c")
        scale_ok = sem("scale_ok")
        u_ok = sem("u_ok")
        z_g = sem("z_g")
        h1_ok = sem("h1_ok")
        st2_ok = sem("st2_ok")
        mv2_ok = sem("mv2_ok")
        ve2_ok = sem("ve2_ok")
        rstd2_ok = sem("rstd2_ok")
        x2_ok = sem("x2_ok")
        x2_turned = sem("x2_turned")
        x2T_ok = sem("x2T_ok")
        routed = sem("routed")
        route_v = sem("route_v")
        route_e = sem("route_e")
        prob_ok = sem("prob_ok")
        prob_kept = sem("prob_kept")
        h1_stored = sem("h1_stored")
        row_stored = sem("row_stored")
        h1_free = sem("h1_free")
        rows_free = sem("rows_free")

        def W(name, a=0, n=None):
            lo, hi = WCOL[name]
            return w[:, lo + a:(lo + a + n if n else hi)]

        def split(name, a=0, n=None):
            lo, hi = WCOL[name]
            hi = lo + a + n if n else hi
            return w_hi[:, lo + a:hi], w_lo[:, lo + a:hi]

        def R(name):
            return row[:, ROW[name][0]:ROW[name][1]]

        def K(name):
            return con[:, CON[name][0]:CON[name][1]]

        ident = K("ident")

        def bank(k):
            return scores[:, (k % 4) * 512:(k % 4 + 1) * 512]

        def mixed_of(t):
            return mixed[:, (t % 2) * 512:(t % 2) * 512 + BR * VW]

        tokens_out = out.rearrange("b (t p) c -> p (b t) c", p=P)
        table_out = table.rearrange("(t p) x -> p t x", p=P)

        first_part = nc.Block()
        block = first_part.__enter__()


        @block.sync
        def _(sp):
            xf = x_tok.rearrange("b (t p) -> (b t) p", p=P)
            sp.wait_ge(setup_g, 1)
            sp.dma_start(xwi[:, 2:P + 2], xf).then_inc(tok_loaded, 16)
            sp.dma_start(xwi[1:TT, 0:2], xf[0:TT - 1, P - 2:P]).then_inc(tok_loaded, 16)
            sp.dma_start(xwi[0:TT - 1, P + 2:P + 3], xf[1:TT, 0:1], allow_slow_non_contiguous=True).then_inc(tok_loaded, 16)
            sp.dma_start(con[:], consts).then_inc(loaded, 16)
            sp.dma_start(row[:], rows).then_inc(loaded, 16)
            sp.dma_start(col[:], cols).then_inc(loaded, 16)
            sp.dma_start(w[:], weights).then_inc(loaded, 16)

            sp.nop().then_inc(h1_free, 1)
            sp.nop().then_inc(rows_free, 1)
            with sp.Fori(0, B) as b:
                sp.wait_ge(h1_ok, b * NT + NT)
                sp.dma_start(tokens_out[:, bass.ds(b * NT, NT), :], h1[:]).then_inc(h1_stored, 16)
                sp.wait_ge(prob_ok, b + 1)
                sp.dma_start(table_out[:, bass.ds(b * NT, NT), :], trow[:]).then_inc(row_stored, 16)
                sp.wait_ge(h1_stored, 16 * b + 16)
                sp.nop().then_inc(h1_free, 1)
                sp.wait_ge(row_stored, 16 * b + 16)
                sp.nop().then_inc(rows_free, 1)

        @block.tensor
        def _(pe):
            def product(dst, lhs, rhs, first_one=True, last_one=True):
                pe.matmul(dst, lhs[0], rhs[0], start=first_one, stop=False)
                pe.matmul(dst, lhs[0], rhs[1], start=False, stop=False)
                return pe.matmul(dst, lhs[1], rhs[0], start=False, stop=last_one)

            def setup():
                pe.wait_ge(loaded, 64)
                pe.wait_ge(ids_ready, 1)
                for g in range(3):
                    last = pe.transpose(turned[:, g * TT:(g + 1) * TT], hashed[:, g, :], ident[0:TT, 0:TT])
                last.then_inc(ids_turned, 1)
                pe.wait_ge(setup_g, 7)
                pe.wait_ge(setup_v, 3)
                pe.matmul(bank(0)[:, 0:9], mean_w[:], gate_w[:], start=True, stop=True).then_inc(setup_t, 1)
                pe.wait_ge(setup_v, 7)
                for i in range(BR):
                    pe.matmul(bank(1)[:, 3 * i:3 * i + 3], W("v_nat", i * C, C), gate_w[:, 3 * i:3 * i + 3],
                              start=True, stop=True)
                for i in range(BR):
                    pe.matmul(bank(2)[:, 3 * i:3 * i + 3], wide[:, i, :], gate_w[:, 3 * i:3 * i + 3],
                              start=True, stop=True)
                for i in range(BR):
                    last = pe.matmul(bank(3)[:, 0:3], wide[:, 3 + i, :], col[:, COL["gw"] + 3 * i:COL["gw"] + 3 * i + 3],
                                     start=(i == 0), stop=(i == BR - 1))
                last.then_inc(setup_t, 1)
                pe.wait_ge(weights_ready, 2)

            def open_bank(b, k, high_of=-1, low_of=-1):
                if k < 4 and (not isinstance(b, int) or b > 0):
                    pe.wait_ge(exped, b * UNITS)
                who = USES[k - 4][1] if k >= 4 else ""
                a_count = max(reads("a", k - 4) if "a" in who else 0, reads("a", high_of) if high_of >= 0 else 0)
                v_count = max(reads("v", k - 4) if "v" in who else 0, reads("v", low_of) if low_of >= 0 else 0)
                if a_count:
                    pe.wait_ge(bank_a, b * A_READS + a_count)
                if v_count:
                    pe.wait_ge(bank_v, b * V_READS + v_count)

            def prologue(b, tail):
                pe.wait_ge(gathered, (b + 1) * (NT * 3 * 16))
                for k in range(6):
                    n, half = k // 2, k % 2
                    open_bank(b, k)
                    for j in range(4):
                        last = pe.transpose(bank(k)[:, j * P:(j + 1) * P], gram[:, half * 4 + j, n, :], ident)
                    last.then_inc(bank_full, 1)
                for half in range(2):
                    k = first("token") + half
                    open_bank(b, k, high_of=4 + half)
                    pe.wait_ge(edges, b * 5 + 5)
                    for j in range(4):
                        t = half * 4 + j
                        for n in range(3):
                            last = pe.matmul(bank(k)[:, j * C:(j + 1) * C], gramT[:, n, t * P:(t + 1) * P],
                                             W("proj", n * C, C), start=(n == 0), stop=(n == 2))
                    last.then_inc(bank_full, 1)
                for half in range(2):
                    k = first("xT") + half
                    open_bank(b, k)
                    pe.wait_ge(x_ready, b * NT + half * 4 + 4)
                    for j in range(4):
                        last = pe.transpose(bank(k)[:, j * P:(j + 1) * P], xn[:, half * 4 + j, :], ident)
                    last.then_inc(bank_full, 1)

                def xT_tile(t):
                    return xT_hi[:, 2 + t * P:2 + (t + 1) * P], xT_lo[:, 2 + t * P:2 + (t + 1) * P]

                def xT_half(half):
                    return xT_hi[:, 2 + half * 512:514 + half * 512], xT_lo[:, 2 + half * 512:514 + half * 512]

                for i in range(4):
                    k = first("qk_raw") + i
                    open_bank(b, k, first("xT") + i // 2, first("xT") + i // 2)
                    for j in range(2):
                        last = product(bank(k)[:, j * 2 * C:(j + 1) * 2 * C], xT_tile(2 * i + j), split("qk_c"))
                    last.then_inc(bank_full, 1)
                k = first("down")
                open_bank(b, k)
                for tap in range(3):
                    last = product(bank(k), split("conv", tap * C, C),
                                   (xT_hi[:, tap + 1:tap + 1 + S - 1:2], xT_lo[:, tap + 1:tap + 1 + S - 1:2]),
                                   tap == 0, tap == 2)
                last.then_inc(bank_full, 1)
                for name in ("q_d", "k_d", "q_cr"):
                    for half in range(2):
                        k = first(name) + half
                        open_bank(b, k)
                        product(bank(k), split(name), xT_half(half)).then_inc(bank_full, 1)
                k = first("k_cr")
                open_bank(b, k, first("down"), first("down"))
                product(bank(k), split("k_cr"), (down_hi[:], down_lo[:])).then_inc(bank_full, 1)
                for i in range(2):
                    k = first("v_cr") + i
                    open_bank(b, k)
                    for j in range(2):
                        t = 2 * i + j
                        dst = bank(k)[:, j * VW:(j + 1) * VW]
                        pe.matmul(dst, one_row[:], bv_hi[:, 0:VW], start=True, stop=False)
                        pe.matmul(dst, one_row[:], bv_lo[:, 0:VW], start=False, stop=False)
                        last = product(dst, (down_hi[:, t * P:(t + 1) * P], down_lo[:, t * P:(t + 1) * P]),
                                       split("v_cr"), False)
                    last.then_inc(bank_full, 1)
                if tail is not None:
                    pe.wait_ge(x2_ok, tail * NT + NT)
                    pe.wait_ge(lo_done, tail * UNITS + UNITS)
                    route_turn()
                for t in range(NT):
                    k = first("v_dc") + t
                    open_bank(b, k)
                    dst = bank(k)[:, 0:2 * VW]
                    pe.matmul(dst, one_row[:], bv_hi[:, VW:3 * VW], start=True, stop=False)
                    pe.matmul(dst, one_row[:], bv_lo[:, VW:3 * VW], start=False, stop=False)
                    w0, w1 = WCOL["v_d"][0], WCOL["v_c"][1]
                    product(dst, xT_tile(t), (w_hi[:, w0:w1], w_lo[:, w0:w1]), False).then_inc(bank_full, 1)
                if tail is not None:
                    pe.wait_ge(u_ok, tail * NT + NT - 1)
                    route_product(tail)
                for which, name in enumerate(("q_c", "k_c")):
                    for half in range(2):
                        k = first(name) + half
                        open_bank(b, k)
                        pe.wait_ge(qk_ready, b * 2 + half + 1)
                        for j in range(4):
                            last = pe.transpose(bank(k)[:, j * P:(j + 1) * P],
                                                qk_raw[:, half * 4 + j, which * C:(which + 1) * C], ident)
                        last.then_inc(bank_full, 1)
                if tail is not None:
                    pe.wait_ge(u_ok, tail * NT + NT)
                    pe.wait_ge(route_v, tail * 5 + 1)

            def route_turn():
                for t in range(NT):
                    last = pe.transpose(turned[:, t * P:(t + 1) * P], trow[:, t, 0:C], ident)
                last.then_inc(x2_turned, 1)

            def route_product(b):
                pe.wait_ge(x2T_ok, b + 1)
                for t in range(NT):
                    last = pe.matmul(mixed[:, t * NE:(t + 1) * NE], x2T[:, t * P:(t + 1) * P], W("router"),
                                     start=True, stop=True)
                last.then_inc(routed, 1)

            def attention(b):
                def turn(i):
                    pe.wait_ge(exped, b * UNITS + i + 1)
                    if i >= 1:
                        pe.wait_ge(lo_done, b * UNITS + i)
                    for j in range((SD if i % BR == 0 else S) // P):
                        last = pe.transpose(turned[:, j * P:(j + 1) * P], probs[:, i % 2, j * P:(j + 1) * P], ident)
                    last.then_inc(turn_done, 1)

                def score(i):
                    t, br = i // BR, i % BR
                    if i >= 2:
                        pe.wait_ge(exped, b * UNITS + i - 1)
                    else:
                        pe.wait_ge(bank_a, b * A_READS + A_READS)
                        pe.wait_ge(bank_v, b * V_READS + V_READS)
                    lhs = q_hi[br][:, t * P:(t + 1) * P], q_lo[br][:, t * P:(t + 1) * P]
                    for half in range(1 if br == 0 else 2):
                        at = (i % 2) * S + half * 512
                        last = product(scores[:, at:at + 512], lhs, (k_hi[br][:, half * 512:(half + 1) * 512],
                                                                     k_lo[br][:, half * 512:(half + 1) * 512]))
                    last.then_inc(scored, 1)

                def mix(i):
                    t, br = i // BR, i % BR
                    pe.wait_ge(hi_done, b * UNITS + i + 1)
                    pe.wait_ge(lo_done, b * UNITS + i + 1)
                    if br == 0 and t >= 2:
                        pe.wait_ge(u_ok, b * NT + t - 1)
                    n = (SD if br == 0 else S) // P
                    for j in range(n):
                        vals = ((v0_hi[:, j, :], v0_lo[:, j, :]) if br == 0 else
                                (v12_hi[:, j, (br - 1) * VW:br * VW], v12_lo[:, j, (br - 1) * VW:br * VW]))
                        last = product(mixed_of(t)[:, br * VW:(br + 1) * VW],
                                       (pT_hi[:, i % 2, j * P:(j + 1) * P], pT_lo[:, i % 2, j * P:(j + 1) * P]),
                                       vals, j == 0, j == n - 1)
                    last.then_inc(pv_done, 1)

                for i in range(UNITS + 3):
                    if 0 <= i - 2 < UNITS:
                        turn(i - 2)
                    if i < UNITS:
                        score(i)
                    if 0 <= i - 3 < UNITS:
                        mix(i - 3)

            setup()
            prologue(0, None)
            with pe.Fori(0, B - 1) as b:
                attention(b)
                prologue(b + 1, b)
            attention(B - 1)
            pe.wait_ge(x2_ok, TT)
            pe.wait_ge(lo_done, B * UNITS)
            route_turn()
            pe.wait_ge(u_ok, TT)
            route_product(B - 1)

        @block.vector
        def _(dve):
            def setup():
                n = [0]

                def step(ins):
                    n[0] += 1
                    ins.then_inc(setup_v, 1)

                dve.wait_ge(loaded, 64)
                for i in range(BR):
                    step(dve.tensor_scalar(gate_w[:, 3 * i:3 * i + 3], col[:, COL["gw"] + 3 * i:COL["gw"] + 3 * i + 3],
                                           col[:, COL["ln_g"] + i:COL["ln_g"] + i + 1], None, ALU.mult))
                dve.wait_ge(setup_t, 1)
                step(dve.tensor_copy(gate_mean[:], bank(0)[:, 0:9]))
                dve.wait_ge(setup_v, 4)
                step(dve.tensor_tensor(gate_w[:], gate_w[:], gate_mean[:], ALU.subtract))
                dve.wait_ge(setup_g, 7)
                for i in range(BR):
                    dve.tensor_scalar(wide[:, i, :], wide[:, i, :], col[:, COL["bv"] + i:COL["bv"] + i + 1], None, ALU.add)
                    last = dve.tensor_scalar(wide[:, 3 + i, :], wide[:, 3 + i, :],
                                             col[:, COL["ln_b"] + i:COL["ln_b"] + i + 1], None, ALU.add)
                step(last)
                step(dve.tensor_scalar(inv_temp[:], R("temp"), 0.01, None, ALU.max))
                for name in ("q_cr", "q_d"):
                    dve.tensor_scalar(W(name), W(name), SCALE, None, ALU.mult)
                    last = dve.tensor_scalar(col[:, COL["b" + name]:COL["b" + name] + 1],
                                             col[:, COL["b" + name]:COL["b" + name] + 1], SCALE, None, ALU.mult)
                step(last)
                dve.wait_ge(setup_v, 8)
                step(dve.reciprocal(inv_temp[:], inv_temp[:]))
                for i in range(BR):
                    dve.tensor_copy(bv_ext[:, i * VW:i * VW + C], R("bv")[:, i * C:(i + 1) * C])
                    dve.memset(bv_ext[:, i * VW + C + 3:(i + 1) * VW], 0.0)
                dve.wait_ge(setup_t, 2)
                for i, name in enumerate(("v_cr", "v_d", "v_c")):
                    dve.tensor_copy(W(name, C, 3), bank(1)[:, 3 * i:3 * i + 3])
                    last = dve.tensor_copy(bv_ext[:, i * VW + C:i * VW + C + 3], bank(2)[:, 3 * i:3 * i + 3])
                step(last)
                step(dve.tensor_tensor(gate_const[:], bank(3)[:, 0:3], R("gb"), ALU.add))
                dve.wait_ge(setup_v, 11)
                dve.tensor_copy(w_hi[:], w[:, 0:WSPLIT])
                step(dve.tensor_copy(bv_hi[:], bv_ext[0:1, :]))
                dve.wait_ge(setup_v, 12)
                dve.tensor_tensor(w_lo[:], w[:, 0:WSPLIT], w_hi[:].bitcast(F32), ALU.subtract)
                dve.tensor_tensor(bv_lo[:], bv_ext[0:1, :], bv_hi[:].bitcast(F32), ALU.subtract).then_inc(weights_ready, 1)
                dve.wait_ge(setup_g, 7)
                dve.tensor_copy(one_row[:], ones_row[:]).then_inc(weights_ready, 1)

            def hashes():
                n = [0]

                def step(ins):
                    n[0] += 1
                    ins.then_inc(norm_v, 1)
                    dve.wait_ge(norm_v, n[0])

                dve.wait_ge(tok_loaded, 48)
                step(dve.tensor_copy(xw[:], xwi[:]))

                def modulo(v):
                    step(dve.tensor_scalar(quot[:], v, 1.0 / VOCAB, None, ALU.mult))
                    step(dve.tensor_copy(quot_i[:], quot[:]))
                    step(dve.tensor_copy(quot[:], quot_i[:]))
                    step(dve.scalar_tensor_tensor(out=v, in0=quot[:], scalar=-float(VOCAB), in1=v,
                                                  op0=ALU.mult, op1=ALU.add))
                    step(dve.tensor_scalar(quot[:], v, 0.0, float(VOCAB), ALU.is_lt, ALU.mult))
                    step(dve.tensor_tensor(v, v, quot[:], ALU.add))
                    step(dve.tensor_scalar(quot[:], v, float(VOCAB), -float(VOCAB), ALU.is_ge, ALU.mult))
                    step(dve.tensor_tensor(v, v, quot[:], ALU.add))

                for g, start in enumerate((1, 1, 0)):
                    v = hashed[:, g, :]
                    step(dve.tensor_copy(v, xw[:, start:start + P]))
                    for j in range(1, g + 2):
                        step(dve.tensor_scalar(v, v, 64.0, None, ALU.mult))
                        step(dve.tensor_tensor(v, v, xw[:, start + j:start + j + P], ALU.add))
                        modulo(v)
                dve.engine_nop().then_inc(ids_ready, 1)
                dve.wait_ge(ids_turned, 1)
                for g in range(3):
                    last = dve.tensor_copy(ids[:].rearrange("p b t g -> p (b t) g")[:, :, g],
                                           turned[:, g * TT:(g + 1) * TT])
                last.then_inc(ids_ready, 1)
                return n[0]

            NORM0 = [0]

            def low(b, k, dst, src, hi):
                dve.wait_ge(bank_full, b * NUSE + k + 1)
                dve.wait_ge(bank_a, b * A_READS + reads("a", k))
                dve.tensor_tensor(dst, src, hi.bitcast(F32), ALU.subtract).then_inc(bank_v, 1)

            def low_bias(b, k, dst, src, bias, hi):
                dve.wait_ge(bank_full, b * NUSE + k + 1)
                dve.wait_ge(bank_a, b * A_READS + reads("a", k))
                dve.scalar_tensor_tensor(out=dst, in0=src, scalar=bias, in1=hi.bitcast(F32), op0=ALU.add,
                                         op1=ALU.subtract).then_inc(bank_v, 1)

            def prologue(b, tail):
                for half in range(2):
                    k = first("token") + half
                    dve.wait_ge(bank_full, b * NUSE + k + 1)
                    dve.tensor_tensor(h[:, bass.ds((b % 2) * NT + half * 4, 4), :],
                                      bank(k).rearrange("p (t c) -> p t c", c=C),
                                      R("proj_b").unsqueeze(1).to_broadcast([P, 4, C]), ALU.add).then_inc(bank_v, 1)
                dve.wait_ge(bank_v, b * V_READS + 2)
                dve.nop(nofuse=True)
                for t in range(NT):
                    last = dve.bn_stats(st1[:, t, :], h[:, bass.ds((b % 2) * NT + t, 1), :])
                last.then_inc(ln1_stats, 1)
                dve.wait_ge(ln1_stats, b + 1)
                dve.nop(nofuse=True)
                for t in range(NT):
                    last = dve.bn_aggr(mv1[:, t, :], st1[:, t, :])
                last.then_inc(ln1_mv, 1)
                if tail is not None:
                    tile_gate_logits(tail, NT - 1)
                    tile_x2(tail, NT - 2)
                dve.wait_ge(ln1_rstd, b + 1)
                for t in range(NT):
                    dve.tensor_scalar(xn[:, t, :], h[:, bass.ds((b % 2) * NT + t, 1), :], mv1[:, t, 0:1], rstd1[:, t:t + 1],
                                      ALU.subtract, ALU.mult).then_inc(x_ready, 1)
                if tail is not None:
                    tile_gate(tail, NT - 1)
                for half in range(2):
                    k = first("xT") + half
                    at = slice(2 + half * 512, 514 + half * 512)
                    low(b, k, xT_lo[:, at], bank(k), xT_hi[:, at])
                for i in range(4):
                    k = first("qk_raw") + i
                    dve.wait_ge(bank_full, b * NUSE + k + 1)
                    dve.tensor_tensor(qk_raw[:, 2 * i:2 * i + 2, :], bank(k).rearrange("p (t c) -> p t c", c=2 * C),
                                      R("bqk_c").unsqueeze(1).to_broadcast([P, 2, 2 * C]), ALU.add).then_inc(bank_v, 1)
                if tail is not None:
                    tile_h1_stats(tail, NT - 1)
                low_bias(b, first("down"), down_lo[:], bank(first("down")), col[:, COL["db"]:COL["db"] + 1], down_hi[:])
                for br, which, name in ((1, q_lo, "q_d"), (1, k_lo, "k_d"), (0, q_lo, "q_cr")):
                    for half in range(2):
                        k = first(name) + half
                        at = slice(half * 512, half * 512 + 512)
                        hi = (q_hi if which is q_lo else k_hi)[br][:, at]
                        low_bias(b, k, which[br][:, at], bank(k), col[:, COL["b" + name]:COL["b" + name] + 1], hi)
                    if tail is not None and name == "q_d":
                        tile_x2(tail, NT - 1)
                low_bias(b, first("k_cr"), k_lo[0][:], bank(first("k_cr")), col[:, COL["bk_cr"]:COL["bk_cr"] + 1],
                         k_hi[0][:])
                n0 = NORM0[0]
                dve.wait_ge(norm_g, b * 2 + 2)
                dve.reciprocal(inv_norm[:], norm[:]).then_inc(norm_v, 1)
                dve.wait_ge(norm_v, n0 + b * 2 + 1)
                dve.tensor_scalar(inv_norm[:, 0:2 * NT:2], inv_norm[:, 0:2 * NT:2], inv_temp[:, 0:1], None,
                                  ALU.mult).then_inc(norm_v, 1)
                dve.wait_ge(norm_v, n0 + b * 2 + 2)
                for half in range(2):
                    part = qk_raw[:, half * 4:half * 4 + 4, :].rearrange("p t (w c) -> p (t w) c", c=C)
                    dve.tensor_tensor(part, part, inv_norm[:, half * 8:half * 8 + 8].unsqueeze(2).to_broadcast([P, 8, C]),
                                      ALU.mult).then_inc(qk_ready, 1)
                for i in range(2):
                    k = first("v_cr") + i
                    low(b, k, v0_lo[:, 2 * i:2 * i + 2, :], bank(k)[:, 0:2 * VW].rearrange("p (t c) -> p t c", c=VW),
                        v0_hi[:, 2 * i:2 * i + 2, :])
                for t in range(NT):
                    k = first("v_dc") + t
                    low(b, k, v12_lo[:, t, :], bank(k)[:, 0:2 * VW], v12_hi[:, t, :])
                if tail is not None:
                    route_softmax_1(tail)
                for which, name in ((0, "q_c"), (1, "k_c")):
                    for half in range(2):
                        k = first(name) + half
                        at = slice(half * 512, half * 512 + 512)
                        low(b, k, (k_lo if which else q_lo)[2][:, at], bank(k), (k_hi if which else q_hi)[2][:, at])
                if tail is not None:
                    route_softmax_2(tail)

            def tile_stats(b, t):
                o, m = mixed_of(t), t % 2
                dve.wait_ge(pv_done, b * UNITS + BR * t + BR)
                for br in range(BR):
                    last = dve.bn_stats(st[:, m, br, :], o[:, br * VW:br * VW + C])
                last.then_inc(o_stats, 1)
                dve.wait_ge(o_stats, b * NT + t + 1)
                dve.nop(nofuse=True)
                for br in range(BR):
                    dve.bn_aggr(mv[:, m, br, :], st[:, m, br, :])
                dve.tensor_copy(og[:, m, :, :], o.rearrange("p (i c) -> p i c", c=VW)[:, :, C:C + 3]).then_inc(o_mv, 1)

            def tile_gate_logits(b, t):
                m, n = t % 2, b * NT + t
                dve.wait_ge(rstd_ok, n + 1)
                dve.tensor_tensor(logit9[:, m, :, :], og[:, m, :, :].rearrange("p i g -> p g i"),
                                  rstd[:, m, :].unsqueeze(1).to_broadcast([P, 3, BR]), ALU.mult).then_inc(logit_c, 1)
                dve.wait_ge(logit_c, n * 3 + 1)
                dve.tensor_reduce(logit_s[:, m, :], logit9[:, m, :, :], AX_X, ALU.add).then_inc(logit_c, 1)
                dve.wait_ge(logit_c, n * 3 + 2)
                dve.tensor_tensor(logit[:, m, :], logit_s[:, m, :], gate_const[:], ALU.add).then_inc(logit_c, 1)
                dve.wait_ge(logit_c, n * 3 + 3)
                dve.tensor_reduce(logit_nm[:, m:m + 1], logit[:, m, :], AX_X, ALU.max, negate=True).then_inc(logit_ok, 1)

            def tile_gate(b, t):
                m, n = t % 2, b * NT + t
                dve.wait_ge(gate_ok, n + 1)
                dve.reciprocal(gate_inv[:, m:m + 1], gate_sum[:, m:m + 1]).then_inc(gate_c, 1)
                dve.wait_ge(gate_c, n * 3 + 1)
                dve.tensor_scalar(gate[:, m, :], gate_e[:, m, :], gate_inv[:, m:m + 1], None, ALU.mult).then_inc(gate_c, 1)
                dve.wait_ge(gate_c, n * 3 + 2)
                dve.tensor_tensor(gate_r[:, m, :], gate[:, m, :], rstd[:, m, :], ALU.mult).then_inc(gate_c, 1)
                dve.wait_ge(gate_c, n * 3 + 3)
                dve.scalar_tensor_tensor(out=gate_b[:, m, :], in0=mv[:, m, :, 0], scalar=-1.0, in1=gate_r[:, m, :],
                                         op0=ALU.mult, op1=ALU.mult).then_inc(scale_ok, 1)

            def tile_h1_stats(b, t):
                m, n = t % 2, b * NT + t
                dve.wait_ge(h1_ok, n + 1)
                dve.bn_stats(st2[:, m, :], h1[:, t, :]).then_inc(st2_ok, 1)
                dve.wait_ge(st2_ok, n + 1)
                dve.nop(nofuse=True)
                dve.bn_aggr(mv2[:, m, :], st2[:, m, :]).then_inc(mv2_ok, 1)

            def tile_x2(b, t):
                m, n = t % 2, b * NT + t
                dve.wait_ge(rstd2_ok, n + 1)
                if t == 0:
                    dve.wait_ge(rows_free, b + 1)
                dve.tensor_scalar(trow[:, t, 0:C], h1[:, t, :], mv2[:, m, 0:1], rstd2[:, m:m + 1],
                                  ALU.subtract, ALU.mult).then_inc(x2_ok, 1)

            def route_softmax_1(b):
                dve.wait_ge(routed, b + 1)
                dve.tensor_tensor(r_log, mixed[:, 0:NT * NE].rearrange("p (t e) -> p t e", e=NE),
                                  R("b_router").unsqueeze(1).to_broadcast([P, NT, NE]), ALU.add).then_inc(route_v, 1)
                dve.wait_ge(route_v, b * 5 + 1)
                dve.tensor_reduce(r_nm[:], r_log, AX_X, ALU.max, negate=True).then_inc(route_v, 1)
                dve.wait_ge(route_v, b * 5 + 2)
                dve.tensor_tensor(r_sub, r_log, r_nm[:].unsqueeze(2).to_broadcast([P, NT, NE]),
                                  ALU.add).then_inc(route_v, 1)

            def route_softmax_2(b):
                dve.wait_ge(route_e, b + 1)
                dve.tensor_reduce(r_sum[:], r_exp, AX_X, ALU.add).then_inc(route_v, 1)
                dve.wait_ge(route_v, b * 5 + 4)
                dve.reciprocal(r_inv[:], r_sum[:]).then_inc(route_v, 1)
                dve.wait_ge(route_v, b * 5 + 5)
                dve.tensor_tensor(trow[:, :, C:XW], r_exp, r_inv[:].unsqueeze(2).to_broadcast([P, NT, NE]),
                                  ALU.mult).then_inc(prob_ok, 1)

            def attention(b):
                def maxima(i):
                    n = SD if i % BR == 0 else S
                    dve.wait_ge(scored, b * UNITS + i + 1)
                    dve.tensor_reduce(neg_max[:, i % 4:i % 4 + 1], scores[:, (i % 2) * S:(i % 2) * S + n], AX_X,
                                      ALU.max, negate=True).then_inc(maxed, 1)

                def low_part(i):
                    n = SD if i % BR == 0 else S
                    dve.wait_ge(hi_done, b * UNITS + i + 1)
                    if i >= 2:
                        dve.wait_ge(pv_done, b * UNITS + i - 1)
                    dve.tensor_tensor(pT_lo[:, i % 2, 0:n], turned[:, 0:n], pT_hi[:, i % 2, 0:n].bitcast(F32),
                                      ALU.subtract).then_inc(lo_done, 1)

                for i in range(UNITS + 3):
                    if 0 <= i - 2 < UNITS:
                        low_part(i - 2)
                    if i < UNITS:
                        maxima(i)
                    for t in range(NT):
                        stage = i - 3 * t - 6
                        if stage == 3:
                            tile_h1_stats(b, t)
                        if stage == 4:
                            tile_x2(b, t)
                        if stage == 0:
                            tile_stats(b, t)
                        if stage == 1:
                            tile_gate_logits(b, t)
                        if stage == 2:
                            tile_gate(b, t)
                tile_h1_stats(b, NT - 2)
                tile_stats(b, NT - 1)

            NORM0[0] = hashes()
            setup()
            prologue(0, None)
            with dve.Fori(0, B - 1) as b:
                attention(b)
                prologue(b + 1, b)
            attention(B - 1)
            tile_gate_logits(B - 1, NT - 1)
            tile_x2(B - 1, NT - 2)
            tile_gate(B - 1, NT - 1)
            tile_h1_stats(B - 1, NT - 1)
            tile_x2(B - 1, NT - 1)
            route_softmax_1(B - 1)
            route_softmax_2(B - 1)

        @block.scalar
        def _(act):
            def high(b, k, dst, src, bias=0.0):
                act.wait_ge(bank_full, b * NUSE + k + 1)
                act.activation(dst, src, ACT.Identity, bias=bias).then_inc(bank_a, 1)

            def prologue(b, tail):
                for k in range(6):
                    n, half = k // 2, k % 2
                    high(b, k, gramT[:, n, half * 512:(half + 1) * 512], bank(k))
                if tail is not None:
                    tile_gate_exp(tail, NT - 1)
                for half in range(2):
                    k = first("xT") + half
                    high(b, k, xT_hi[:, 2 + half * 512:514 + half * 512], bank(k))
                if tail is not None:
                    tile_scale(tail, NT - 1)
                for t in range(NT):
                    act.wait_ge(bank_v, b * V_READS + reads("v", first("qk_raw") + t // 2))
                    for which in range(2):
                        last = act.activation(square[:, t, which * C:(which + 1) * C], qk_raw[:, t, which * C:(which + 1) * C], ACT.Square,
                                              accum_out=norm[:, 2 * t + which:2 * t + which + 1])
                    last.then_inc(sq_ready, 1)
                high(b, first("down"), down_hi[:], bank(first("down")), col[:, COL["db"]:COL["db"] + 1])
                for br, which, name in ((1, q_hi, "q_d"), (1, k_hi, "k_d"), (0, q_hi, "q_cr")):
                    for half in range(2):
                        k = first(name) + half
                        high(b, k, which[br][:, half * 512:half * 512 + 512], bank(k),
                             col[:, COL["b" + name]:COL["b" + name] + 1])
                high(b, first("k_cr"), k_hi[0][:], bank(first("k_cr")), col[:, COL["bk_cr"]:COL["bk_cr"] + 1])
                for i in range(2):
                    k = first("v_cr") + i
                    high(b, k, v0_hi[:, 2 * i:2 * i + 2, :], bank(k)[:, 0:2 * VW].rearrange("p (t c) -> p t c", c=VW))
                if tail is not None:
                    route_copy(tail)
                for t in range(NT):
                    k = first("v_dc") + t
                    high(b, k, v12_hi[:, t, :], bank(k)[:, 0:2 * VW])
                if tail is not None:
                    route_exp(tail)
                for which, name in ((0, "q_c"), (1, "k_c")):
                    for half in range(2):
                        k = first(name) + half
                        high(b, k, (k_hi if which else q_hi)[2][:, half * 512:half * 512 + 512], bank(k))
                if tail is not None:
                    act.wait_ge(h1_ok, tail * NT + NT)

            def route_copy(b):
                act.wait_ge(x2_turned, b + 1)
                act.activation(x2T, turned[:], ACT.Identity).then_inc(x2T_ok, 1)

            def route_exp(b):
                act.wait_ge(route_v, b * 5 + 3)
                act.activation(r_exp, r_sub, ACT.Exp).then_inc(route_e, 1)

            def tile_gate_exp(b, t):
                m = t % 2
                act.wait_ge(logit_ok, b * NT + t + 1)
                act.activation(gate_e[:, m, :], logit[:, m, :], ACT.Exp, bias=logit_nm[:, m:m + 1],
                               accum_out=gate_sum[:, m:m + 1]).then_inc(gate_ok, 1)

            def tile_scale(b, t):
                m = t % 2
                act.wait_ge(scale_ok, b * NT + t + 1)
                if t >= 2:
                    act.wait_ge(h1_ok, b * NT + t - 1)
                for br in range(BR):
                    last = act.activation(u[:, m, br, :], mixed_of(t)[:, br * VW:br * VW + C], ACT.Identity,
                                          bias=gate_b[:, m, br:br + 1], scale=gate_r[:, m, br:br + 1])
                last.then_inc(u_ok, 1)

            def attention(b):
                def exponent(i):
                    t, br = i // BR, i % BR
                    n = SD if br == 0 else S
                    act.wait_ge(maxed, b * UNITS + i + 1)
                    if i >= 2:
                        act.wait_ge(turn_done, b * UNITS + i - 1)
                    act.activation(probs[:, i % 2, 0:n], scores[:, (i % 2) * S:(i % 2) * S + n], ACT.Exp,
                                   bias=neg_max[:, i % 4:i % 4 + 1],
                                   accum_out=exp_sum[:, t % 4, br:br + 1]).then_inc(exped, 1)

                def high_part(i):
                    n = SD if i % BR == 0 else S
                    act.wait_ge(turn_done, b * UNITS + i + 1)
                    if i >= 2:
                        act.wait_ge(pv_done, b * UNITS + i - 1)
                    act.activation(pT_hi[:, i % 2, 0:n], turned[:, 0:n], ACT.Identity).then_inc(hi_done, 1)

                for i in range(UNITS + 3):
                    if 0 <= i - 2 < UNITS:
                        high_part(i - 2)
                    if i < UNITS:
                        exponent(i)
                    for t in range(NT):
                        stage = i - 3 * t - 6
                        if stage == 1:
                            tile_gate_exp(b, t)
                        if stage == 2:
                            tile_scale(b, t)

            act.wait_ge(loaded, 64)
            act.wait_ge(weights_ready, 2)
            prologue(0, None)
            with act.Fori(0, B - 1) as b:
                attention(b)
                prologue(b + 1, b)
            attention(B - 1)
            tile_gate_exp(B - 1, NT - 1)
            tile_scale(B - 1, NT - 1)
            route_copy(B - 1)
            route_exp(B - 1)

        @block.gpsimd
        def _(pool):
            def gathers(t):
                for g in range(3):
                    pool.indirect_dma_start(gram[:, t, g, :], None, emb[g],
                                            bass.IndirectOffsetOnAxis(ap=ids_now[:, 3 * t + g:3 * t + g + 1], axis=0)
                                            ).then_inc(gathered, 16)

            def stage_ids(b):
                if not isinstance(b, int) or b > 0:
                    pool.wait_ge(gathered, b * (NT * 3 * 16))
                    pool.wait_ge(bank_full, (b - 1) * NUSE + 6)
                pool.tensor_copy(ids_now[:], ids[:, bass.ds(b, 1), :, :].rearrange("p b t g -> p (b t g)")
                                 ).then_inc(staged, 1)
                pool.wait_ge(staged, b + 1)

            def prologue(b, tail):
                if tail is not None:
                    tile_rstd2(tail, NT - 2)
                    tile_rstd(tail, NT - 1)
                pool.wait_ge(bank_a, b * A_READS + 6)
                pool.nop(nofuse=True)
                for g in range(3):
                    pool.memset(gramT[:, g, 0:(2 if g == 2 else 1)], 0.0).then_inc(edges, 1)
                    if g > 0:
                        pool.memset(gramT[:, g, S - 1:S], 0.0).then_inc(edges, 1)
                pool.wait_ge(ln1_mv, b + 1)
                pool.nop(nofuse=True)
                pool.tensor_scalar(rstd1[:], mv1[:, :, 1], LN_EPS, None, ALU.add).then_inc(ln1_g, 1)
                pool.wait_ge(ln1_g, b + 1)
                pool.tensor_tensor(rstd1[:], rstd1[:], m_half[:, 0:NT], ALU.pow).then_inc(ln1_rstd, 1)
                if tail is not None:
                    tile_sum(tail, NT - 1)
                    tile_rstd2(tail, NT - 1)
                pool.wait_ge(sq_ready, b * NT + NT)
                pool.tensor_tensor(norm[:], norm[:], p_half[:], ALU.pow).then_inc(norm_g, 1)
                pool.wait_ge(norm_g, b * 2 + 1)
                pool.nop(nofuse=True)
                pool.tensor_scalar(norm[:], norm[:], NORM_EPS, None, ALU.add).then_inc(norm_g, 1)
                if tail is not None:
                    keep_probs(tail)

            def keep_probs(b):
                pool.wait_ge(prob_ok, b + 1)
                pool.tensor_copy(prob[:].rearrange("p (u c) e -> p c u e", c=CHUNKS)[
                    :, bass.ds(b // SEQ_OF_CHUNK, 1), bass.ds((b % SEQ_OF_CHUNK) * NT, NT), :],
                    trow[:, :, C:XW]).then_inc(prob_kept, 1)

            def tile_rstd(b, t):
                m, n = t % 2, b * NT + t
                pool.wait_ge(o_mv, n + 1)
                pool.wait_ge(exped, b * UNITS + BR * t + BR)
                s = exp_sum[:, t % 4, :]
                pool.tensor_tensor(sum_sq[:, m, :], s, s, ALU.mult).then_inc(rstd_g, 1)
                pool.wait_ge(rstd_g, n * 3 + 1)
                pool.nop(nofuse=True)
                pool.tensor_scalar(var_eps[:, m, :], sum_sq[:, m, :], LN_EPS, None, ALU.mult).then_inc(rstd_g, 1)
                pool.wait_ge(rstd_g, n * 3 + 2)
                pool.tensor_tensor(var_eps[:, m, :], var_eps[:, m, :], mv[:, m, :, 1], ALU.add).then_inc(rstd_g, 1)
                pool.wait_ge(rstd_g, n * 3 + 3)
                pool.tensor_tensor(rstd[:, m, :], var_eps[:, m, :], m_half[:, 0:BR], ALU.pow).then_inc(rstd_ok, 1)

            def tile_sum(b, t):
                m, n = t % 2, b * NT + t
                k = [n * 5]

                def step(ins):
                    k[0] = k[0] + 1
                    ins.then_inc(z_g, 1)
                    pool.wait_ge(z_g, k[0])

                pool.wait_ge(scale_ok, n + 1)
                shift = R("ln_b")
                step(pool.tensor_tensor(zb[:, m, :, :], shift.rearrange("p (i c) -> p i c", c=C),
                                        gate[:, m, :].unsqueeze(2).to_broadcast([P, BR, C]), ALU.mult))
                step(pool.tensor_tensor(zb[:, m, 0, :], zb[:, m, 0, :], h[:, bass.ds((b % 2) * NT + t, 1), :], ALU.add))
                pool.wait_ge(u_ok, n + 1)
                step(pool.tensor_tensor(u[:, m, :, :].rearrange("p i c -> p (i c)"),
                                        u[:, m, :, :].rearrange("p i c -> p (i c)"), R("ln_g"), ALU.mult))
                step(pool.tensor_tensor(u[:, m, :, :], u[:, m, :, :], zb[:, m, :, :], ALU.add))
                step(pool.tensor_tensor(u[:, m, 0, :], u[:, m, 0, :], u[:, m, 1, :], ALU.add))
                if t == 0:
                    pool.wait_ge(h1_free, b + 1)
                pool.tensor_tensor(h1[:, t, :], u[:, m, 0, :], u[:, m, 2, :], ALU.add).then_inc(h1_ok, 1)

            def tile_rstd2(b, t):
                m, n = t % 2, b * NT + t
                pool.wait_ge(mv2_ok, n + 1)
                pool.nop(nofuse=True)
                pool.tensor_scalar(ve2[:, m:m + 1], mv2[:, m, 1:2], LN_EPS, None, ALU.add).then_inc(ve2_ok, 1)
                pool.wait_ge(ve2_ok, n + 1)
                pool.tensor_tensor(rstd2[:, m:m + 1], ve2[:, m:m + 1], m_half[:, 0:1], ALU.pow).then_inc(rstd2_ok, 1)

            def attention(b, more):
                if more:
                    stage_ids(b + 1)
                for t in range(NT - 1):
                    if t > 0:
                        tile_rstd2(b, t - 1)
                    tile_rstd(b, t)
                    if more:
                        gathers(t)
                    tile_sum(b, t)
                if more:
                    gathers(NT - 1)

            pool.memset(xwi[:], 0).then_inc(setup_g, 1)
            pool.memset(wide[:], 0.0).then_inc(setup_g, 1)
            pool.memset(mean_w[:], 1.0 / C).then_inc(setup_g, 1)
            pool.memset(ones_row[:], 1.0).then_inc(setup_g, 1)
            pool.memset(m_half[:], -0.5).then_inc(setup_g, 1)
            pool.memset(p_half[:], 0.5).then_inc(setup_g, 1)
            pool.memset(xT_hi[:, 0:2].bitcast(F32), 0.0)
            pool.memset(xT_lo[:, 0:2].bitcast(F32), 0.0).then_inc(setup_g, 1)
            pool.wait_ge(setup_g, 7)
            pool.wait_ge(ids_ready, 2)
            stage_ids(0)
            for t in range(NT):
                gathers(t)
            prologue(0, None)
            with pool.Fori(0, B - 1) as b:
                attention(b, True)
                prologue(b + 1, b)
            attention(B - 1, False)
            tile_rstd2(B - 1, NT - 2)
            tile_rstd(B - 1, NT - 1)
            tile_sum(B - 1, NT - 1)
            tile_rstd2(B - 1, NT - 1)
            keep_probs(B - 1)

        first_part.__exit__(None, None, None)
        attn.close()
        experts(nc, ctx, con, prob, ones_row, scores, turned, mixed, table, cand_bits, w_up, b_up, w_down, out)


def experts(nc, ctx, con, prob, ones_row, scores, turned, mixed, table, cand_bits, w_up, b_up, w_down, out):
    CT = TT // CHUNKS
    RW = P + 2

    def sb(name, shape, dt=F32):
        return ctx.enter_context(nc.sbuf_tensor(name, shape, dt))

    def sem(name):
        return ctx.enter_context(nc.semaphore(name))

    def K(name):
        return con[:, CON[name][0]:CON[name][1]]

    ident = K("ident")

    bits_i = sb("bits_i", [P, BITS + 1], I32)
    bits_f = sb("bits_f", [P, BITS + 1])
    probT = sb("probT", [P, CT * P])
    above = sb("above", [P, CT * P], BF16)
    count = sb("count", [P, 1])
    cand = sb("cand", [P, 1], I32)
    cand_next = sb("cand_next", [P, 1], I32)
    drop = sb("drop", [P, 1], I32)
    thr_row = sb("thr_row", [NE, P])
    thr = sb("thr", [P, NE])
    ones_bf = sb("ones_bf", [P, P], BF16)
    upto_bf = sb("upto_bf", [P, P], BF16)
    after_bf = sb("after_bf", [P, P], BF16)
    below_bf = sb("below_bf", [P, P], BF16)
    slot_bf = sb("slot_bf", [P, TOPK], BF16)
    over = sb("over", [P, TT, NE], BF16)
    tie = sb("tie", [P, TT, NE], BF16)
    tie_in = sb("tie_in", [P, TT, NE], BF16)
    n_over = sb("n_over", [P, NE])
    room = sb("room", [P, NE])
    tie_tile = sb("tie_tile", [P, NE, TT + 1])
    keep = sb("keep", [P, NE, TT + 1])
    tie_before = sb("tie_before", [P, NE, TT + 1])
    tie_rank = sb("tie_rank", [P, TT, NE])
    chosen = sb("chosen", [P, TT + 1, NE], BF16)
    ranks = sb("ranks", [TT, NE, RW], BF16)
    before = sb("before", [TT, NE])
    reached = sb("reached", [TT, NE, TOPK], BF16)
    less = sb("less", [P, NE * HALVES, P], BF16)
    n_less = sb("n_less", [P, NE * HALVES])
    tile_no = sb("tile_no", [P, NE * HALVES])
    slot_f = sb("slot_f", [P, NE * HALVES])
    slots = sb("slots", [P, NE * HALVES], I32)
    EB = GROUP
    g_ids = sb("g_ids", [P, EB * HALVES], I32)
    s_ids = sb("s_ids", [P, EB * HALVES], I32)
    bup = sb("bup", [FP, NG * FC])
    wu = sb("wu", [P, EB, DFF])
    wd = sb("wd", [FP, EB, FC, C])
    xg = sb("xg", [P, EB, HALVES, XW])
    xT = sb("xT", [P, 2, TOPK])
    hid = sb("hid", [FP, 2, FC, TOPK])
    yw = sb("yw", [P, EB, HALVES, C])

    bits_in = sem("bits_in")
    prob_turned = sem("prob_turned")
    prob_copied = sem("prob_copied")
    made = sem("made")
    made_g = sem("made_g")
    counted = sem("counted")
    totalled = sem("totalled")
    cand_c = sem("cand_c")
    drop_ok = sem("drop_ok")
    cand_ok = sem("cand_ok")
    thr_v = sem("thr_v")
    thr_t = sem("thr_t")
    masks = sem("masks")
    sums_t = sem("sums_t")
    pick_v = sem("pick_v")
    chosen_ok = sem("chosen_ok")
    rank_t = sem("rank_t")
    rank_a = sem("rank_a")
    before_t = sem("before_t")
    before_v = sem("before_v")
    reached_ok = sem("reached_ok")
    row_t = sem("row_t")
    row_v = sem("row_v")
    slots_v = sem("slots_v")
    slots_ok = sem("slots_ok")
    g_staged = sem("g_staged")
    s_staged = sem("s_staged")
    bup_in = sem("bup_in")
    w_in = [sem(f"w_in{j}") for j in range(EB)]
    x_in = [sem(f"x_in{j}") for j in range(EB)]
    xt_t = sem("xt_t")
    xt_v = sem("xt_v")
    up_t = sem("up_t")
    hid_a = sem("hid_a")
    down_t = sem("down_t")
    y_v = sem("y_v")
    added = sem("added")
    ones_set = sem("ones_set")

    rows_out = out.rearrange("b s c -> (b s) c")

    def wave(e):
        return e // EB + 1

    def slot_bank(k):
        k = k % 8
        return (scores[:, k * 512:(k + 1) * 512] if k < 4 else turned[:, (k - 4) * 512:(k - 3) * 512] if k < 6
                else mixed[:, (k - 6) * 512:(k - 5) * 512])

    row_banks = [(half, e0, min(3, NE - e0)) for e0 in range(0, NE, 3) for half in range(HALVES)]

    block = ctx.enter_context(nc.Block())

    @block.sync
    def _(sp):
        sp.dma_start(bits_i[:], cand_bits[0]).then_inc(bits_in, 16)
        sp.dma_start(bits_f[:], cand_bits[1]).then_inc(bits_in, 16)
        sp.dma_start(bup[:], b_up.rearrange("p g c -> p (g c)")).then_inc(bup_in, 16)

        def load(g, j):
            sp.dma_start(wu[:, j, :], w_up[bass.ds(g, 1), :, :].rearrange("g h f -> (g h) f")).then_inc(w_in[j], 16)
            sp.dma_start(wd[:, j, :, :], w_down[bass.ds(g * GROUP + j, 1), :, :].rearrange("e (c p) h -> p (e c) h", p=FP)
                         ).then_inc(w_in[j], 16)

        for j in range(EB):
            load(0, j)
        with sp.Fori(0, NG - 1) as g:
            for j in range(EB):
                sp.wait_ge(down_t, g * GROUP + j + 1)
                load(g + 1, j)

    @block.tensor
    def _(pe):
        for u in range(CT):
            last = pe.transpose(scores[:, u * P:(u + 1) * P], prob[:, u * CHUNKS:(u + 1) * CHUNKS, :].rearrange("p c e -> p (c e)"), ident)
            if u % 4 == 3:
                last.then_inc(prob_turned, 1)
        with pe.Fori(0, BITS) as k:
            pe.wait_ge(counted, k + 1)
            pe.matmul(turned[:, 0:1], K("same"), count[:], start=True, stop=True).then_inc(totalled, 1)
        pe.wait_ge(thr_v, 1)
        pe.transpose(turned[:, 512:512 + NE], thr_row[:], ident[0:NE, 0:NE]).then_inc(thr_t, 1)
        pe.wait_ge(made, 4)
        pe.wait_ge(made_g, 1)
        pe.wait_ge(masks, 1)
        for q in range(4):
            last = pe.matmul(turned[:, 0:512], ones_bf[:], over[:, q * 16:(q + 1) * 16, :], start=(q == 0), stop=(q == 3))
        last.then_inc(sums_t, 1)
        pe.wait_ge(masks, 2)
        pe.wait_ge(prob_copied, 4)
        for q in range(4):
            last = pe.matmul(scores[:, q * 512:(q + 1) * 512], ones_bf[:], tie[:, q * 16:(q + 1) * 16, :],
                             start=True, stop=True)
        last.then_inc(sums_t, 1)
        pe.wait_ge(pick_v, 1)
        for q in range(4):
            last = pe.matmul(slot_bank(4 + q), upto_bf[:], tie[:, q * 16:(q + 1) * 16, :], start=True, stop=True)
        last.then_inc(sums_t, 1)
        pe.wait_ge(chosen_ok, 1)
        for e in range(NE):
            dst = slot_bank(e // 4)[0:TT, (e % 4) * P:(e % 4 + 1) * P]
            pe.matmul(dst, chosen[:, 1:TT + 1, e], upto_bf[:], start=True, stop=False)
            last = pe.matmul(dst, chosen[:, 0:TT, e], after_bf[:], start=False, stop=True)
            if e % 4 == 3:
                last.then_inc(rank_t, 1)
        pe.wait_ge(rank_a, 8)
        pe.matmul(scores[0:TT, 0:NE], below_bf[0:TT, 0:TT], ranks[:, :, P - 1], start=True, stop=True).then_inc(before_t, 1)
        pe.wait_ge(before_v, 1)
        for n, (half, e0, m) in enumerate(row_banks):
            pe.wait_ge(reached_ok, min(e0 + m, NE))
            if n >= 8:
                pe.wait_ge(row_v, n - 7)
            for i in range(m):
                last = pe.matmul(slot_bank(n)[:, i * RW:(i + 1) * RW], reached[:, e0 + i, half * P:(half + 1) * P],
                                 ranks[:, e0 + i, :], start=True, stop=True)
            last.then_inc(row_t, 1)
        pe.wait_ge(row_v, len(row_banks))

        def turn(e, j):
            pe.wait_ge(x_in[j % EB], wave(e) * 32)
            if not isinstance(e, int) or e >= 2:
                pe.wait_ge(xt_v, e - 1)
            for half in range(HALVES):
                last = pe.transpose(scores[:, (j % 2) * 512 + half * P:(j % 2) * 512 + (half + 1) * P],
                                    xg[:, j % EB, half, 0:C], ident)
            last.then_inc(xt_t, 1)

        def up_bank(j):
            return scores[:, 1024:2048] if j % 2 == 0 else turned[:]

        def up(e, j):
            pe.wait_ge(w_in[j % EB], wave(e) * 32)
            pe.wait_ge(xt_v, e + 1)
            if not isinstance(e, int) or e >= 2:
                pe.wait_ge(hid_a, e - 1)
            for c in range(FC):
                n = FP if c < FC - 1 else FP - 1
                last = pe.matmul(up_bank(j)[0:n, c * TOPK:(c + 1) * TOPK], wu[:, j % EB, c * FP:c * FP + n],
                                 xT[:, j % 2, :], start=True, stop=True)
            last.then_inc(up_t, 1)

        def down(e, j):
            pe.wait_ge(hid_a, e + 1)
            if not isinstance(e, int) or e >= 2:
                pe.wait_ge(y_v, e - 1)
            for half in range(HALVES):
                for c in range(FC):
                    last = pe.matmul(mixed[:, (j % 2) * 512 + half * C:(j % 2) * 512 + (half + 1) * C],
                                     hid[:, j % 2, c, half * P:(half + 1) * P], wd[:, j % EB, c, :],
                                     start=(c == 0), stop=(c == FC - 1))
            last.then_inc(down_t, 1)

        pe.wait_ge(ones_set, 2)
        turn(0, 0)
        turn(1, 1)
        up(0, 0)

        def group(first_e):
            for j in range(EB):
                turn(first_e + j + 2, j + 2)
                up(first_e + j + 1, j + 1)
                down(first_e + j, j)

        group(0)
        with pe.Fori(1, NG - 1) as g:
            group(g * GROUP)
        for j in range(EB):
            e = NE - GROUP + j
            if e + 2 < NE:
                turn(e + 2, j + 2)
            if e + 1 < NE:
                up(e + 1, j + 1)
            down(e, j)

    @block.vector
    def _(dve):
        dve.memset(cand[:], 1 << (BITS - 1)).then_inc(cand_ok, 1)
        dve.wait_ge(bits_in, 32)
        dve.wait_ge(prob_copied, 4)
        with dve.Fori(0, BITS) as k:
            dve.wait_ge(cand_ok, k + 1)
            dve.tensor_scalar(above[:], probT[:], cand[:].bitcast(F32), None, ALU.is_ge, ALU.add,
                              accum_out=count[:]).then_inc(counted, 1)
            dve.tensor_tensor(cand_next[:], cand[:], bits_i[:, bass.ds(k + 1, 1)], ALU.bitwise_or).then_inc(cand_c, 1)
            dve.wait_ge(totalled, k + 1)
            dve.scalar_tensor_tensor(out=drop[:], in0=turned[:, 0:1], scalar=float(TOPK), in1=bits_f[:, bass.ds(k, 1)],
                                     op0=ALU.is_lt, op1=ALU.mult).then_inc(drop_ok, 1)
            dve.wait_ge(drop_ok, k + 1)
            dve.wait_ge(cand_c, k + 1)
            dve.tensor_tensor(cand[:], cand_next[:], drop[:], ALU.bitwise_xor).then_inc(cand_ok, 1)
        dve.wait_ge(cand_ok, BITS + 1)
        dve.wait_ge(made_g, 1)
        dve.tensor_scalar(thr_row[:], thr_row[:], cand[0:NE, :].bitcast(F32), None, ALU.add).then_inc(thr_v, 1)
        dve.wait_ge(thr_t, 1)
        dve.tensor_copy(thr[:], turned[:, 512:512 + NE]).then_inc(thr_v, 1)
        dve.wait_ge(thr_v, 2)
        everywhere = thr[:].unsqueeze(1).to_broadcast([P, CT, NE])
        for mask, op in ((over, ALU.is_gt), (tie, ALU.is_equal)):
            for c in range(CHUNKS):
                last = dve.tensor_tensor(mask[:, c * CT:(c + 1) * CT, :], prob[:, c:TT:CHUNKS, :], everywhere, op)
            last.then_inc(masks, 1)
        dve.wait_ge(sums_t, 1)
        dve.tensor_reduce(n_over[:], turned[:, 0:512].rearrange("p (t e) -> p e t", e=NE), AX_X, ALU.add).then_inc(pick_v, 1)
        dve.wait_ge(sums_t, 2)
        for q in range(4):
            last = dve.tensor_copy(tie_tile[:, :, 1 + q * 16:17 + q * 16],
                                   scores[:, q * 512:(q + 1) * 512].rearrange("p (t e) -> p e t", e=NE))
        last.then_inc(pick_v, 1)
        dve.wait_ge(pick_v, 2)
        dve.tensor_scalar(room[:], n_over[:], -1.0, float(TOPK), ALU.mult, ALU.add)
        dve.tensor_tensor_scan(tie_before[:].rearrange("p e t -> p (e t)"), keep[:].rearrange("p e t -> p (e t)"),
                               tie_tile[:].rearrange("p e t -> p (e t)"), 0.0, ALU.mult, ALU.add).then_inc(pick_v, 1)
        dve.wait_ge(pick_v, 3)
        dve.wait_ge(sums_t, 3)
        for n, part in enumerate((turned, mixed)):
            last = dve.tensor_tensor(tie_rank[:, n * 32:(n + 1) * 32, :], part[:].rearrange("p (t e) -> p t e", e=NE),
                                     tie_before[:].rearrange("p e t -> p t e")[:, n * 32:(n + 1) * 32, :], ALU.add)
        last.then_inc(pick_v, 1)
        dve.wait_ge(pick_v, 4)
        dve.tensor_tensor(tie_in[:], tie_rank[:], room[:].unsqueeze(1).to_broadcast([P, TT, NE]),
                          ALU.is_le).then_inc(pick_v, 1)
        dve.wait_ge(pick_v, 5)
        dve.tensor_tensor(tie_in[:], tie_in[:], tie[:], ALU.mult).then_inc(pick_v, 1)
        dve.wait_ge(pick_v, 6)
        dve.tensor_tensor(chosen[:, 1:TT + 1, :], tie_in[:], over[:], ALU.add).then_inc(chosen_ok, 1)
        dve.wait_ge(before_t, 1)
        dve.tensor_copy(before[:], scores[0:TT, 0:NE]).then_inc(before_v, 1)
        dve.wait_ge(before_v, 1)
        for e in range(NE):
            dve.tensor_scalar(reached[:, e, :], slot_bf[0:TT, :], before[:, e:e + 1], None, ALU.is_gt).then_inc(reached_ok, 1)
        for n, (half, e0, m) in enumerate(row_banks):
            dve.wait_ge(row_t, n + 1)
            for i in range(m):
                k = (e0 + i) * HALVES + half
                dve.tensor_scalar(less[:, k, :], slot_bank(n)[:, i * RW:i * RW + P],
                                  K("slotcol")[:, half:half + 1], None, ALU.is_lt, ALU.add, accum_out=n_less[:, k:k + 1])
            at = slice(e0 * HALVES + half, (e0 + m - 1) * HALVES + half + 1, HALVES)
            dve.tensor_copy(tile_no[:, at], slot_bank(n)[:, 0:m * RW].rearrange("p (i r) -> p i r", r=RW)[:, :, P]
                            ).then_inc(row_v, 1)
        dve.wait_ge(row_v, len(row_banks))
        dve.tensor_scalar(slot_f[:], tile_no[:], float(P), -float(P), ALU.mult, ALU.add).then_inc(slots_v, 1)
        dve.wait_ge(slots_v, 1)
        dve.tensor_tensor(slots[:], slot_f[:], n_less[:], ALU.add).then_inc(slots_ok, 1)

        def copy_x(e, j):
            dve.wait_ge(xt_t, e + 1)
            if not isinstance(e, int) or e >= 2:
                dve.wait_ge(up_t, e - 1)
            dve.tensor_copy(xT[:, j % 2, :], scores[:, (j % 2) * 512:(j % 2) * 512 + TOPK]).then_inc(xt_v, 1)

        def weigh(e, j):
            dve.wait_ge(down_t, e + 1)
            if not isinstance(e, int) or e >= EB:
                dve.wait_ge(added, (e - (EB - 1)) * 32)
            for half in range(HALVES):
                last = dve.tensor_scalar(yw[:, j % EB, half, :],
                                         mixed[:, (j % 2) * 512 + half * C:(j % 2) * 512 + (half + 1) * C],
                                         xg[:, j % EB, half, bass.ds(C + e, 1)], None, ALU.mult)
            last.then_inc(y_v, 1)

        copy_x(0, 0)
        copy_x(1, 1)
        for j in range(EB):
            copy_x(j + 2, j + 2)
            weigh(j, j)
        with dve.Fori(1, NG - 1) as g:
            for j in range(EB):
                copy_x(g * GROUP + j + 2, j + 2)
                weigh(g * GROUP + j, j)
        for j in range(EB):
            e = NE - GROUP + j
            if e + 2 < NE:
                copy_x(e + 2, j + 2)
            weigh(e, j)

    @block.scalar
    def _(act):
        act.activation(upto_bf[:], K("upto"), ACT.Identity).then_inc(made, 1)
        act.activation(after_bf[:], K("after"), ACT.Identity).then_inc(made, 1)
        act.activation(below_bf[:], K("below"), ACT.Identity).then_inc(made, 1)
        act.activation(slot_bf[:], K("slot"), ACT.Identity).then_inc(made, 1)
        for q in range(4):
            act.wait_ge(prob_turned, q + 1)
            act.activation(probT[:, q * 512:(q + 1) * 512], scores[:, q * 512:(q + 1) * 512],
                           ACT.Identity).then_inc(prob_copied, 1)
        act.wait_ge(made_g, 1)
        for q in range(8):
            act.wait_ge(rank_t, q + 1)
            act.activation(ranks[:, 4 * q:4 * q + 4, 0:P], slot_bank(q)[0:TT, :].rearrange("p (e t) -> p e t", t=P),
                           ACT.Identity).then_inc(rank_a, 1)

        def silu(g, e, j):
            act.wait_ge(up_t, e + 1)
            if not isinstance(e, int) or e >= 2:
                act.wait_ge(down_t, e - 1)
            if not isinstance(e, int):
                act.nop(nofuse=True)
            src = scores[:, 1024:2048] if j % 2 == 0 else turned[:]
            for c in range(FC):
                n = FP if c < FC - 1 else FP - 1
                last = act.activation(hid[0:n, j % 2, c, :], src[0:n, c * TOPK:(c + 1) * TOPK], ACT.Silu,
                                      bias=bup[0:n, bass.ds(g * FC + c, 1)])
            last.then_inc(hid_a, 1)

        act.wait_ge(bup_in, 16)
        act.wait_ge(ones_set, 2)
        for j in range(EB):
            silu(0, j, j)
        with act.Fori(1, NG) as g:
            for j in range(EB):
                silu(g, g * GROUP + j, j)

    @block.gpsimd
    def _(pool):
        pool.memset(ones_bf[:], 1.0)
        pool.memset(thr_row[:], 0.0)
        pool.memset(tie_tile[:, :, 0:1], 0.0)
        pool.memset(keep[:, :, 1:TT + 1], 1.0)
        pool.memset(keep[:, :, 0:1], 0.0)
        pool.memset(chosen[:, 0:1, :], 0.0)
        pool.memset(ranks[:, :, P:P + 1], 1.0)
        pool.memset(ranks[:, :, P + 1:RW], 0.0).then_inc(made_g, 1)
        pool.wait_ge(made_g, 1)
        for j in range(2):
            pool.memset(hid[96:FP, j, FC - 1, :], 1.0).then_inc(ones_set, 1)

        def stage(to, e, j, done):
            pool.tensor_copy(to[:, j * HALVES:(j + 1) * HALVES], slots[:, bass.ds(e * HALVES, HALVES)]).then_inc(done, 1)
            pool.wait_ge(done, e + 1)
            pool.nop(nofuse=True)

        def gather(e, j):
            j = j % EB
            if not isinstance(e, int) or e >= EB:
                pool.wait_ge(y_v, e - (EB - 1))
                pool.nop(nofuse=True)
            stage(g_ids, e, j, g_staged)
            for half in range(HALVES):
                at = j * HALVES + half
                pool.indirect_dma_start(xg[:, j, half, :], None, table,
                                        bass.IndirectOffsetOnAxis(ap=g_ids[:, at:at + 1], axis=0)
                                        ).then_inc(x_in[j], 16)

        def scatter(e, j):
            if not isinstance(e, int) or e >= 1:
                pool.wait_ge(added, e * 32)
                pool.nop(nofuse=True)
            stage(s_ids, e, j, s_staged)
            pool.wait_ge(y_v, e + 1)
            pool.nop(nofuse=True)
            for half in range(HALVES):
                at = j * HALVES + half
                pool.indirect_dma_start(rows_out, bass.IndirectOffsetOnAxis(ap=s_ids[:, at:at + 1], axis=0),
                                        yw[:, j, half, :], None, compute_op=ALU.add).then_inc(added, 16)

        def group(first_e, ahead=EB):
            for j in range(EB):
                if j < ahead:
                    gather(first_e + j + 3, j + 3)
                scatter(first_e + j, j)

        pool.wait_ge(ones_set, 2)
        pool.wait_ge(slots_ok, 1)
        for j in range(3):
            gather(j, j)
        group(0)
        with pool.Fori(1, NG - 1) as g:
            group(g * GROUP)
        group(NE - GROUP, 1)
        pool.wait_ge(added, NE * 32)


def kernel(**inputs):
    import numpy as np
    import concourse.bacc as bacc
    from concourse.bass_utils import run_bass_kernel_spmd

    g = {k: np.ascontiguousarray(v) for k, v in inputs.items()}

    def a(name):
        return g["L0_attn_" + name]

    zero3 = np.zeros((C, VW - C), np.float32)
    parts = [a("dw").transpose(1, 2, 0).reshape(C, 3 * C), a("wq_cr").T, a("wk_cr").T, a("wq_d").T, a("wk_d").T,
             a("wq_c").T, a("wk_c").T]
    for br in ("cr", "d", "c"):
        parts += [a(f"wv_{br}").T, zero3]
    parts += [g["L0_tok_proj_w"].reshape(C, 3, C).transpose(2, 1, 0).reshape(C, 3 * C)]
    parts += [a(f"wv_{br}") for br in ("cr", "d", "c")]
    parts += [g["L0_ffn_W_router"]]
    weights = np.ascontiguousarray(np.concatenate(parts, axis=1))
    gw = a("gw").reshape(3, 3, C).transpose(2, 1, 0).reshape(C, 9)
    cols = np.ascontiguousarray(np.concatenate(
        [np.stack([a("db"), a("bq_cr"), a("bk_cr"), a("bq_d"), a("bk_d")] + [a(f"ln_{n}_g") for n in ("cr", "d", "c")]
                  + [a(f"ln_{n}_b") for n in ("cr", "d", "c")] + [a(f"bv_{n}") for n in ("cr", "d", "c")], axis=1), gw],
        axis=1))
    rows1 = np.concatenate([g["L0_tok_proj_b"], a("bq_c"), a("bk_c")] + [a(f"bv_{n}") for n in ("cr", "d", "c")]
                           + [a(f"ln_{n}_g") for n in ("cr", "d", "c")] + [a(f"ln_{n}_b") for n in ("cr", "d", "c")]
                           + [g["L0_ffn_b_router"], a("gb"), a("temp").reshape(1)])
    rows = np.ascontiguousarray(np.broadcast_to(rows1[None, :], (P, NROW)))
    i = np.arange(P)
    consts = np.ascontiguousarray(np.concatenate([
        np.eye(P), i[:, None] <= i[None, :], i[:, None] > i[None, :], i[:, None] < i[None, :],
        (i[:, None] % NE) == (i[None, :] % NE), np.broadcast_to(np.arange(1, TOPK + 1), (P, TOPK)),
        i[:, None] + 1 + P * np.arange(HALVES)[None, :]], axis=1).astype(np.float32))
    bits = np.concatenate([1 << np.arange(BITS - 1, -1, -1), [0]])
    bits_i = np.ascontiguousarray(np.broadcast_to(bits.astype(np.int32), (P, BITS + 1)))
    bits_f = np.ascontiguousarray(np.broadcast_to(bits.astype(np.float32), (P, BITS + 1)))
    w_down = np.ascontiguousarray(np.concatenate([g["L0_ffn_W_down"], g["L0_ffn_b_down"][:, None, :]], axis=1))
    b_up = np.ascontiguousarray(np.concatenate([g["L0_ffn_b_up"], np.zeros((NG, 1), np.float32)], axis=1)
                                .reshape(NG, FC, FP).transpose(2, 0, 1))
    arrays = dict(x_tok=g["x"], emb_2=g["L0_tok_emb_2"], emb_3=g["L0_tok_emb_3"], emb_4=g["L0_tok_emb_4"],
                  weights=weights, cols=cols, rows=rows, consts=consts, bits_i=bits_i, bits_f=bits_f, w_up=g["L0_ffn_W_up"], b_up=b_up, w_down=w_down)
    nc = bacc.Bacc("TRN2", target_bir_lowering=False, num_devices=1)
    ap = {n: nc.dram_tensor(f"in_{n}", v.shape, mybir.dt.from_np(v.dtype), kind="ExternalInput").ap()
          for n, v in arrays.items()}
    out = nc.dram_tensor("out_h", (B, S, C), F32, kind="ExternalOutput").ap()
    build_program(nc, ap["x_tok"], (ap["emb_2"], ap["emb_3"], ap["emb_4"]), ap["weights"], ap["cols"], ap["rows"],
                  ap["consts"], (ap["bits_i"], ap["bits_f"]), ap["w_up"], ap["b_up"], ap["w_down"], out)
    r = run_bass_kernel_spmd(nc, [{f"in_{n}": v for n, v in arrays.items()}], core_ids=[0])
    return r.results[0]["out_h"]
```

```python
from contextlib import ExitStack

import concourse.bass as bass
from concourse import mybir

ALU = mybir.AluOpType
ACT = mybir.ActivationFunctionType
AX_X = mybir.AxisListType.X
F32 = mybir.dt.float32
F32R = mybir.dt.float32r
BF16 = mybir.dt.bfloat16
I32 = mybir.dt.int32

B, S, C = 8, 1024, 128
P = 128
NT = S // P
TOK = B * S
TT = TOK // P
VOCAB = 25000
SD = S // 2
NE, GROUP = 32, 4
NG = NE // GROUP
DFF = 341
FC = 3
FP = (DFF + 1) // FC
TOPK = TOK // NE
HALVES = TOPK // P
LN_EPS = 1e-5
NORM_EPS = 1e-8
SCALE = 1.0 / float(C) ** 0.5
VW = 132
XW = C + NE
BR = 3
UNITS = NT * BR
CHUNKS = P // NE
SEQ_OF_CHUNK = B // CHUNKS
BITS = 30

WCOL, _at = {}, 0
for _name, _width in (("conv", 3 * C), ("q_cr", C), ("k_cr", C), ("q_d", C), ("k_d", C), ("qk_c", 2 * C),
                      ("v_cr", VW), ("v_d", VW), ("v_c", VW)):
    WCOL[_name] = (_at, _at + _width)
    _at += _width
WSPLIT = _at
for _name, _width in (("proj", 3 * C), ("v_nat", 3 * C), ("router", NE)):
    WCOL[_name] = (_at, _at + _width)
    _at += _width
WALL = _at

COL = dict(db=0, bq_cr=1, bk_cr=2, bq_d=3, bk_d=4, ln_g=5, ln_b=8, bv=11, gw=14)
NCOL = 23
ROW, _at = {}, 0
for _name, _width in (("proj_b", C), ("bqk_c", 2 * C), ("bv", 3 * C), ("ln_g", 3 * C), ("ln_b", 3 * C),
                      ("b_router", NE), ("gb", 3), ("temp", 1)):
    ROW[_name] = (_at, _at + _width)
    _at += _width
NROW = _at
CON, _at = {}, 0
for _name, _width in (("ident", P), ("upto", P), ("after", P), ("below", P), ("same", P), ("slot", TOPK),
                      ("slotcol", HALVES)):
    CON[_name] = (_at, _at + _width)
    _at += _width
NCON = _at

USES = ([("xT", "av")] * 2 + [("qk_raw", "v")] * 4 + [("down", "av")]
        + [("q_d", "av")] * 2 + [("k_d", "av")] * 2 + [("q_cr", "av")] * 2 + [("k_cr", "av")]
        + [("v_cr", "av")] * 2 + [("v_dc", "av")] * 8 + [("q_c", "av")] * 2 + [("k_c", "av")] * 2)
NUSE = len(USES)


def first(name):
    return [n for n, _ in USES].index(name)


def reads(engine, k):
    return sum(engine in who for _, who in USES[:k + 1])


PARTS = NT * (2 * BR - 1)


def part(i, half=None):
    t, br = i // BR, i % BR
    return t * (2 * BR - 1) + max(2 * br - 1, 0) + ((1 if br else 0) if half is None else half) + 1


A_READS, V_READS = reads("a", NUSE - 1), reads("v", NUSE - 1)


def build_program(nc, x_tok, emb, weights, cols, rows, consts, cand_bits, w_up, b_up, w_down, out):
    table = nc.dram_tensor("token_table", (TOK, XW), F32, kind="Internal").ap()
    with ExitStack() as ctx:
        def sb(name, shape, dt=F32):
            return ctx.enter_context(nc.sbuf_tensor(name, shape, dt))

        def sem(name):
            return ctx.enter_context(nc.semaphore(name))

        attn = ExitStack()

        def asb(name, shape, dt=F32):
            return attn.enter_context(nc.sbuf_tensor(name, shape, dt))

        scores = ctx.enter_context(nc.psum_tensor("scores", [P, 4 * 512], F32))
        turned = ctx.enter_context(nc.psum_tensor("turned", [P, 2 * 512], F32))
        mixed = ctx.enter_context(nc.psum_tensor("mixed", [P, 2 * 512], F32))

        con = sb("con", [P, NCON])
        prob = sb("prob", [P, TT, NE])
        ones_row = sb("ones_row", [1, P])

        w = asb("w", [P, WALL])
        w_hi = asb("w_hi", [P, WSPLIT], F32R)
        w_lo = asb("w_lo", [P, WSPLIT], F32R)
        col = asb("col", [P, NCOL])
        row = asb("row", [P, NROW])
        gate_w = asb("gate_w", [P, 9])
        gate_mean = asb("gate_mean", [P, 9])
        wide = asb("wide", [P, 6, C])
        v_mean = asb("v_mean", [P, 2 * BR])
        mean_w = asb("mean_w", [P, P])
        bv_ext = asb("bv_ext", [P, 3 * VW])
        bv_hi = asb("bv_hi", [1, 3 * VW], F32R)
        bv_lo = asb("bv_lo", [1, 3 * VW], F32R)
        one_row = asb("one_row", [1, P], F32R)
        inv_temp = asb("inv_temp", [P, 1])
        m_half = asb("m_half", [P, 16])
        p_half = asb("p_half", [P, 16])

        xw = asb("xw", [TT, P + 3])
        xwi = asb("xwi", [TT, P + 3], I32)
        hashed = asb("hashed", [TT, 3, P + 1])
        quot = asb("quot", [TT, 3, P + 1])
        quot_i = asb("quot_i", [TT, 3, P + 1], I32)
        ids = asb("ids", [P, B, NT, 3], I32)
        ids_now = asb("ids_now", [P, NT * 3], I32)

        gram = asb("gram", [P, 4, 3, C])
        gramT = asb("gramT", [P, 4, 3, P])
        h = asb("h", [P, 2 * NT, C])
        st1 = asb("st1", [P, NT, 6])
        mv1 = asb("mv1", [P, NT, 2])
        rstd1 = asb("rstd1", [P, NT])
        xn = asb("xn", [P, NT, C])
        xT_hi = asb("xT_hi", [P, S + 2], F32R)
        xT_lo = asb("xT_lo", [P, S + 2], F32R)
        square = xn[:].bitcast(BF16)
        norm = asb("norm", [P, NT * 2])
        inv_norm = asb("inv_norm", [P, NT * 2])
        down_hi = asb("down_hi", [P, SD], F32R)
        down_lo = asb("down_lo", [P, SD], F32R)
        q_hi = [asb(f"q_hi{i}", [P, S], F32R) for i in range(BR)]
        q_lo = [asb(f"q_lo{i}", [P, S], F32R) for i in range(BR)]
        k_hi = [asb(f"k_hi{i}", [P, S if i else SD], F32R) for i in range(BR)]
        k_lo = [asb(f"k_lo{i}", [P, S if i else SD], F32R) for i in range(BR)]
        v0 = asb("v0", [P, SD // P, 2, VW], F32R)
        v12 = asb("v12", [P, NT, 2, 2, VW], F32R)

        neg_max = asb("neg_max", [P, 4])
        exp_sum = asb("exp_sum", [P, 4, BR])
        probs = asb("probs", [P, 2, S])
        qk_raw = probs[:].rearrange("p a (t c) -> p (a t) c", c=2 * C)
        pT_hi = asb("pT_hi", [P, 2, S], F32R)
        pT_lo = asb("pT_lo", [P, 2, S], F32R)

        st = asb("st", [P, 2, BR, 6])
        mv = asb("mv", [P, 2, BR, 2])
        o = asb("o", [P, 4, BR, VW])
        sum_sq = asb("sum_sq", [P, 2, BR])
        var_eps = asb("var_eps", [P, 2, BR])
        rstd = asb("rstd", [P, 2, BR])
        logit9 = asb("logit9", [P, 2, 3, BR + 1])
        logit = asb("logit", [P, 2, 3])
        logit_nm = asb("logit_nm", [P, 2])
        gate_e = asb("gate_e", [P, 2, 3])
        gate_sum = asb("gate_sum", [P, 2])
        gate_inv = asb("gate_inv", [P, 2])
        gate = asb("gate", [P, 2, 3])
        gate_r = asb("gate_r", [P, 2, 3])
        u = asb("u", [P, 2, BR, C])
        zb = asb("zb", [P, 2, BR, C])
        h1 = asb("h1", [P, NT, C])
        st2 = asb("st2", [P, 2, 6])
        mv2 = asb("mv2", [P, 2, 2])
        ve2 = asb("ve2", [P, 2])
        rstd2 = asb("rstd2", [P, 2])
        trow = asb("trow", [P, NT, XW])
        x2T = w[:, 0:S]
        r_log, r_sub, r_exp = (wide[:, 2 * i:2 * i + 2, :].rearrange("p a (t e) -> p (a t) e", e=NE) for i in range(3))
        r_nm = asb("r_nm", [P, NT])
        r_sum = asb("r_sum", [P, NT])
        r_inv = asb("r_inv", [P, NT])

        loaded = sem("loaded")
        tok_loaded = sem("tok_loaded")
        setup_v = sem("setup_v")
        setup_t = sem("setup_t")
        setup_g = sem("setup_g")
        ids_ready = sem("ids_ready")
        ids_turned = sem("ids_turned")
        weights_ready = sem("weights_ready")
        staged = sem("staged")
        gathered = [sem(f"gathered{j}") for j in range(4)]
        bank_full = sem("bank_full")
        bank_a = sem("bank_a")
        bank_v = sem("bank_v")
        gram_turned = sem("gram_turned")
        gram_copied = sem("gram_copied")
        token_done = sem("token_done")
        h_added = sem("h_added")
        ln1_stats = sem("ln1_stats")
        ln1_mv = sem("ln1_mv")
        ln1_g = sem("ln1_g")
        ln1_rstd = sem("ln1_rstd")
        x_ready = sem("x_ready")
        sq_ready = sem("sq_ready")
        norm_g = sem("norm_g")
        norm_v = sem("norm_v")
        qk_ready = sem("qk_ready")
        scored = sem("scored")
        maxed = sem("maxed")
        exped = sem("exped")
        turn_done = sem("turn_done")
        hi_done = sem("hi_done")
        lo_done = sem("lo_done")
        pv_done = sem("pv_done")
        o_ok = sem("o_ok")
        o_stats = sem("o_stats")
        o_mv = sem("o_mv")
        rstd_g = sem("rstd_g")
        rstd_ok = sem("rstd_ok")
        logit_c = sem("logit_c")
        logit_ok = sem("logit_ok")
        gate_ok = sem("gate_ok")
        gate_c = sem("gate_c")
        gate_r_ok = sem("gate_r_ok")
        scale_ok = sem("scale_ok")
        u_ok = sem("u_ok")
        z_g = sem("z_g")
        h1_ok = sem("h1_ok")
        st2_ok = sem("st2_ok")
        mv2_ok = sem("mv2_ok")
        ve2_ok = sem("ve2_ok")
        rstd2_ok = sem("rstd2_ok")
        x2_ok = sem("x2_ok")
        x2_turned = sem("x2_turned")
        x2T_ok = sem("x2T_ok")
        routed = sem("routed")
        route_v = sem("route_v")
        route_e = sem("route_e")
        prob_ok = sem("prob_ok")
        prob_kept = sem("prob_kept")
        h1_stored = sem("h1_stored")
        row_stored = sem("row_stored")
        h1_free = sem("h1_free")
        rows_free = sem("rows_free")

        def W(name, a=0, n=None):
            lo, hi = WCOL[name]
            return w[:, lo + a:(lo + a + n if n else hi)]

        def split(name, a=0, n=None):
            lo, hi = WCOL[name]
            hi = lo + a + n if n else hi
            return w_hi[:, lo + a:hi], w_lo[:, lo + a:hi]

        def R(name):
            return row[:, ROW[name][0]:ROW[name][1]]

        def K(name):
            return con[:, CON[name][0]:CON[name][1]]

        ident = K("ident")

        def gramT_of(t):
            return gramT[:, 0 if t == 0 else 3 if t == NT - 1 else 1 + t % 2]

        def spare(t):
            return scores[:, (t % 2) * S + 512:(t % 2) * S + S]

        def first_psum(t):
            return mixed[:, t % 2 * 512:t % 2 * 512 + C]

        def token_psum(t):
            return scores[:, 0:C] if t == NT - 1 else spare(t + 1)[:, 3 * P:3 * P + C]

        def bank(k):
            return scores[:, (k % 4) * 512:(k % 4 + 1) * 512]

        def mixed_of(i):
            return mixed[:, (i % 2) * 512:(i % 2) * 512 + 2 * VW]

        tokens_out = out.rearrange("b (t p) c -> p (b t) c", p=P)
        table_out = table.rearrange("(t p) x -> p t x", p=P)

        first_part = nc.Block()
        block = first_part.__enter__()


        @block.sync
        def _(sp):
            xf = x_tok.rearrange("b (t p) -> (b t) p", p=P)
            sp.wait_ge(setup_g, 1)
            sp.dma_start(xwi[:, 2:P + 2], xf).then_inc(tok_loaded, 16)
            sp.dma_start(xwi[1:TT, 0:2], xf[0:TT - 1, P - 2:P]).then_inc(tok_loaded, 16)
            sp.dma_start(xwi[0:TT - 1, P + 2:P + 3], xf[1:TT, 0:1], allow_slow_non_contiguous=True).then_inc(tok_loaded, 16)
            sp.dma_start(con[:], consts).then_inc(loaded, 16)
            sp.dma_start(row[:], rows).then_inc(loaded, 16)
            sp.dma_start(col[:], cols).then_inc(loaded, 16)
            sp.dma_start(w[:], weights).then_inc(loaded, 16)

            sp.nop().then_inc(h1_free, 1)
            sp.nop().then_inc(rows_free, 1)
            with sp.Fori(0, B) as b:
                sp.wait_ge(h1_ok, b * NT + NT)
                sp.dma_start(tokens_out[:, bass.ds(b * NT, NT), :], h1[:]).then_inc(h1_stored, 16)
                sp.wait_ge(prob_ok, b + 1)
                sp.dma_start(table_out[:, bass.ds(b * NT, NT), :], trow[:]).then_inc(row_stored, 16)
                sp.wait_ge(h1_stored, 16 * b + 16)
                sp.nop().then_inc(h1_free, 1)
                sp.wait_ge(row_stored, 16 * b + 16)
                sp.nop().then_inc(rows_free, 1)

        @block.tensor
        def _(pe):
            def product(dst, lhs, rhs, first_one=True, last_one=True):
                pe.matmul(dst, lhs[0], rhs[0], start=first_one, stop=False)
                pe.matmul(dst, lhs[0], rhs[1], start=False, stop=False)
                return pe.matmul(dst, lhs[1], rhs[0], start=False, stop=last_one)

            def setup():
                pe.wait_ge(loaded, 64)
                pe.wait_ge(ids_ready, 1)
                for g in range(3):
                    last = pe.transpose(turned[:, g * TT:(g + 1) * TT],
                                        hashed[:, g, (1 if g < 2 else 0):(1 if g < 2 else 0) + P], ident[0:TT, 0:TT])
                last.then_inc(ids_turned, 1)
                pe.wait_ge(setup_g, 8)
                pe.wait_ge(setup_v, 3)
                pe.matmul(bank(0)[:, 0:9], mean_w[:], gate_w[:], start=True, stop=True).then_inc(setup_t, 1)
                pe.wait_ge(setup_v, 7)
                for i in range(BR):
                    pe.matmul(bank(1)[:, 3 * i:3 * i + 3], W("v_nat", i * C, C), gate_w[:, 3 * i:3 * i + 3],
                              start=True, stop=True)
                for i in range(BR):
                    pe.matmul(bank(2)[:, 3 * i:3 * i + 3], wide[:, i, :], gate_w[:, 3 * i:3 * i + 3],
                              start=True, stop=True)
                for i in range(BR):
                    last = pe.matmul(bank(3)[:, 0:3], wide[:, 3 + i, :], col[:, COL["gw"] + 3 * i:COL["gw"] + 3 * i + 3],
                                     start=(i == 0), stop=(i == BR - 1))
                last.then_inc(setup_t, 1)
                pe.wait_ge(weights_ready, 2)

            def open_bank(b, k, high_of=-1, low_of=-1):
                if k < 4 and (not isinstance(b, int) or b > 0):
                    pe.wait_ge(exped, b * UNITS)
                who = USES[k - 4][1] if k >= 4 else ""
                a_count = max(reads("a", k - 4) if "a" in who else 0, reads("a", high_of) if high_of >= 0 else 0)
                v_count = max(reads("v", k - 4) if "v" in who else 0, reads("v", low_of) if low_of >= 0 else 0)
                if a_count:
                    pe.wait_ge(bank_a, b * A_READS + a_count)
                if v_count:
                    pe.wait_ge(bank_v, b * V_READS + v_count)

            def turn_gram(s, t):
                pe.wait_ge(gathered[t % 4], (s * (NT // 4) + t // 4 + 1) * (3 * 16))
                for g in range(3):
                    last = pe.transpose(spare(t)[:, g * P:(g + 1) * P], gram[:, t % 4, g, :], ident)
                last.then_inc(gram_turned, 1)

            def token(s, t, dst):
                pe.wait_ge(gram_copied, s * NT + t + 1)
                for g in range(3):
                    last = pe.matmul(dst, gramT_of(t)[:, g, :], W("proj", g * C, C), start=(g == 0), stop=(g == 2))
                last.then_inc(token_done, 1)

            def prologue(b, tail):
                pe.wait_ge(h_added, b * NT + NT)
                for half in range(2):
                    k = first("xT") + half
                    open_bank(b, k)
                    pe.wait_ge(x_ready, b * NT + half * 4 + 4)
                    for j in range(4):
                        last = pe.transpose(bank(k)[:, j * P:(j + 1) * P], xn[:, half * 4 + j, :], ident)
                    last.then_inc(bank_full, 1)

                def xT_tile(t):
                    return xT_hi[:, 2 + t * P:2 + (t + 1) * P], xT_lo[:, 2 + t * P:2 + (t + 1) * P]

                def xT_half(half):
                    return xT_hi[:, 2 + half * 512:514 + half * 512], xT_lo[:, 2 + half * 512:514 + half * 512]

                for i in range(4):
                    k = first("qk_raw") + i
                    open_bank(b, k, first("xT") + i // 2, first("xT") + i // 2)
                    for j in range(2):
                        last = product(bank(k)[:, j * 2 * C:(j + 1) * 2 * C], xT_tile(2 * i + j), split("qk_c"))
                    last.then_inc(bank_full, 1)
                k = first("down")
                open_bank(b, k)
                for tap in range(3):
                    last = product(bank(k), split("conv", tap * C, C),
                                   (xT_hi[:, tap + 1:tap + 1 + S - 1:2], xT_lo[:, tap + 1:tap + 1 + S - 1:2]),
                                   tap == 0, tap == 2)
                last.then_inc(bank_full, 1)
                for name in ("q_d", "k_d", "q_cr"):
                    for half in range(2):
                        k = first(name) + half
                        open_bank(b, k)
                        product(bank(k), split(name), xT_half(half)).then_inc(bank_full, 1)
                k = first("k_cr")
                open_bank(b, k, first("down"), first("down"))
                product(bank(k), split("k_cr"), (down_hi[:], down_lo[:])).then_inc(bank_full, 1)
                for i in range(2):
                    k = first("v_cr") + i
                    open_bank(b, k)
                    for j in range(2):
                        t = 2 * i + j
                        dst = bank(k)[:, j * VW:(j + 1) * VW]
                        pe.matmul(dst, one_row[:], bv_hi[:, 0:VW], start=True, stop=False)
                        pe.matmul(dst, one_row[:], bv_lo[:, 0:VW], start=False, stop=False)
                        last = product(dst, (down_hi[:, t * P:(t + 1) * P], down_lo[:, t * P:(t + 1) * P]),
                                       split("v_cr"), False)
                    last.then_inc(bank_full, 1)
                if tail is not None:
                    pe.wait_ge(x2_ok, tail * NT + NT)
                    pe.wait_ge(lo_done, (tail + 1) * PARTS)
                    route_turn()
                for t in range(NT):
                    if tail is not None and t == 3:
                        pe.wait_ge(o_ok, (tail + 1) * UNITS - 1)
                        route_product(tail)
                    k = first("v_dc") + t
                    open_bank(b, k)
                    dst = bank(k)[:, 0:2 * VW]
                    pe.matmul(dst, one_row[:], bv_hi[:, VW:3 * VW], start=True, stop=False)
                    pe.matmul(dst, one_row[:], bv_lo[:, VW:3 * VW], start=False, stop=False)
                    w0, w1 = WCOL["v_d"][0], WCOL["v_c"][1]
                    product(dst, xT_tile(t), (w_hi[:, w0:w1], w_lo[:, w0:w1]), False).then_inc(bank_full, 1)
                for which, name in enumerate(("q_c", "k_c")):
                    for half in range(2):
                        k = first(name) + half
                        open_bank(b, k)
                        pe.wait_ge(qk_ready, b * 2 + half + 1)
                        for j in range(4):
                            last = pe.transpose(bank(k)[:, j * P:(j + 1) * P],
                                                qk_raw[:, half * 4 + j, which * C:(which + 1) * C], ident)
                        last.then_inc(bank_full, 1)
                if tail is not None:
                    pe.wait_ge(o_ok, (tail + 1) * UNITS)
                    pe.wait_ge(route_v, tail * 5 + 1)

            def route_turn():
                for t in range(NT):
                    last = pe.transpose(turned[:, t * P:(t + 1) * P], trow[:, t, 0:C], ident)
                last.then_inc(x2_turned, 1)

            def route_product(b):
                pe.wait_ge(x2T_ok, b + 1)
                for t in range(NT):
                    last = pe.matmul(mixed[:, t * NE:(t + 1) * NE], x2T[:, t * P:(t + 1) * P], W("router"),
                                     start=True, stop=True)
                last.then_inc(routed, 1)

            def attention(b, more):
                def turn(i):
                    pe.wait_ge(exped, b * UNITS + i + 1)
                    for half in range(1 if i % BR == 0 else 2):
                        before = i - 1 if half == 0 or i % BR == 2 else i - 2
                        if before >= 0:
                            pe.wait_ge(lo_done, b * PARTS + part(before, half))
                        for j in range(half * 4, half * 4 + 4):
                            last = pe.transpose(turned[:, j * P:(j + 1) * P], probs[:, i % 2, j * P:(j + 1) * P], ident)
                        last.then_inc(turn_done, 1)

                def score(i):
                    t, br = i // BR, i % BR
                    if more and br == 2:
                        pe.wait_ge(gram_copied, b * NT + NT + t + 1)
                        if t > 0:
                            pe.wait_ge(h_added, b * NT + NT + t)
                    if i >= 2:
                        pe.wait_ge(exped, b * UNITS + i - 1)
                    elif i == 1:
                        pe.wait_ge(bank_a, b * A_READS + A_READS)
                        pe.wait_ge(bank_v, b * V_READS + V_READS)
                    else:
                        pe.wait_ge(bank_a, b * A_READS + A_READS - 3)
                        pe.wait_ge(bank_v, b * V_READS + V_READS - 3)
                    lhs = q_hi[br][:, t * P:(t + 1) * P], q_lo[br][:, t * P:(t + 1) * P]
                    for half in range(1 if br == 0 else 2):
                        at = (i % 2) * S + half * 512
                        last = product(scores[:, at:at + 512], lhs, (k_hi[br][:, half * 512:(half + 1) * 512],
                                                                     k_lo[br][:, half * 512:(half + 1) * 512]))
                    last.then_inc(scored, 1)

                def mix(i):
                    t, br = i // BR, i % BR
                    pe.wait_ge(hi_done, b * PARTS + part(i))
                    pe.wait_ge(lo_done, b * PARTS + part(i))
                    if i >= 2:
                        pe.wait_ge(o_ok, b * UNITS + i - 1)
                    n = (SD if br == 0 else S) // P
                    for j in range(n):
                        vals = (v0[:, j, :, :] if br == 0 else v12[:, j, br - 1, :, :]).rearrange("p h c -> p (h c)")
                        parts = [(mixed_of(i), pT_hi, vals), (mixed_of(i)[:, 0:VW], pT_lo, vals[:, 0:VW])]
                        for dst, probabilities, v in (parts[::-1] if j == n - 1 else parts):
                            last = pe.matmul(dst, probabilities[:, i % 2, j * P:(j + 1) * P], v,
                                             start=(j == 0 and v is vals), stop=(j == n - 1 and v is vals))
                    last.then_inc(pv_done, 1)

                for i in range(UNITS + 3):
                    if 0 <= i - 2 < UNITS:
                        turn(i - 2)
                    if i < UNITS:
                        score(i)
                    if more:
                        if i == 1:
                            turn_gram(b + 1, 0)
                        elif i % BR == 0 and 0 < i < UNITS:
                            token(b + 1, i // BR - 1, token_psum(i // BR - 1))
                            turn_gram(b + 1, i // BR)
                        elif i == UNITS:
                            token(b + 1, NT - 1, token_psum(NT - 1))
                    if 0 <= i - 3 < UNITS:
                        mix(i - 3)

            setup()
            for t in range(NT + 1):
                if t < NT:
                    if t >= 2:
                        pe.wait_ge(gram_copied, t - 1)
                    turn_gram(0, t)
                if t > 0:
                    if t >= 3:
                        pe.wait_ge(h_added, t - 2)
                    token(0, t - 1, first_psum(t - 1))
            prologue(0, None)
            with pe.Fori(0, B - 1) as b:
                attention(b, True)
                prologue(b + 1, b)
            attention(B - 1, False)
            pe.wait_ge(x2_ok, TT)
            pe.wait_ge(lo_done, B * PARTS)
            route_turn()
            pe.wait_ge(o_ok, B * UNITS - 1)
            route_product(B - 1)

        @block.vector
        def _(dve):
            def setup():
                n = [0]

                def step(ins):
                    n[0] += 1
                    ins.then_inc(setup_v, 1)

                dve.wait_ge(loaded, 64)
                for i in range(BR):
                    step(dve.tensor_scalar(gate_w[:, 3 * i:3 * i + 3], col[:, COL["gw"] + 3 * i:COL["gw"] + 3 * i + 3],
                                           col[:, COL["ln_g"] + i:COL["ln_g"] + i + 1], None, ALU.mult))
                dve.wait_ge(setup_t, 1)
                step(dve.tensor_copy(gate_mean[:], bank(0)[:, 0:9]))
                dve.wait_ge(setup_v, 4)
                step(dve.tensor_tensor(gate_w[:], gate_w[:], gate_mean[:], ALU.subtract))
                dve.wait_ge(setup_g, 8)
                for i in range(BR):
                    dve.tensor_scalar(wide[:, i, :], wide[:, i, :], col[:, COL["bv"] + i:COL["bv"] + i + 1], None, ALU.add)
                    last = dve.tensor_scalar(wide[:, 3 + i, :], wide[:, 3 + i, :],
                                             col[:, COL["ln_b"] + i:COL["ln_b"] + i + 1], None, ALU.add)
                step(last)
                step(dve.tensor_scalar(inv_temp[:], R("temp"), 0.01, None, ALU.max))
                for name in ("q_cr", "q_d"):
                    dve.tensor_scalar(W(name), W(name), SCALE, None, ALU.mult)
                    last = dve.tensor_scalar(col[:, COL["b" + name]:COL["b" + name] + 1],
                                             col[:, COL["b" + name]:COL["b" + name] + 1], SCALE, None, ALU.mult)
                step(last)
                dve.wait_ge(setup_v, 8)
                step(dve.reciprocal(inv_temp[:], inv_temp[:]))
                for i in range(BR):
                    dve.memset(bv_ext[:, i * VW + C + 3:(i + 1) * VW], 0.0)
                for i, name in enumerate(("v_cr", "v_d", "v_c")):
                    dve.tensor_reduce(v_mean[:, i:i + 1], W(name, 0, C), AX_X, ALU.add, negate=True)
                    last = dve.tensor_reduce(v_mean[:, BR + i:BR + i + 1], R("bv")[:, i * C:(i + 1) * C], AX_X, ALU.add,
                                             negate=True)
                step(last)
                dve.wait_ge(setup_v, 10)
                step(dve.tensor_scalar(v_mean[:], v_mean[:], 1.0 / C, None, ALU.mult))
                dve.wait_ge(setup_v, 11)
                for i, name in enumerate(("v_cr", "v_d", "v_c")):
                    dve.tensor_scalar(W(name, 0, C), W(name, 0, C), v_mean[:, i:i + 1], None, ALU.add)
                    dve.tensor_scalar(bv_ext[:, i * VW:i * VW + C], R("bv")[:, i * C:(i + 1) * C],
                                      v_mean[:, BR + i:BR + i + 1], None, ALU.add)
                dve.wait_ge(setup_t, 2)
                for i, name in enumerate(("v_cr", "v_d", "v_c")):
                    dve.tensor_copy(W(name, C, 3), bank(1)[:, 3 * i:3 * i + 3])
                    last = dve.tensor_copy(bv_ext[:, i * VW + C:i * VW + C + 3], bank(2)[:, 3 * i:3 * i + 3])
                step(last)
                for m in range(2):
                    last = dve.tensor_tensor(logit9[:, m, :, BR:BR + 1], bank(3)[:, 0:3].unsqueeze(2), R("gb").unsqueeze(2), ALU.add)
                step(last)
                dve.wait_ge(setup_v, 13)
                dve.tensor_copy(w_hi[:], w[:, 0:WSPLIT])
                step(dve.tensor_copy(bv_hi[:], bv_ext[0:1, :]))
                dve.wait_ge(setup_v, 14)
                dve.tensor_tensor(w_lo[:], w[:, 0:WSPLIT], w_hi[:].bitcast(F32), ALU.subtract)
                dve.tensor_tensor(bv_lo[:], bv_ext[0:1, :], bv_hi[:].bitcast(F32), ALU.subtract).then_inc(weights_ready, 1)
                dve.wait_ge(setup_g, 8)
                dve.tensor_copy(one_row[:], ones_row[:]).then_inc(weights_ready, 1)

            def hashes():
                n = [0]

                def step(ins):
                    n[0] += 1
                    ins.then_inc(norm_v, 1)
                    dve.wait_ge(norm_v, n[0])

                dve.wait_ge(tok_loaded, 48)
                step(dve.tensor_copy(xw[:], xwi[:]))

                def modulo(v, quot, quot_i):
                    step(dve.tensor_scalar(quot, v, 1.0 / VOCAB, None, ALU.mult))
                    step(dve.tensor_copy(quot_i, quot))
                    step(dve.tensor_copy(quot, quot_i))
                    step(dve.scalar_tensor_tensor(out=v, in0=quot, scalar=-float(VOCAB), in1=v,
                                                  op0=ALU.mult, op1=ALU.add))
                    step(dve.tensor_scalar(quot, v, 0.0, float(VOCAB), ALU.is_lt, ALU.mult))
                    step(dve.tensor_tensor(v, v, quot, ALU.add))
                    step(dve.tensor_scalar(quot, v, float(VOCAB), -float(VOCAB), ALU.is_ge, ALU.mult))
                    step(dve.tensor_tensor(v, v, quot, ALU.add))

                def longer(g, n):
                    step(dve.scalar_tensor_tensor(out=hashed[:, g, 0:n], in0=(hashed[:, g - 1, 0:n] if g else xw[:, 0:n]),
                                                  scalar=64.0, in1=xw[:, g + 1:g + 1 + n], op0=ALU.mult, op1=ALU.add))

                longer(0, P + 1)
                longer(1, P + 1)
                modulo(hashed[:, 0:2, :], quot[:, 0:2, :], quot_i[:, 0:2, :])
                longer(2, P)
                modulo(hashed[:, 2, 0:P], quot[:, 2, 0:P], quot_i[:, 2, 0:P])
                dve.engine_nop().then_inc(ids_ready, 1)
                dve.wait_ge(ids_turned, 1)
                for g in range(3):
                    last = dve.tensor_copy(ids[:].rearrange("p b t g -> p (b t) g")[:, :, g],
                                           turned[:, g * TT:(g + 1) * TT])
                last.then_inc(ids_ready, 1)
                return n[0]

            NORM0 = [0]

            def low(b, k, dst, src, hi):
                dve.wait_ge(bank_full, b * NUSE + k + 1)
                dve.wait_ge(bank_a, b * A_READS + reads("a", k))
                dve.tensor_tensor(dst, src, hi.bitcast(F32), ALU.subtract).then_inc(bank_v, 1)

            def low_bias(b, k, dst, src, bias, hi):
                dve.wait_ge(bank_full, b * NUSE + k + 1)
                dve.wait_ge(bank_a, b * A_READS + reads("a", k))
                dve.scalar_tensor_tensor(out=dst, in0=src, scalar=bias, in1=hi.bitcast(F32), op0=ALU.add,
                                         op1=ALU.subtract).then_inc(bank_v, 1)

            def token_add(s, t, src):
                dve.wait_ge(token_done, s * NT + t + 1)
                if src is not first_psum and t < NT - 1:
                    dve.wait_ge(gram_copied, s * NT + t + 2)
                dve.tensor_tensor(h[:, bass.ds((s % 2) * NT + t, 1), :], src(t).unsqueeze(1),
                                  R("proj_b").unsqueeze(1), ALU.add).then_inc(h_added, 1)

            def token_stats(s, t):
                dve.wait_ge(h_added, s * NT + t + 1)
                dve.nop(nofuse=True)
                dve.bn_stats(st1[:, t, :], h[:, bass.ds((s % 2) * NT + t, 1), :]).then_inc(ln1_stats, 1)
                dve.wait_ge(ln1_stats, s * NT + t + 1)
                dve.nop(nofuse=True)
                dve.bn_aggr(mv1[:, t, :], st1[:, t, :]).then_inc(ln1_mv, 1)

            def normalise(s, half):
                dve.wait_ge(ln1_rstd, s * 2 + half + 1)
                for t in range(half * 4, half * 4 + 4):
                    dve.tensor_scalar(xn[:, t, :], h[:, bass.ds((s % 2) * NT + t, 1), :], mv1[:, t, 0:1], rstd1[:, t:t + 1],
                                      ALU.subtract, ALU.mult).then_inc(x_ready, 1)

            def prologue(b, tail):
                for half in range(2):
                    k = first("xT") + half
                    at = slice(2 + half * 512, 514 + half * 512)
                    low(b, k, xT_lo[:, at], bank(k), xT_hi[:, at])
                if tail is not None:
                    tile_gate(tail, NT - 2)
                    tile_gate_logits(tail, NT - 1)
                    tile_h1_stats(tail, NT - 3)
                for i in range(4):
                    k = first("qk_raw") + i
                    dve.wait_ge(bank_full, b * NUSE + k + 1)
                    dve.tensor_tensor(qk_raw[:, 2 * i:2 * i + 2, :], bank(k).rearrange("p (t c) -> p t c", c=2 * C),
                                      R("bqk_c").unsqueeze(1).to_broadcast([P, 2, 2 * C]), ALU.add).then_inc(bank_v, 1)
                    if tail is not None and i == 0:
                        tile_gate(tail, NT - 1)
                    if tail is not None and i == 2:
                        tile_h1_stats(tail, NT - 2)
                low_bias(b, first("down"), down_lo[:], bank(first("down")), col[:, COL["db"]:COL["db"] + 1], down_hi[:])
                if tail is not None:
                    tile_h1_stats(tail, NT - 1)
                for br, which, name in ((1, q_lo, "q_d"), (1, k_lo, "k_d"), (0, q_lo, "q_cr")):
                    for half in range(2):
                        k = first(name) + half
                        at = slice(half * 512, half * 512 + 512)
                        hi = (q_hi if which is q_lo else k_hi)[br][:, at]
                        low_bias(b, k, which[br][:, at], bank(k), col[:, COL["b" + name]:COL["b" + name] + 1], hi)
                low_bias(b, first("k_cr"), k_lo[0][:], bank(first("k_cr")), col[:, COL["bk_cr"]:COL["bk_cr"] + 1],
                         k_hi[0][:])
                n0 = NORM0[0]
                dve.wait_ge(norm_g, b * 2 + 2)
                dve.reciprocal(inv_norm[:], norm[:]).then_inc(norm_v, 1)
                dve.wait_ge(norm_v, n0 + b * 2 + 1)
                dve.tensor_scalar(inv_norm[:, 0:2 * NT:2], inv_norm[:, 0:2 * NT:2], inv_temp[:, 0:1], None,
                                  ALU.mult).then_inc(norm_v, 1)
                dve.wait_ge(norm_v, n0 + b * 2 + 2)
                for half in range(2):
                    part = qk_raw[:, half * 4:half * 4 + 4, :].rearrange("p t (w c) -> p (t w) c", c=C)
                    dve.tensor_tensor(part, part, inv_norm[:, half * 8:half * 8 + 8].unsqueeze(2).to_broadcast([P, 8, C]),
                                      ALU.mult).then_inc(qk_ready, 1)
                for i in range(2):
                    k = first("v_cr") + i
                    low(b, k, v0[:, 2 * i:2 * i + 2, 1, :], bank(k)[:, 0:2 * VW].rearrange("p (t c) -> p t c", c=VW),
                        v0[:, 2 * i:2 * i + 2, 0, :])
                for t in range(NT):
                    k = first("v_dc") + t
                    low(b, k, v12[:, t, :, 1, :], bank(k)[:, 0:2 * VW].rearrange("p (i c) -> p i c", c=VW),
                        v12[:, t, :, 0, :])
                    if tail is not None and t == 4:
                        route_softmax_1(tail)
                if tail is not None:
                    route_softmax_2(tail)
                for which, name in ((0, "q_c"), (1, "k_c")):
                    for half in range(2):
                        k = first(name) + half
                        at = slice(half * 512, half * 512 + 512)
                        low(b, k, (k_lo if which else q_lo)[2][:, at], bank(k), (k_hi if which else q_hi)[2][:, at])

            def output(b, i):
                t, br = i // BR, i % BR
                dve.wait_ge(pv_done, b * UNITS + i + 1)
                dve.tensor_reduce(o[:, t % 4, br, :], mixed_of(i).rearrange("p (h c) -> p c h", h=2), AX_X,
                                  ALU.add).then_inc(o_ok, 1)

            def tile_stats(b, t):
                m = t % 2
                dve.wait_ge(o_ok, b * UNITS + BR * t + BR)
                for br in range(BR):
                    last = dve.bn_stats(st[:, m, br, :], o[:, t % 4, br, 0:C])
                last.then_inc(o_stats, 1)
                dve.wait_ge(o_stats, b * NT + t + 1)
                dve.nop(nofuse=True)
                for br in range(BR):
                    last = dve.bn_aggr(mv[:, m, br, :], st[:, m, br, :])
                last.then_inc(o_mv, 1)

            def tile_gate_logits(b, t):
                m, n = t % 2, b * NT + t
                dve.wait_ge(rstd_ok, n + 1)
                dve.tensor_tensor(logit9[:, m, :, 0:BR], o[:, t % 4, :, C:C + 3].rearrange("p i g -> p g i"),
                                  rstd[:, m, :].unsqueeze(1).to_broadcast([P, 3, BR]), ALU.mult).then_inc(logit_c, 1)
                dve.wait_ge(logit_c, n * 2 + 1)
                dve.tensor_reduce(logit[:, m, :], logit9[:, m, :, :], AX_X, ALU.add).then_inc(logit_c, 1)
                dve.wait_ge(logit_c, n * 2 + 2)
                dve.tensor_reduce(logit_nm[:, m:m + 1], logit[:, m, :], AX_X, ALU.max, negate=True).then_inc(logit_ok, 1)

            def tile_gate(b, t):
                m, n = t % 2, b * NT + t
                dve.wait_ge(gate_ok, n + 1)
                dve.reciprocal(gate_inv[:, m:m + 1], gate_sum[:, m:m + 1]).then_inc(gate_c, 1)
                dve.wait_ge(gate_c, n + 1)
                dve.scalar_tensor_tensor(out=gate_r[:, m, :], in0=gate_e[:, m, :], scalar=gate_inv[:, m:m + 1],
                                         in1=rstd[:, m, :], op0=ALU.mult, op1=ALU.mult).then_inc(gate_r_ok, 1)
                dve.tensor_scalar(gate[:, m, :], gate_e[:, m, :], gate_inv[:, m:m + 1], None, ALU.mult).then_inc(scale_ok, 1)
                dve.wait_ge(gate_r_ok, n + 1)
                if t >= 2:
                    dve.wait_ge(h1_ok, n - 1)
                for br in range(BR):
                    last = dve.scalar_tensor_tensor(out=u[:, m, br, :], in0=o[:, t % 4, br, 0:C],
                                                    scalar=gate_r[:, m, br:br + 1], in1=R("ln_g")[:, br * C:(br + 1) * C],
                                                    op0=ALU.mult, op1=ALU.mult)
                last.then_inc(u_ok, 1)

            def tile_h1_stats(b, t):
                m, n = t % 2, b * NT + t
                dve.wait_ge(h1_ok, n + 1)
                dve.bn_stats(st2[:, m, :], h1[:, t, :]).then_inc(st2_ok, 1)
                dve.wait_ge(st2_ok, n + 1)
                dve.nop(nofuse=True)
                dve.bn_aggr(mv2[:, m, :], st2[:, m, :]).then_inc(mv2_ok, 1)

            def route_softmax_1(b):
                dve.wait_ge(routed, b + 1)
                dve.tensor_tensor(r_log, mixed[:, 0:NT * NE].rearrange("p (t e) -> p t e", e=NE),
                                  R("b_router").unsqueeze(1).to_broadcast([P, NT, NE]), ALU.add).then_inc(route_v, 1)
                dve.wait_ge(route_v, b * 5 + 1)
                dve.tensor_reduce(r_nm[:], r_log, AX_X, ALU.max, negate=True).then_inc(route_v, 1)
                dve.wait_ge(route_v, b * 5 + 2)
                dve.tensor_tensor(r_sub, r_log, r_nm[:].unsqueeze(2).to_broadcast([P, NT, NE]),
                                  ALU.add).then_inc(route_v, 1)

            def route_softmax_2(b):
                dve.wait_ge(route_e, b + 1)
                dve.tensor_reduce(r_sum[:], r_exp, AX_X, ALU.add).then_inc(route_v, 1)
                dve.wait_ge(route_v, b * 5 + 4)
                dve.reciprocal(r_inv[:], r_sum[:]).then_inc(route_v, 1)
                dve.wait_ge(route_v, b * 5 + 5)
                dve.tensor_tensor(trow[:, :, C:XW], r_exp, r_inv[:].unsqueeze(2).to_broadcast([P, NT, NE]),
                                  ALU.mult).then_inc(prob_ok, 1)

            def attention(b, more):
                def maxima(i):
                    n = SD if i % BR == 0 else S
                    dve.wait_ge(scored, b * UNITS + i + 1)
                    dve.tensor_reduce(neg_max[:, i % 4:i % 4 + 1], scores[:, (i % 2) * S:(i % 2) * S + n], AX_X,
                                      ALU.max, negate=True).then_inc(maxed, 1)

                def low_part(i):
                    if i >= 2:
                        dve.wait_ge(pv_done, b * UNITS + i - 1)
                    for half in range(1 if i % BR == 0 else 2):
                        at = slice(half * 512, half * 512 + 512)
                        dve.wait_ge(hi_done, b * PARTS + part(i, half))
                        dve.tensor_tensor(pT_lo[:, i % 2, at], turned[:, at], pT_hi[:, i % 2, at].bitcast(F32),
                                          ALU.subtract).then_inc(lo_done, 1)

                for i in range(UNITS + 3):
                    if 0 <= i - 2 < UNITS:
                        low_part(i - 2)
                    if i < UNITS:
                        maxima(i)
                    if i >= 4:
                        output(b, i - 4)
                    for t in range(NT):
                        stage = i - 3 * t - 6
                        if stage == 6:
                            tile_h1_stats(b, t)
                        if stage == 0:
                            tile_stats(b, t)
                        if stage == 2:
                            tile_gate_logits(b, t)
                        if stage == 4:
                            tile_gate(b, t)
                    if more:
                        if i == UNITS + 1:
                            normalise(b + 1, 1)
                        if i % BR == 0 and 0 < i <= UNITS:
                            token_add(b + 1, i // BR - 1, token_psum)
                        if i % BR == 1 and 1 < i < UNITS:
                            token_stats(b + 1, i // BR - 1)
                        if i == UNITS:
                            token_stats(b + 1, NT - 1)
                        if i == 6 * BR:
                            normalise(b + 1, 0)
                output(b, UNITS - 1)
                tile_stats(b, NT - 1)

            NORM0[0] = hashes()
            setup()
            for t in range(NT):
                token_add(0, t, first_psum)
                token_stats(0, t)
                if t == 5:
                    normalise(0, 0)
            normalise(0, 1)
            prologue(0, None)
            with dve.Fori(0, B - 1) as b:
                attention(b, True)
                prologue(b + 1, b)
            attention(B - 1, False)
            tile_gate(B - 1, NT - 2)
            tile_gate_logits(B - 1, NT - 1)
            tile_h1_stats(B - 1, NT - 3)
            tile_gate(B - 1, NT - 1)
            tile_h1_stats(B - 1, NT - 2)
            tile_h1_stats(B - 1, NT - 1)
            route_softmax_1(B - 1)
            route_softmax_2(B - 1)

        @block.scalar
        def _(act):
            def high(b, k, dst, src, bias=0.0):
                act.wait_ge(bank_full, b * NUSE + k + 1)
                act.activation(dst, src, ACT.Identity, bias=bias).then_inc(bank_a, 1)

            def gram_copy(s, t):
                act.wait_ge(gram_turned, s * NT + t + 1)
                src, dst = spare(t)[:, 0:3 * P].rearrange("p (g t) -> p g t", t=P), gramT_of(t)
                for g0, g1, at in (((0, 2, slice(1, P)), (2, 3, slice(2, P))) if t == 0 else
                                   ((0, 1, slice(0, P)), (1, 3, slice(0, P - 1))) if t == NT - 1 else
                                   ((0, 3, slice(0, P)),)):
                    last = act.activation(dst[:, g0:g1, at], src[:, g0:g1, at], ACT.Identity)
                last.then_inc(gram_copied, 1)

            def prologue(b, tail):
                for half in range(2):
                    k = first("xT") + half
                    high(b, k, xT_hi[:, 2 + half * 512:514 + half * 512], bank(k))
                if tail is not None:
                    tile_gate_exp(tail, NT - 1)
                for t in range(NT):
                    act.wait_ge(bank_v, b * V_READS + reads("v", first("qk_raw") + t // 2))
                    for which in range(2):
                        last = act.activation(square[:, t, which * C:(which + 1) * C], qk_raw[:, t, which * C:(which + 1) * C], ACT.Square,
                                              accum_out=norm[:, 2 * t + which:2 * t + which + 1])
                    last.then_inc(sq_ready, 1)
                high(b, first("down"), down_hi[:], bank(first("down")), col[:, COL["db"]:COL["db"] + 1])
                for br, which, name in ((1, q_hi, "q_d"), (1, k_hi, "k_d"), (0, q_hi, "q_cr")):
                    for half in range(2):
                        k = first(name) + half
                        high(b, k, which[br][:, half * 512:half * 512 + 512], bank(k),
                             col[:, COL["b" + name]:COL["b" + name] + 1])
                high(b, first("k_cr"), k_hi[0][:], bank(first("k_cr")), col[:, COL["bk_cr"]:COL["bk_cr"] + 1])
                for i in range(2):
                    k = first("v_cr") + i
                    high(b, k, v0[:, 2 * i:2 * i + 2, 0, :], bank(k)[:, 0:2 * VW].rearrange("p (t c) -> p t c", c=VW))
                if tail is not None:
                    route_copy(tail)
                for t in range(NT):
                    k = first("v_dc") + t
                    high(b, k, v12[:, t, :, 0, :], bank(k)[:, 0:2 * VW].rearrange("p (i c) -> p i c", c=VW))
                if tail is not None:
                    route_exp(tail)
                for which, name in ((0, "q_c"), (1, "k_c")):
                    for half in range(2):
                        k = first(name) + half
                        high(b, k, (k_hi if which else q_hi)[2][:, half * 512:half * 512 + 512], bank(k))

            def route_copy(b):
                act.wait_ge(x2_turned, b + 1)
                act.activation(x2T, turned[:], ACT.Identity).then_inc(x2T_ok, 1)

            def route_exp(b):
                act.wait_ge(route_v, b * 5 + 3)
                act.activation(r_exp, r_sub, ACT.Exp).then_inc(route_e, 1)

            def tile_gate_exp(b, t):
                m = t % 2
                act.wait_ge(logit_ok, b * NT + t + 1)
                act.activation(gate_e[:, m, :], logit[:, m, :], ACT.Exp, bias=logit_nm[:, m:m + 1],
                               accum_out=gate_sum[:, m:m + 1]).then_inc(gate_ok, 1)

            def attention(b, more):
                def exponent(i):
                    t, br = i // BR, i % BR
                    n = SD if br == 0 else S
                    act.wait_ge(maxed, b * UNITS + i + 1)
                    if i >= 2:
                        act.wait_ge(turn_done, b * PARTS + part(i - 2))
                    act.activation(probs[:, i % 2, 0:n], scores[:, (i % 2) * S:(i % 2) * S + n], ACT.Exp,
                                   bias=neg_max[:, i % 4:i % 4 + 1],
                                   accum_out=exp_sum[:, t % 4, br:br + 1]).then_inc(exped, 1)

                def high_part(i):
                    if i >= 2:
                        act.wait_ge(pv_done, b * UNITS + i - 1)
                    for half in range(1 if i % BR == 0 else 2):
                        at = slice(half * 512, half * 512 + 512)
                        act.wait_ge(turn_done, b * PARTS + part(i, half))
                        act.activation(pT_hi[:, i % 2, at], turned[:, at], ACT.Identity).then_inc(hi_done, 1)

                for i in range(UNITS + 3):
                    if 0 <= i - 2 < UNITS:
                        high_part(i - 2)
                    if i < UNITS:
                        exponent(i)
                    for t in range(NT):
                        stage = i - 3 * t - 6
                        if stage == 3:
                            tile_gate_exp(b, t)
                    if more and (i == 1 or i % BR == 0 and 0 < i < UNITS):
                        gram_copy(b + 1, i // BR)
                tile_gate_exp(b, NT - 2)

            act.wait_ge(loaded, 64)
            act.wait_ge(weights_ready, 2)
            for t in range(NT):
                gram_copy(0, t)
            prologue(0, None)
            with act.Fori(0, B - 1) as b:
                attention(b, True)
                prologue(b + 1, b)
            attention(B - 1, False)
            tile_gate_exp(B - 1, NT - 1)
            route_copy(B - 1)
            route_exp(B - 1)

        @block.gpsimd
        def _(pool):
            def gathers(s, t):
                if t >= 4 or not isinstance(s, int) or s > 0:
                    pool.wait_ge(gram_turned, s * NT + t - 3)
                    pool.nop(nofuse=True)
                pool.tensor_copy(ids_now[:, 3 * t:3 * t + 3],
                                 ids[:, bass.ds(s, 1), t, :].rearrange("p b g -> p (b g)")).then_inc(staged, 1)
                pool.wait_ge(staged, s * NT + t + 1)
                pool.nop(nofuse=True)
                for g in range(3):
                    pool.indirect_dma_start(gram[:, t % 4, g, :], None, emb[g],
                                            bass.IndirectOffsetOnAxis(ap=ids_now[:, 3 * t + g:3 * t + g + 1], axis=0)
                                            ).then_inc(gathered[t % 4], 16)

            def token_rstd(s, half):
                part = rstd1[:, half * 4:half * 4 + 4]
                pool.wait_ge(ln1_mv, s * NT + half * 4 + 4)
                pool.nop(nofuse=True)
                pool.tensor_scalar(part, mv1[:, half * 4:half * 4 + 4, 1], LN_EPS, None, ALU.add).then_inc(ln1_g, 1)
                pool.wait_ge(ln1_g, s * 2 + half + 1)
                pool.tensor_tensor(part, part, m_half[:, 0:4], ALU.pow).then_inc(ln1_rstd, 1)

            def prologue(b, tail):
                if tail is not None:
                    last_tiles(tail)
                pool.wait_ge(sq_ready, b * NT + NT)
                pool.tensor_tensor(norm[:], norm[:], p_half[:], ALU.pow).then_inc(norm_g, 1)
                pool.wait_ge(norm_g, b * 2 + 1)
                pool.nop(nofuse=True)
                pool.tensor_scalar(norm[:], norm[:], NORM_EPS, None, ALU.add).then_inc(norm_g, 1)
                if tail is not None:
                    keep_probs(tail)

            def keep_probs(b):
                pool.wait_ge(prob_ok, b + 1)
                pool.tensor_copy(prob[:].rearrange("p (u c) e -> p c u e", c=CHUNKS)[
                    :, bass.ds(b // SEQ_OF_CHUNK, 1), bass.ds((b % SEQ_OF_CHUNK) * NT, NT), :],
                    trow[:, :, C:XW]).then_inc(prob_kept, 1)

            def tile_rstd(b, t):
                m, n = t % 2, b * NT + t
                pool.wait_ge(exped, b * UNITS + BR * t + BR)
                s = exp_sum[:, t % 4, :]
                pool.tensor_tensor(sum_sq[:, m, :], s, s, ALU.mult).then_inc(rstd_g, 1)
                pool.wait_ge(rstd_g, n * 3 + 1)
                pool.nop(nofuse=True)
                pool.tensor_scalar(var_eps[:, m, :], sum_sq[:, m, :], LN_EPS, None, ALU.mult).then_inc(rstd_g, 1)
                pool.wait_ge(rstd_g, n * 3 + 2)
                pool.wait_ge(o_mv, n + 1)
                pool.tensor_tensor(var_eps[:, m, :], var_eps[:, m, :], mv[:, m, :, 1], ALU.add).then_inc(rstd_g, 1)
                pool.wait_ge(rstd_g, n * 3 + 3)
                pool.tensor_tensor(rstd[:, m, :], var_eps[:, m, :], m_half[:, 0:BR], ALU.pow).then_inc(rstd_ok, 1)

            def tile_sum(b, t):
                m, n = t % 2, b * NT + t
                k = [n * 4]

                def step(ins):
                    k[0] = k[0] + 1
                    ins.then_inc(z_g, 1)
                    pool.wait_ge(z_g, k[0])

                pool.wait_ge(scale_ok, n + 1)
                shift = R("ln_b")
                step(pool.tensor_tensor(zb[:, m, :, :], shift.rearrange("p (i c) -> p i c", c=C),
                                        gate[:, m, :].unsqueeze(2).to_broadcast([P, BR, C]), ALU.mult))
                step(pool.tensor_tensor(zb[:, m, 0, :], zb[:, m, 0, :], h[:, bass.ds((b % 2) * NT + t, 1), :], ALU.add))
                pool.wait_ge(u_ok, n + 1)
                step(pool.tensor_tensor(u[:, m, :, :], u[:, m, :, :], zb[:, m, :, :], ALU.add))
                step(pool.tensor_tensor(u[:, m, 0, :], u[:, m, 0, :], u[:, m, 1, :], ALU.add))
                if t == 0:
                    pool.wait_ge(h1_free, b + 1)
                pool.tensor_tensor(h1[:, t, :], u[:, m, 0, :], u[:, m, 2, :], ALU.add).then_inc(h1_ok, 1)

            def tile_x2(b, t):
                m, n = t % 2, b * NT + t
                pool.wait_ge(mv2_ok, n + 1)
                pool.nop(nofuse=True)
                pool.tensor_scalar(ve2[:, m:m + 1], mv2[:, m, 1:2], LN_EPS, None, ALU.add).then_inc(ve2_ok, 1)
                pool.wait_ge(ve2_ok, n + 1)
                pool.tensor_tensor(rstd2[:, m:m + 1], ve2[:, m:m + 1], m_half[:, 0:1], ALU.pow).then_inc(rstd2_ok, 1)
                if t == 0:
                    pool.wait_ge(rows_free, b + 1)
                pool.wait_ge(rstd2_ok, n + 1)
                pool.nop(nofuse=True)
                pool.tensor_scalar(trow[:, t, 0:C], h1[:, t, :], mv2[:, m, 0:1], rstd2[:, m:m + 1],
                                   ALU.subtract, ALU.mult).then_inc(x2_ok, 1)

            def last_tiles(b):
                tile_rstd(b, NT - 1)
                tile_x2(b, NT - 3)
                tile_sum(b, NT - 2)
                tile_sum(b, NT - 1)
                tile_x2(b, NT - 2)
                tile_x2(b, NT - 1)

            def attention(b, more):
                if more:
                    for t in range(4):
                        gathers(b + 1, t)
                for t in range(NT - 1):
                    tile_rstd(b, t)
                    if more and t == 3:
                        token_rstd(b + 1, 0)
                    if more and t == 6:
                        token_rstd(b + 1, 1)
                    if t >= 2:
                        tile_x2(b, t - 2)
                    if t >= 1:
                        tile_sum(b, t - 1)
                    if more and t < 4:
                        gathers(b + 1, t + 4)

            pool.memset(xwi[:], 0).then_inc(setup_g, 1)
            pool.memset(wide[:], 0.0).then_inc(setup_g, 1)
            pool.memset(mean_w[:], 1.0 / C).then_inc(setup_g, 1)
            pool.memset(ones_row[:], 1.0).then_inc(setup_g, 1)
            pool.memset(m_half[:], -0.5).then_inc(setup_g, 1)
            pool.memset(p_half[:], 0.5).then_inc(setup_g, 1)
            pool.memset(xT_hi[:, 0:2].bitcast(F32), 0.0)
            pool.memset(xT_lo[:, 0:2].bitcast(F32), 0.0).then_inc(setup_g, 1)
            pool.memset(gramT[:, 0, :, 0:1], 0.0)
            pool.memset(gramT[:, 0, 2, 1:2], 0.0)
            pool.memset(gramT[:, 3, 1:3, P - 1:P], 0.0).then_inc(setup_g, 1)
            pool.wait_ge(setup_g, 8)
            pool.wait_ge(ids_ready, 2)
            for t in range(NT):
                gathers(0, t)
                if t == 6:
                    token_rstd(0, 0)
            token_rstd(0, 1)
            prologue(0, None)
            with pool.Fori(0, B - 1) as b:
                attention(b, True)
                prologue(b + 1, b)
            attention(B - 1, False)
            last_tiles(B - 1)
            keep_probs(B - 1)

        first_part.__exit__(None, None, None)
        attn.close()
        experts(nc, ctx, con, prob, ones_row, scores, turned, mixed, table, cand_bits, w_up, b_up, w_down, out)


def experts(nc, ctx, con, prob, ones_row, scores, turned, mixed, table, cand_bits, w_up, b_up, w_down, out):
    CT = TT // CHUNKS
    RW = P + 2

    def sb(name, shape, dt=F32):
        return ctx.enter_context(nc.sbuf_tensor(name, shape, dt))

    def sem(name):
        return ctx.enter_context(nc.semaphore(name))

    def K(name):
        return con[:, CON[name][0]:CON[name][1]]

    ident = K("ident")

    bits_i = sb("bits_i", [P, BITS + 1], I32)
    bits_f = sb("bits_f", [P, BITS + 1])
    probT = sb("probT", [P, CT * P])
    above = sb("above", [P, CT * P], BF16)
    count = sb("count", [P, 1])
    cand = sb("cand", [P, 1], I32)
    cand_next = sb("cand_next", [P, 1], I32)
    drop = sb("drop", [P, 1], I32)
    thr_row = sb("thr_row", [NE, P])
    thr = sb("thr", [P, NE])
    ones_bf = sb("ones_bf", [P, P], BF16)
    upto_bf = sb("upto_bf", [P, P], BF16)
    after_bf = sb("after_bf", [P, P], BF16)
    below_bf = sb("below_bf", [P, P], BF16)
    slot_bf = sb("slot_bf", [P, TOPK], BF16)
    over = sb("over", [P, TT, NE], BF16)
    tie = sb("tie", [P, TT, NE], BF16)
    tie_in = sb("tie_in", [P, TT, NE], BF16)
    n_over = sb("n_over", [P, NE])
    room = sb("room", [P, NE])
    tie_tile = sb("tie_tile", [P, NE, TT + 1])
    keep = sb("keep", [P, NE, TT + 1])
    tie_before = sb("tie_before", [P, NE, TT + 1])
    tie_rank = sb("tie_rank", [P, TT, NE])
    chosen = sb("chosen", [P, TT + 1, NE], BF16)
    ranks = sb("ranks", [TT, NE, RW], BF16)
    before = sb("before", [TT, NE])
    reached = sb("reached", [TT, NE, TOPK], BF16)
    less = sb("less", [P, NE * HALVES, P], BF16)
    n_less = sb("n_less", [P, NE * HALVES])
    tile_no = sb("tile_no", [P, NE * HALVES])
    slot_f = sb("slot_f", [P, NE * HALVES])
    slots = sb("slots", [P, NE * HALVES], I32)
    EB = GROUP
    g_ids = sb("g_ids", [P, EB * HALVES], I32)
    s_ids = sb("s_ids", [P, EB * HALVES], I32)
    bup = sb("bup", [FP, NG * FC])
    wu = sb("wu", [P, EB, DFF])
    wd = sb("wd", [FP, EB, FC, C])
    xg = sb("xg", [P, EB, HALVES, XW])
    xT = sb("xT", [P, 2, TOPK])
    hid = sb("hid", [FP, 2, FC, TOPK])
    yw = sb("yw", [P, EB, HALVES, C])

    bits_in = sem("bits_in")
    prob_turned = sem("prob_turned")
    prob_copied = sem("prob_copied")
    made = sem("made")
    made_g = sem("made_g")
    counted = sem("counted")
    totalled = sem("totalled")
    cand_c = sem("cand_c")
    drop_ok = sem("drop_ok")
    cand_ok = sem("cand_ok")
    thr_v = sem("thr_v")
    thr_t = sem("thr_t")
    masks = sem("masks")
    sums_t = sem("sums_t")
    pick_v = sem("pick_v")
    chosen_ok = sem("chosen_ok")
    rank_t = sem("rank_t")
    rank_a = sem("rank_a")
    before_t = sem("before_t")
    before_v = sem("before_v")
    reached_ok = sem("reached_ok")
    row_t = sem("row_t")
    row_v = sem("row_v")
    slots_v = sem("slots_v")
    slots_ok = sem("slots_ok")
    g_staged = sem("g_staged")
    s_staged = sem("s_staged")
    bup_in = sem("bup_in")
    w_in = [sem(f"w_in{j}") for j in range(EB)]
    x_in = [sem(f"x_in{j}") for j in range(EB)]
    xt_t = sem("xt_t")
    xt_v = sem("xt_v")
    up_t = sem("up_t")
    hid_a = sem("hid_a")
    down_t = sem("down_t")
    y_v = sem("y_v")
    added = sem("added")
    ones_set = sem("ones_set")

    rows_out = out.rearrange("b s c -> (b s) c")

    def wave(e):
        return e // EB + 1

    def slot_bank(k):
        k = k % 8
        return (scores[:, k * 512:(k + 1) * 512] if k < 4 else turned[:, (k - 4) * 512:(k - 3) * 512] if k < 6
                else mixed[:, (k - 6) * 512:(k - 5) * 512])

    row_banks = [(half, e0, min(3, NE - e0)) for e0 in range(0, NE, 3) for half in range(HALVES)]

    block = ctx.enter_context(nc.Block())

    @block.sync
    def _(sp):
        sp.dma_start(bits_i[:], cand_bits[0]).then_inc(bits_in, 16)
        sp.dma_start(bits_f[:], cand_bits[1]).then_inc(bits_in, 16)
        sp.dma_start(bup[:], b_up.rearrange("p g c -> p (g c)")).then_inc(bup_in, 16)

        def load(g, j):
            sp.dma_start(wu[:, j, :], w_up[bass.ds(g, 1), :, :].rearrange("g h f -> (g h) f")).then_inc(w_in[j], 16)
            sp.dma_start(wd[:, j, :, :], w_down[bass.ds(g * GROUP + j, 1), :, :].rearrange("e (c p) h -> p (e c) h", p=FP)
                         ).then_inc(w_in[j], 16)

        for j in range(EB):
            load(0, j)
        with sp.Fori(0, NG - 1) as g:
            for j in range(EB):
                sp.wait_ge(down_t, g * GROUP + j + 1)
                load(g + 1, j)

    @block.tensor
    def _(pe):
        for u in range(CT):
            last = pe.transpose(scores[:, u * P:(u + 1) * P], prob[:, u * CHUNKS:(u + 1) * CHUNKS, :].rearrange("p c e -> p (c e)"), ident)
            if u % 4 == 3:
                last.then_inc(prob_turned, 1)
        with pe.Fori(0, BITS) as k:
            pe.wait_ge(counted, k + 1)
            pe.matmul(turned[:, 0:1], K("same"), count[:], start=True, stop=True).then_inc(totalled, 1)
        pe.wait_ge(thr_v, 1)
        pe.transpose(turned[:, 512:512 + NE], thr_row[:], ident[0:NE, 0:NE]).then_inc(thr_t, 1)
        pe.wait_ge(made, 4)
        pe.wait_ge(made_g, 1)
        pe.wait_ge(masks, 1)
        for q in range(4):
            last = pe.matmul(turned[:, 0:512], ones_bf[:], over[:, q * 16:(q + 1) * 16, :], start=(q == 0), stop=(q == 3))
        last.then_inc(sums_t, 1)
        pe.wait_ge(masks, 2)
        pe.wait_ge(prob_copied, 4)
        for q in range(4):
            last = pe.matmul(scores[:, q * 512:(q + 1) * 512], ones_bf[:], tie[:, q * 16:(q + 1) * 16, :],
                             start=True, stop=True)
        last.then_inc(sums_t, 1)
        pe.wait_ge(pick_v, 1)
        for q in range(4):
            last = pe.matmul(slot_bank(4 + q), upto_bf[:], tie[:, q * 16:(q + 1) * 16, :], start=True, stop=True)
        last.then_inc(sums_t, 1)
        pe.wait_ge(chosen_ok, 1)
        for e in range(NE):
            dst = slot_bank(e // 4)[0:TT, (e % 4) * P:(e % 4 + 1) * P]
            pe.matmul(dst, chosen[:, 1:TT + 1, e], upto_bf[:], start=True, stop=False)
            last = pe.matmul(dst, chosen[:, 0:TT, e], after_bf[:], start=False, stop=True)
            if e % 4 == 3:
                last.then_inc(rank_t, 1)
        pe.wait_ge(rank_a, 8)
        pe.matmul(scores[0:TT, 0:NE], below_bf[0:TT, 0:TT], ranks[:, :, P - 1], start=True, stop=True).then_inc(before_t, 1)
        pe.wait_ge(before_v, 1)
        for n, (half, e0, m) in enumerate(row_banks):
            pe.wait_ge(reached_ok, min(e0 + m, NE))
            if n >= 8:
                pe.wait_ge(row_v, n - 7)
            for i in range(m):
                last = pe.matmul(slot_bank(n)[:, i * RW:(i + 1) * RW], reached[:, e0 + i, half * P:(half + 1) * P],
                                 ranks[:, e0 + i, :], start=True, stop=True)
            last.then_inc(row_t, 1)
        pe.wait_ge(row_v, len(row_banks))

        def turn(e, j):
            pe.wait_ge(x_in[j % EB], wave(e) * 32)
            if not isinstance(e, int) or e >= 2:
                pe.wait_ge(xt_v, e - 1)
            for half in range(HALVES):
                last = pe.transpose(scores[:, (j % 2) * 512 + half * P:(j % 2) * 512 + (half + 1) * P],
                                    xg[:, j % EB, half, 0:C], ident)
            last.then_inc(xt_t, 1)

        def up_bank(j):
            return scores[:, 1024:2048] if j % 2 == 0 else turned[:]

        def up(e, j):
            pe.wait_ge(w_in[j % EB], wave(e) * 32)
            pe.wait_ge(xt_v, e + 1)
            if not isinstance(e, int) or e >= 2:
                pe.wait_ge(hid_a, e - 1)
            for c in range(FC):
                n = FP if c < FC - 1 else FP - 1
                last = pe.matmul(up_bank(j)[0:n, c * TOPK:(c + 1) * TOPK], wu[:, j % EB, c * FP:c * FP + n],
                                 xT[:, j % 2, :], start=True, stop=True)
            last.then_inc(up_t, 1)

        def down(e, j):
            pe.wait_ge(hid_a, e + 1)
            if not isinstance(e, int) or e >= 2:
                pe.wait_ge(y_v, e - 1)
            for half in range(HALVES):
                for c in range(FC):
                    last = pe.matmul(mixed[:, (j % 2) * 512 + half * C:(j % 2) * 512 + (half + 1) * C],
                                     hid[:, j % 2, c, half * P:(half + 1) * P], wd[:, j % EB, c, :],
                                     start=(c == 0), stop=(c == FC - 1))
            last.then_inc(down_t, 1)

        pe.wait_ge(ones_set, 2)
        turn(0, 0)
        up(0, 0)
        turn(1, 1)

        def group(first_e):
            for j in range(EB):
                up(first_e + j + 1, j + 1)
                down(first_e + j, j)
                turn(first_e + j + 2, j + 2)

        group(0)
        with pe.Fori(1, NG - 1) as g:
            group(g * GROUP)
        for j in range(EB):
            e = NE - GROUP + j
            if e + 1 < NE:
                up(e + 1, j + 1)
            down(e, j)
            if e + 2 < NE:
                turn(e + 2, j + 2)

    @block.vector
    def _(dve):
        dve.memset(cand[:], 1 << (BITS - 1)).then_inc(cand_ok, 1)
        dve.wait_ge(bits_in, 32)
        dve.wait_ge(prob_copied, 4)
        with dve.Fori(0, BITS) as k:
            dve.wait_ge(cand_ok, k + 1)
            dve.tensor_scalar(above[:], probT[:], cand[:].bitcast(F32), None, ALU.is_ge, ALU.add,
                              accum_out=count[:]).then_inc(counted, 1)
            dve.tensor_tensor(cand_next[:], cand[:], bits_i[:, bass.ds(k + 1, 1)], ALU.bitwise_or).then_inc(cand_c, 1)
            dve.wait_ge(totalled, k + 1)
            dve.scalar_tensor_tensor(out=drop[:], in0=turned[:, 0:1], scalar=float(TOPK), in1=bits_f[:, bass.ds(k, 1)],
                                     op0=ALU.is_lt, op1=ALU.mult).then_inc(drop_ok, 1)
            dve.wait_ge(drop_ok, k + 1)
            dve.wait_ge(cand_c, k + 1)
            dve.tensor_tensor(cand[:], cand_next[:], drop[:], ALU.bitwise_xor).then_inc(cand_ok, 1)
        dve.wait_ge(cand_ok, BITS + 1)
        dve.wait_ge(made_g, 1)
        dve.tensor_scalar(thr_row[:], thr_row[:], cand[0:NE, :].bitcast(F32), None, ALU.add).then_inc(thr_v, 1)
        dve.wait_ge(thr_t, 1)
        dve.tensor_copy(thr[:], turned[:, 512:512 + NE]).then_inc(thr_v, 1)
        dve.wait_ge(thr_v, 2)
        everywhere = thr[:].unsqueeze(1).to_broadcast([P, CT, NE])
        for mask, op in ((over, ALU.is_gt), (tie, ALU.is_equal)):
            for c in range(CHUNKS):
                last = dve.tensor_tensor(mask[:, c * CT:(c + 1) * CT, :], prob[:, c:TT:CHUNKS, :], everywhere, op)
            last.then_inc(masks, 1)
        dve.wait_ge(sums_t, 1)
        dve.tensor_reduce(n_over[:], turned[:, 0:512].rearrange("p (t e) -> p e t", e=NE), AX_X, ALU.add).then_inc(pick_v, 1)
        dve.wait_ge(sums_t, 2)
        for q in range(4):
            last = dve.tensor_copy(tie_tile[:, :, 1 + q * 16:17 + q * 16],
                                   scores[:, q * 512:(q + 1) * 512].rearrange("p (t e) -> p e t", e=NE))
        last.then_inc(pick_v, 1)
        dve.wait_ge(pick_v, 2)
        dve.tensor_scalar(room[:], n_over[:], -1.0, float(TOPK), ALU.mult, ALU.add)
        dve.tensor_tensor_scan(tie_before[:].rearrange("p e t -> p (e t)"), keep[:].rearrange("p e t -> p (e t)"),
                               tie_tile[:].rearrange("p e t -> p (e t)"), 0.0, ALU.mult, ALU.add).then_inc(pick_v, 1)
        dve.wait_ge(pick_v, 3)
        dve.wait_ge(sums_t, 3)
        for n, part in enumerate((turned, mixed)):
            last = dve.tensor_tensor(tie_rank[:, n * 32:(n + 1) * 32, :], part[:].rearrange("p (t e) -> p t e", e=NE),
                                     tie_before[:].rearrange("p e t -> p t e")[:, n * 32:(n + 1) * 32, :], ALU.add)
        last.then_inc(pick_v, 1)
        dve.wait_ge(pick_v, 4)
        dve.tensor_tensor(tie_in[:], tie_rank[:], room[:].unsqueeze(1).to_broadcast([P, TT, NE]),
                          ALU.is_le).then_inc(pick_v, 1)
        dve.wait_ge(pick_v, 5)
        dve.tensor_tensor(tie_in[:], tie_in[:], tie[:], ALU.mult).then_inc(pick_v, 1)
        dve.wait_ge(pick_v, 6)
        dve.tensor_tensor(chosen[:, 1:TT + 1, :], tie_in[:], over[:], ALU.add).then_inc(chosen_ok, 1)
        dve.wait_ge(before_t, 1)
        dve.tensor_copy(before[:], scores[0:TT, 0:NE]).then_inc(before_v, 1)
        dve.wait_ge(before_v, 1)
        for e in range(NE):
            dve.tensor_scalar(reached[:, e, :], slot_bf[0:TT, :], before[:, e:e + 1], None, ALU.is_gt).then_inc(reached_ok, 1)
        for n, (half, e0, m) in enumerate(row_banks):
            dve.wait_ge(row_t, n + 1)
            for i in range(m):
                k = (e0 + i) * HALVES + half
                dve.tensor_scalar(less[:, k, :], slot_bank(n)[:, i * RW:i * RW + P],
                                  K("slotcol")[:, half:half + 1], None, ALU.is_lt, ALU.add, accum_out=n_less[:, k:k + 1])
            at = slice(e0 * HALVES + half, (e0 + m - 1) * HALVES + half + 1, HALVES)
            dve.tensor_copy(tile_no[:, at], slot_bank(n)[:, 0:m * RW].rearrange("p (i r) -> p i r", r=RW)[:, :, P]
                            ).then_inc(row_v, 1)
        dve.wait_ge(row_v, len(row_banks))
        dve.tensor_scalar(slot_f[:], tile_no[:], float(P), -float(P), ALU.mult, ALU.add).then_inc(slots_v, 1)
        dve.wait_ge(slots_v, 1)
        dve.tensor_tensor(slots[:], slot_f[:], n_less[:], ALU.add).then_inc(slots_ok, 1)

        def copy_x(e, j):
            dve.wait_ge(xt_t, e + 1)
            if not isinstance(e, int) or e >= 2:
                dve.wait_ge(up_t, e - 1)
            dve.tensor_copy(xT[:, j % 2, :], scores[:, (j % 2) * 512:(j % 2) * 512 + TOPK]).then_inc(xt_v, 1)

        def weigh(e, j):
            dve.wait_ge(down_t, e + 1)
            if not isinstance(e, int) or e >= EB:
                dve.wait_ge(added, (e - (EB - 1)) * 32)
            for half in range(HALVES):
                last = dve.tensor_scalar(yw[:, j % EB, half, :],
                                         mixed[:, (j % 2) * 512 + half * C:(j % 2) * 512 + (half + 1) * C],
                                         xg[:, j % EB, half, bass.ds(C + e, 1)], None, ALU.mult)
            last.then_inc(y_v, 1)

        copy_x(0, 0)
        copy_x(1, 1)
        for j in range(EB):
            weigh(j, j)
            copy_x(j + 2, j + 2)
        with dve.Fori(1, NG - 1) as g:
            for j in range(EB):
                weigh(g * GROUP + j, j)
                copy_x(g * GROUP + j + 2, j + 2)
        for j in range(EB):
            e = NE - GROUP + j
            weigh(e, j)
            if e + 2 < NE:
                copy_x(e + 2, j + 2)

    @block.scalar
    def _(act):
        act.activation(upto_bf[:], K("upto"), ACT.Identity).then_inc(made, 1)
        act.activation(after_bf[:], K("after"), ACT.Identity).then_inc(made, 1)
        act.activation(below_bf[:], K("below"), ACT.Identity).then_inc(made, 1)
        act.activation(slot_bf[:], K("slot"), ACT.Identity).then_inc(made, 1)
        for q in range(4):
            act.wait_ge(prob_turned, q + 1)
            act.activation(probT[:, q * 512:(q + 1) * 512], scores[:, q * 512:(q + 1) * 512],
                           ACT.Identity).then_inc(prob_copied, 1)
        act.wait_ge(made_g, 1)
        for q in range(8):
            act.wait_ge(rank_t, q + 1)
            act.activation(ranks[:, 4 * q:4 * q + 4, 0:P], slot_bank(q)[0:TT, :].rearrange("p (e t) -> p e t", t=P),
                           ACT.Identity).then_inc(rank_a, 1)

        def silu(g, e, j):
            act.wait_ge(up_t, e + 1)
            if not isinstance(e, int) or e >= 2:
                act.wait_ge(down_t, e - 1)
            if not isinstance(e, int):
                act.nop(nofuse=True)
            src = scores[:, 1024:2048] if j % 2 == 0 else turned[:]
            for c in range(FC):
                n = FP if c < FC - 1 else FP - 1
                last = act.activation(hid[0:n, j % 2, c, :], src[0:n, c * TOPK:(c + 1) * TOPK], ACT.Silu,
                                      bias=bup[0:n, bass.ds(g * FC + c, 1)])
            last.then_inc(hid_a, 1)

        act.wait_ge(bup_in, 16)
        act.wait_ge(ones_set, 2)
        for j in range(EB):
            silu(0, j, j)
        with act.Fori(1, NG) as g:
            for j in range(EB):
                silu(g, g * GROUP + j, j)

    @block.gpsimd
    def _(pool):
        pool.memset(ones_bf[:], 1.0)
        pool.memset(thr_row[:], 0.0)
        pool.memset(tie_tile[:, :, 0:1], 0.0)
        pool.memset(keep[:, :, 1:TT + 1], 1.0)
        pool.memset(keep[:, :, 0:1], 0.0)
        pool.memset(chosen[:, 0:1, :], 0.0)
        pool.memset(ranks[:, :, P:P + 1], 1.0)
        pool.memset(ranks[:, :, P + 1:RW], 0.0).then_inc(made_g, 1)
        pool.wait_ge(made_g, 1)
        for j in range(2):
            pool.memset(hid[96:FP, j, FC - 1, :], 1.0).then_inc(ones_set, 1)

        def stage(to, e, j, done):
            pool.tensor_copy(to[:, j * HALVES:(j + 1) * HALVES], slots[:, bass.ds(e * HALVES, HALVES)]).then_inc(done, 1)
            pool.wait_ge(done, e + 1)
            pool.nop(nofuse=True)

        def gather(e, j):
            j = j % EB
            if not isinstance(e, int) or e >= EB:
                pool.wait_ge(y_v, e - (EB - 1))
                pool.nop(nofuse=True)
            stage(g_ids, e, j, g_staged)
            for half in range(HALVES):
                at = j * HALVES + half
                pool.indirect_dma_start(xg[:, j, half, :], None, table,
                                        bass.IndirectOffsetOnAxis(ap=g_ids[:, at:at + 1], axis=0)
                                        ).then_inc(x_in[j], 16)

        def scatter(e, j):
            if not isinstance(e, int) or e >= 1:
                pool.wait_ge(added, e * 32)
                pool.nop(nofuse=True)
            stage(s_ids, e, j, s_staged)
            pool.wait_ge(y_v, e + 1)
            pool.nop(nofuse=True)
            for half in range(HALVES):
                at = j * HALVES + half
                pool.indirect_dma_start(rows_out, bass.IndirectOffsetOnAxis(ap=s_ids[:, at:at + 1], axis=0),
                                        yw[:, j, half, :], None, compute_op=ALU.add).then_inc(added, 16)

        def group(first_e, ahead=EB):
            for j in range(EB):
                if j < ahead:
                    gather(first_e + j + 3, j + 3)
                scatter(first_e + j, j)

        pool.wait_ge(ones_set, 2)
        pool.wait_ge(slots_ok, 1)
        for j in range(3):
            gather(j, j)
        group(0)
        with pool.Fori(1, NG - 1) as g:
            group(g * GROUP)
        group(NE - GROUP, 1)
        pool.wait_ge(added, NE * 32)


def kernel(**inputs):
    import numpy as np
    import concourse.bacc as bacc
    from concourse.bass_utils import run_bass_kernel_spmd

    g = {k: np.ascontiguousarray(v) for k, v in inputs.items()}

    def a(name):
        return g["L0_attn_" + name]

    zero3 = np.zeros((C, VW - C), np.float32)
    parts = [a("dw").transpose(1, 2, 0).reshape(C, 3 * C), a("wq_cr").T, a("wk_cr").T, a("wq_d").T, a("wk_d").T,
             a("wq_c").T, a("wk_c").T]
    for br in ("cr", "d", "c"):
        parts += [a(f"wv_{br}").T, zero3]
    parts += [g["L0_tok_proj_w"].reshape(C, 3, C).transpose(2, 1, 0).reshape(C, 3 * C)]
    parts += [a(f"wv_{br}") for br in ("cr", "d", "c")]
    parts += [g["L0_ffn_W_router"]]
    weights = np.ascontiguousarray(np.concatenate(parts, axis=1))
    gw = a("gw").reshape(3, 3, C).transpose(2, 1, 0).reshape(C, 9)
    cols = np.ascontiguousarray(np.concatenate(
        [np.stack([a("db"), a("bq_cr"), a("bk_cr"), a("bq_d"), a("bk_d")] + [a(f"ln_{n}_g") for n in ("cr", "d", "c")]
                  + [a(f"ln_{n}_b") for n in ("cr", "d", "c")] + [a(f"bv_{n}") for n in ("cr", "d", "c")], axis=1), gw],
        axis=1))
    rows1 = np.concatenate([g["L0_tok_proj_b"], a("bq_c"), a("bk_c")] + [a(f"bv_{n}") for n in ("cr", "d", "c")]
                           + [a(f"ln_{n}_g") for n in ("cr", "d", "c")] + [a(f"ln_{n}_b") for n in ("cr", "d", "c")]
                           + [g["L0_ffn_b_router"], a("gb"), a("temp").reshape(1)])
    rows = np.ascontiguousarray(np.broadcast_to(rows1[None, :], (P, NROW)))
    i = np.arange(P)
    consts = np.ascontiguousarray(np.concatenate([
        np.eye(P), i[:, None] <= i[None, :], i[:, None] > i[None, :], i[:, None] < i[None, :],
        (i[:, None] % NE) == (i[None, :] % NE), np.broadcast_to(np.arange(1, TOPK + 1), (P, TOPK)),
        i[:, None] + 1 + P * np.arange(HALVES)[None, :]], axis=1).astype(np.float32))
    bits = np.concatenate([1 << np.arange(BITS - 1, -1, -1), [0]])
    bits_i = np.ascontiguousarray(np.broadcast_to(bits.astype(np.int32), (P, BITS + 1)))
    bits_f = np.ascontiguousarray(np.broadcast_to(bits.astype(np.float32), (P, BITS + 1)))
    w_down = np.ascontiguousarray(np.concatenate([g["L0_ffn_W_down"], g["L0_ffn_b_down"][:, None, :]], axis=1))
    b_up = np.ascontiguousarray(np.concatenate([g["L0_ffn_b_up"], np.zeros((NG, 1), np.float32)], axis=1)
                                .reshape(NG, FC, FP).transpose(2, 0, 1))
    arrays = dict(x_tok=g["x"], emb_2=g["L0_tok_emb_2"], emb_3=g["L0_tok_emb_3"], emb_4=g["L0_tok_emb_4"],
                  weights=weights, cols=cols, rows=rows, consts=consts, bits_i=bits_i, bits_f=bits_f, w_up=g["L0_ffn_W_up"], b_up=b_up, w_down=w_down)
    nc = bacc.Bacc("TRN2", target_bir_lowering=False, num_devices=1)
    ap = {n: nc.dram_tensor(f"in_{n}", v.shape, mybir.dt.from_np(v.dtype), kind="ExternalInput").ap()
          for n, v in arrays.items()}
    out = nc.dram_tensor("out_h", (B, S, C), F32, kind="ExternalOutput").ap()
    build_program(nc, ap["x_tok"], (ap["emb_2"], ap["emb_3"], ap["emb_4"]), ap["weights"], ap["cols"], ap["rows"],
                  ap["consts"], (ap["bits_i"], ap["bits_f"]), ap["w_up"], ap["b_up"], ap["w_down"], out)
    r = run_bass_kernel_spmd(nc, [{f"in_{n}": v for n, v in arrays.items()}], core_ids=[0])
    return r.results[0]["out_h"]
```

```python
from contextlib import ExitStack

import concourse.bass as bass
from concourse import mybir

ALU = mybir.AluOpType
ACT = mybir.ActivationFunctionType
AX_X = mybir.AxisListType.X
F32 = mybir.dt.float32
F32R = mybir.dt.float32r
BF16 = mybir.dt.bfloat16
I32 = mybir.dt.int32

B, S, C = 8, 1024, 128
P = 128
NT = S // P
TOK = B * S
TT = TOK // P
VOCAB = 25000
SD = S // 2
NE, GROUP = 32, 4
NG = NE // GROUP
DFF = 341
FC = 3
FP = (DFF + 1) // FC
TOPK = TOK // NE
HALVES = TOPK // P
LN_EPS = 1e-5
NORM_EPS = 1e-8
SCALE = 1.0 / float(C) ** 0.5
VW = 132
XW = C + NE
BR = 3
UNITS = NT * BR
CHUNKS = P // NE
SEQ_OF_CHUNK = B // CHUNKS
SPLIT = 1152
EARLY = 5
STEP = 7
BITS = 30

WCOL, _at = {}, 0
for _name, _width in (("conv", 3 * C), ("q_cr", C), ("k_cr", C), ("q_d", C), ("k_d", C), ("qk_c", 2 * C),
                      ("v_cr", VW), ("v_d", VW), ("v_c", VW)):
    WCOL[_name] = (_at, _at + _width)
    _at += _width
WSPLIT = _at
for _name, _width in (("proj", 3 * C), ("v_nat", 3 * C), ("router", NE)):
    WCOL[_name] = (_at, _at + _width)
    _at += _width
WALL = _at

COL = dict(db=0, bq_cr=1, bk_cr=2, bq_d=3, bk_d=4, ln_g=5, ln_b=8, bv=11, gw=14)
NCOL = 23
ROW, _at = {}, 0
for _name, _width in (("proj_b", C), ("bqk_c", 2 * C), ("bv", 3 * C), ("ln_g", 3 * C), ("ln_b", 3 * C),
                      ("b_router", NE), ("gb", 3), ("temp", 1)):
    ROW[_name] = (_at, _at + _width)
    _at += _width
NROW = _at
CON, _at = {}, 0
for _name, _width in (("ident", P), ("upto", P), ("after", P), ("below", P), ("same", P), ("slot", TOPK),
                      ("slotcol", HALVES), ("slotmid", HALVES)):
    CON[_name] = (_at, _at + _width)
    _at += _width
NCON = _at

USES = ([("xT", "av")] * 2 + [("qk_raw", "a")] * 4 + [("down", "av")]
        + [("q_d", "av")] * 2 + [("k_d", "av")] * 2 + [("q_cr", "av")] * 2 + [("k_cr", "av")]
        + [("v_cr", "av")] * 2 + [("v_dc", "av")] * 8 + [("q_c", "av")] * 2 + [("k_c", "av")] * 2)
NUSE = len(USES)


def first(name):
    return [n for n, _ in USES].index(name)


def reads(engine, k):
    return sum(engine in who for _, who in USES[:k + 1])


PARTS = NT * (2 * BR - 1)


def part(i, half=None):
    t, br = i // BR, i % BR
    return t * (2 * BR - 1) + max(2 * br - 1, 0) + ((1 if br else 0) if half is None else half) + 1


A_READS, V_READS = reads("a", NUSE - 1), reads("v", NUSE - 1)


def build_program(nc, x_tok, emb, weights, cols, rows, consts, cand_bits, w_up, b_up, w_down, out):
    table = nc.dram_tensor("token_table", (TOK, XW), F32, kind="Internal").ap()
    with ExitStack() as ctx:
        def sb(name, shape, dt=F32):
            return ctx.enter_context(nc.sbuf_tensor(name, shape, dt))

        def sem(name):
            return ctx.enter_context(nc.semaphore(name))

        attn = ExitStack()

        def asb(name, shape, dt=F32):
            return attn.enter_context(nc.sbuf_tensor(name, shape, dt))

        scores = ctx.enter_context(nc.psum_tensor("scores", [P, 4 * 512], F32))
        turned = ctx.enter_context(nc.psum_tensor("turned", [P, 2 * 512], F32))
        mixed = ctx.enter_context(nc.psum_tensor("mixed", [P, 2 * 512], F32))

        con = sb("con", [P, NCON])
        prob = sb("prob", [P, TT, NE])
        ones_row = sb("ones_row", [1, P])

        w = asb("w", [P, WALL])
        w_hi = asb("w_hi", [P, WSPLIT], F32R)
        w_lo = asb("w_lo", [P, WSPLIT], F32R)
        col = asb("col", [P, NCOL])
        row = asb("row", [P, NROW])
        gate_w = asb("gate_w", [P, 9])
        gate_mean = asb("gate_mean", [P, 9])
        wide = asb("wide", [P, 6, C])
        v_mean = asb("v_mean", [P, 2 * BR])
        mean_w = asb("mean_w", [P, P])
        bv_hi = asb("bv_hi", [1, 3 * VW + 2 * C], F32R)
        bv_lo = asb("bv_lo", [1, 3 * VW + 2 * C], F32R)
        one_row = asb("one_row", [1, P], F32R)
        inv_temp = asb("inv_temp", [P, 1])
        m_half = asb("m_half", [P, 16])
        p_half = asb("p_half", [P, 16])

        xw = asb("xw", [TT, P + 3])
        xwi = asb("xwi", [TT, P + 3], I32)
        hashed = asb("hashed", [TT, 3, P + 1])
        quot = asb("quot", [TT, 3, P + 1])
        quot_i = asb("quot_i", [TT, 3, P + 1], I32)
        ids = asb("ids", [P, B, NT, 3], I32)
        ids_now = asb("ids_now", [P, NT * 3], I32)

        gram = asb("gram", [P, 4, 3, C])
        gramT = asb("gramT", [P, 4, 3, P])
        h = asb("h", [P, 2 * NT, C])
        st1 = asb("st1", [P, NT, 6])
        mv1 = asb("mv1", [P, NT, 2])
        rstd1 = asb("rstd1", [P, NT])
        xn = asb("xn", [P, NT, C])
        xT_hi = asb("xT_hi", [P, S + 2], F32R)
        xT_lo = asb("xT_lo", [P, S + 2], F32R)
        square = xn[:].bitcast(BF16)
        norm = asb("norm", [P, NT * 2])
        inv_norm = asb("inv_norm", [P, NT * 2])
        down_hi = asb("down_hi", [P, SD], F32R)
        down_lo = asb("down_lo", [P, SD], F32R)
        q_hi = [asb(f"q_hi{i}", [P, S], F32R) for i in range(BR)]
        q_lo = [asb(f"q_lo{i}", [P, S], F32R) for i in range(BR)]
        k_hi = [asb(f"k_hi{i}", [P, S if i else SD], F32R) for i in range(BR)]
        k_lo = [asb(f"k_lo{i}", [P, S if i else SD], F32R) for i in range(BR)]
        v0 = asb("v0", [P, SD // P, 2, VW], F32R)
        v12 = asb("v12", [P, NT, 2, 2, VW], F32R)

        neg_max = asb("neg_max", [P, 4])
        exp_sum = asb("exp_sum", [P, 4, BR])
        probs = asb("probs", [P, 2, S])
        qk_raw = probs[:].rearrange("p a (t c) -> p (a t) c", c=2 * C)
        bv_ext = probs[:].rearrange("p a n -> p (a n)")[:, 0:3 * VW + 2 * C]
        pT_hi = asb("pT_hi", [P, 2, S], F32R)
        pT_lo = asb("pT_lo", [P, 2, S], F32R)

        st = asb("st", [P, 2, BR, 6])
        mv = asb("mv", [P, 2, BR, 2])
        o = asb("o", [P, 4, BR, VW])
        sum_sq = asb("sum_sq", [P, 2, BR])
        var_eps = asb("var_eps", [P, 2, BR])
        rstd = asb("rstd", [P, 2, BR])
        logit9 = asb("logit9", [P, 2, 3, BR + 1])
        logit = asb("logit", [P, 2, 3])
        logit_nm = asb("logit_nm", [P, 2])
        gate_e = asb("gate_e", [P, 2, 3])
        gate_sum = asb("gate_sum", [P, 2])
        gate_inv = asb("gate_inv", [P, 2])
        gate = asb("gate", [P, 2, 3])
        gate_r = asb("gate_r", [P, 2, 3])
        u = asb("u", [P, 2, BR, C])
        zb = asb("zb", [P, 2, BR, C])
        st2_last = asb("st2_last", [P, 2, 6])
        mv2_last = asb("mv2_last", [P, 2, 2])
        rstd2_last = asb("rstd2_last", [P, 2])
        h1 = asb("h1", [P, NT, C])
        st2 = asb("st2", [P, 2, 6])
        mv2 = asb("mv2", [P, 2, 2])
        ve2 = asb("ve2", [P, 2])
        rstd2 = asb("rstd2", [P, 2])
        trow = asb("trow", [P, NT, XW])
        x2T = w[:, 0:S]
        r_log, r_sub, r_exp = (wide[:, 2 * i:2 * i + 2, :].rearrange("p a (t e) -> p (a t) e", e=NE) for i in range(3))
        r_nm = asb("r_nm", [P, NT])
        r_sum = asb("r_sum", [P, NT])
        r_inv = asb("r_inv", [P, NT])

        loaded = sem("loaded")
        tok_loaded = sem("tok_loaded")
        setup_v = sem("setup_v")
        setup_t = sem("setup_t")
        setup_g = sem("setup_g")
        ids_ready = sem("ids_ready")
        hash_step = sem("hash_step")
        ids_turned = sem("ids_turned")
        weights_ready = sem("weights_ready")
        staged = sem("staged")
        gathered = [sem(f"gathered{j}") for j in range(4)]
        bank_full = sem("bank_full")
        bank_a = sem("bank_a")
        bank_v = sem("bank_v")
        gram_turned = sem("gram_turned")
        gram_copied = sem("gram_copied")
        token_done = sem("token_done")
        h_added = sem("h_added")
        ln1_stats = sem("ln1_stats")
        ln1_mv = sem("ln1_mv")
        ln1_g = sem("ln1_g")
        ln1_rstd = sem("ln1_rstd")
        x_ready = sem("x_ready")
        sq_ready = sem("sq_ready")
        norm_g = sem("norm_g")
        norm_v = sem("norm_v")
        qk_ready = sem("qk_ready")
        scored = sem("scored")
        maxed = sem("maxed")
        exped = sem("exped")
        turn_done = sem("turn_done")
        hi_done = sem("hi_done")
        lo_done = sem("lo_done")
        pv_done = sem("pv_done")
        o_ok = sem("o_ok")
        o_stats = sem("o_stats")
        o_mv = sem("o_mv")
        rstd_g = sem("rstd_g")
        rstd_ok = sem("rstd_ok")
        logit_c = sem("logit_c")
        logit_ok = sem("logit_ok")
        gate_ok = sem("gate_ok")
        gate_c = sem("gate_c")
        gate_r_ok = sem("gate_r_ok")
        scale_ok = sem("scale_ok")
        u_ok = sem("u_ok")
        z_g = sem("z_g")
        h1_ok = sem("h1_ok")
        st2_ok = sem("st2_ok")
        mv2_ok = sem("mv2_ok")
        last_g = sem("last_g")
        last_v = sem("last_v")
        ve2_ok = sem("ve2_ok")
        rstd2_ok = sem("rstd2_ok")
        x2_ok = sem("x2_ok")
        x2_turned = sem("x2_turned")
        x2T_ok = sem("x2T_ok")
        routed = sem("routed")
        route_v = sem("route_v")
        route_e = sem("route_e")
        prob_ok = sem("prob_ok")
        prob_kept = sem("prob_kept")
        h1_stored = sem("h1_stored")
        row_stored = sem("row_stored")
        h1_free = sem("h1_free")
        rows_free = sem("rows_free")

        def W(name, a=0, n=None):
            lo, hi = WCOL[name]
            return w[:, lo + a:(lo + a + n if n else hi)]

        def split(name, a=0, n=None):
            lo, hi = WCOL[name]
            hi = lo + a + n if n else hi
            return w_hi[:, lo + a:hi], w_lo[:, lo + a:hi]

        def R(name):
            return row[:, ROW[name][0]:ROW[name][1]]

        def K(name):
            return con[:, CON[name][0]:CON[name][1]]

        ident = K("ident")

        def gramT_of(t):
            return gramT[:, 0 if t == 0 else 3 if t == NT - 1 else 1 + t % 2]

        def spare(t):
            return scores[:, (t % 2) * S + 512:(t % 2) * S + S]

        def first_psum(t):
            return mixed[:, t % 2 * 512:t % 2 * 512 + C]

        def token_psum(t):
            return scores[:, 0:C] if t == NT - 1 else spare(t + 1)[:, 3 * P:3 * P + C]

        def bank(k):
            return scores[:, (k % 4) * 512:(k % 4 + 1) * 512]

        def mixed_of(i):
            return mixed[:, (i % 2) * 512:(i % 2) * 512 + 2 * VW]

        tokens_out = out.rearrange("b (t p) c -> p (b t) c", p=P)
        table_out = table.rearrange("(t p) x -> p t x", p=P)

        first_part = nc.Block()
        block = first_part.__enter__()


        def prob_rows(b):
            if isinstance(b, int):
                return prob[:].rearrange("p (u c) e -> p c u e", c=CHUNKS)[
                    :, b // SEQ_OF_CHUNK, (b % SEQ_OF_CHUNK) * NT:(b % SEQ_OF_CHUNK) * NT + NT, :]
            return prob[:].rearrange("p (u c) e -> p c u e", c=CHUNKS)[
                :, bass.ds(b // SEQ_OF_CHUNK, 1), bass.ds((b % SEQ_OF_CHUNK) * NT, NT), :]

        @block.sync
        def _(sp):
            xf = x_tok.rearrange("b (t p) -> (b t) p", p=P)
            sp.wait_ge(setup_g, 1)
            sp.dma_start(xwi[:, 2:P + 2], xf).then_inc(tok_loaded, 16)
            sp.dma_start(xwi[1:TT, 0:2], xf[0:TT - 1, P - 2:P]).then_inc(tok_loaded, 16)
            sp.dma_start(xwi[0:TT - 1, P + 2:P + 3], xf[1:TT, 0:1], allow_slow_non_contiguous=True).then_inc(tok_loaded, 16)
            sp.dma_start(con[:], consts).then_inc(loaded, 16)
            sp.dma_start(row[:], rows).then_inc(loaded, 16)
            sp.dma_start(col[:], cols).then_inc(loaded, 16)
            sp.dma_start(w[:], weights).then_inc(loaded, 16)

            sp.nop().then_inc(h1_free, 1)
            sp.nop().then_inc(rows_free, 1)
            with sp.Fori(0, B) as b:
                sp.wait_ge(h1_ok, b * NT + NT)
                sp.dma_start(tokens_out[:, bass.ds(b * NT, NT), :], h1[:]).then_inc(h1_stored, 16)
                sp.wait_ge(prob_ok, b + 1)
                sp.dma_start(table_out[:, bass.ds(b * NT, NT), :], trow[:]).then_inc(row_stored, 16)
                sp.wait_ge(h1_stored, 16 * b + 16)
                sp.nop().then_inc(h1_free, 1)
                sp.wait_ge(row_stored, 16 * b + 16)
                sp.nop().then_inc(rows_free, 1)

        @block.tensor
        def _(pe):
            def product(dst, lhs, rhs, first_one=True, last_one=True):
                pe.matmul(dst, lhs[0], rhs[0], start=first_one, stop=False)
                pe.matmul(dst, lhs[0], rhs[1], start=False, stop=False)
                return pe.matmul(dst, lhs[1], rhs[0], start=False, stop=last_one)

            def bias(dst, at, n):
                pe.matmul(dst, one_row[:], bv_hi[:, at:at + n], start=True, stop=False)
                pe.matmul(dst, one_row[:], bv_lo[:, at:at + n], start=False, stop=False)

            def setup():
                pe.wait_ge(loaded, 64)
                pe.wait_ge(ids_ready, 1)
                for g in range(3):
                    last = pe.transpose(turned[:, g * TT:(g + 1) * TT],
                                        hashed[:, g, (1 if g < 2 else 0):(1 if g < 2 else 0) + P], ident[0:TT, 0:TT])
                last.then_inc(ids_turned, 1)
                pe.wait_ge(setup_g, 8)
                pe.wait_ge(setup_v, 3)
                pe.matmul(bank(0)[:, 0:9], mean_w[:], gate_w[:], start=True, stop=True).then_inc(setup_t, 1)
                pe.wait_ge(setup_v, 7)
                for i in range(BR):
                    pe.matmul(bank(1)[:, 3 * i:3 * i + 3], W("v_nat", i * C, C), gate_w[:, 3 * i:3 * i + 3],
                              start=True, stop=True)
                for i in range(BR):
                    pe.matmul(bank(2)[:, 3 * i:3 * i + 3], wide[:, i, :], gate_w[:, 3 * i:3 * i + 3],
                              start=True, stop=True)
                for i in range(BR):
                    last = pe.matmul(bank(3)[:, 0:3], wide[:, 3 + i, :], col[:, COL["gw"] + 3 * i:COL["gw"] + 3 * i + 3],
                                     start=(i == 0), stop=(i == BR - 1))
                last.then_inc(setup_t, 1)
                pe.wait_ge(weights_ready, 2)

            def open_bank(b, k, high_of=-1, low_of=-1):
                if k < 4 and (not isinstance(b, int) or b > 0):
                    pe.wait_ge(exped, b * UNITS)
                who = USES[k - 4][1] if k >= 4 else ""
                a_count = max(reads("a", k - 4) if "a" in who else 0, reads("a", high_of) if high_of >= 0 else 0)
                v_count = max(reads("v", k - 4) if "v" in who else 0, reads("v", low_of) if low_of >= 0 else 0)
                if a_count:
                    pe.wait_ge(bank_a, b * A_READS + a_count)
                if v_count:
                    pe.wait_ge(bank_v, b * V_READS + v_count)

            def turn_gram(s, t):
                pe.wait_ge(gathered[t % 4], (s * (NT // 4) + t // 4 + 1) * (3 * 16))
                for g in range(3):
                    last = pe.transpose(spare(t)[:, g * P:(g + 1) * P], gram[:, t % 4, g, :], ident)
                last.then_inc(gram_turned, 1)

            def token(s, t, dst):
                pe.wait_ge(gram_copied, s * NT + t + 1)
                for g in range(3):
                    last = pe.matmul(dst, gramT_of(t)[:, g, :], W("proj", g * C, C), start=(g == 0), stop=(g == 2))
                last.then_inc(token_done, 1)

            def turn_tokens(b):
                pe.wait_ge(h_added, b * NT + NT)
                for half in range(2):
                    k = first("xT") + half
                    open_bank(b, k)
                    pe.wait_ge(x_ready, b * NT + half * 4 + 4)
                    for j in range(4):
                        last = pe.transpose(bank(k)[:, j * P:(j + 1) * P], xn[:, half * 4 + j, :], ident)
                    last.then_inc(bank_full, 1)

            def keep_clock(b, n):
                pe.wait_ge(exped, b * UNITS)
                for _ in range(n):
                    pe.matmul(bank(first("qk_raw")), w_hi[:, 0:P], w_hi[:, 0:512], start=True, stop=True)

            def prologue(b, tail):
                if tail is None:
                    turn_tokens(b)
                else:
                    keep_clock(b, 8)

                def xT_tile(t):
                    return xT_hi[:, 2 + t * P:2 + (t + 1) * P], xT_lo[:, 2 + t * P:2 + (t + 1) * P]

                def xT_half(half):
                    return xT_hi[:, 2 + half * 512:514 + half * 512], xT_lo[:, 2 + half * 512:514 + half * 512]

                for i in range(4):
                    k = first("qk_raw") + i
                    open_bank(b, k, first("xT") + i // 2, first("xT") + i // 2)
                    for j in range(2):
                        dst = bank(k)[:, j * 2 * C:(j + 1) * 2 * C]
                        bias(dst, 3 * VW, 2 * C)
                        last = product(dst, xT_tile(2 * i + j), split("qk_c"), False)
                    last.then_inc(bank_full, 1)
                k = first("down")
                open_bank(b, k)
                for tap in range(3):
                    last = product(bank(k), split("conv", tap * C, C),
                                   (xT_hi[:, tap + 1:tap + 1 + S - 1:2], xT_lo[:, tap + 1:tap + 1 + S - 1:2]),
                                   tap == 0, tap == 2)
                last.then_inc(bank_full, 1)
                for name in ("q_d", "k_d", "q_cr"):
                    for half in range(2):
                        k = first(name) + half
                        open_bank(b, k)
                        product(bank(k), split(name), xT_half(half)).then_inc(bank_full, 1)
                k = first("k_cr")
                open_bank(b, k, first("down"), first("down"))
                product(bank(k), split("k_cr"), (down_hi[:], down_lo[:])).then_inc(bank_full, 1)
                for i in range(2):
                    k = first("v_cr") + i
                    open_bank(b, k)
                    for j in range(2):
                        t = 2 * i + j
                        dst = bank(k)[:, j * VW:(j + 1) * VW]
                        bias(dst, 0, VW)
                        last = product(dst, (down_hi[:, t * P:(t + 1) * P], down_lo[:, t * P:(t + 1) * P]),
                                       split("v_cr"), False)
                    last.then_inc(bank_full, 1)
                for t in range(NT):
                    k = first("v_dc") + t
                    open_bank(b, k)
                    dst = bank(k)[:, 0:2 * VW]
                    bias(dst, VW, 2 * VW)
                    w0, w1 = WCOL["v_d"][0], WCOL["v_c"][1]
                    product(dst, xT_tile(t), (w_hi[:, w0:w1], w_lo[:, w0:w1]), False).then_inc(bank_full, 1)
                for which, name in enumerate(("q_c", "k_c")):
                    for half in range(2):
                        k = first(name) + half
                        open_bank(b, k)
                        pe.wait_ge(qk_ready, b * 2 + half + 1)
                        for j in range(4):
                            last = pe.transpose(bank(k)[:, j * P:(j + 1) * P],
                                                qk_raw[:, half * 4 + j, which * C:(which + 1) * C], ident)
                        last.then_inc(bank_full, 1)
            def route_turn(tiles=range(NT)):
                for t in tiles:
                    last = pe.transpose(turned[:, t * P:(t + 1) * P], trow[:, t, 0:C], ident)
                last.then_inc(x2_turned, 1)

            def route_product(b, tiles=range(NT)):
                pe.wait_ge(x2T_ok, b + 1)
                for t in tiles:
                    last = pe.matmul(mixed[:, 512 + t * NE:512 + (t + 1) * NE], x2T[:, t * P:(t + 1) * P], W("router"),
                                     start=True, stop=True)
                last.then_inc(routed, 1)

            def attention(b, more, tail):
                def turn(i):
                    pe.wait_ge(exped, b * UNITS + i + 1)
                    if i == 0 and tail is not None:
                        pe.wait_ge(x2T_ok, tail + 1)
                    for half in range(1 if i % BR == 0 else 2):
                        before = i - 1 if half == 0 or i % BR == 2 else i - 2
                        if before >= 0:
                            pe.wait_ge(lo_done, b * PARTS + part(before, half))
                        for j in range(half * 4, half * 4 + 4):
                            last = pe.transpose(turned[:, j * P:(j + 1) * P], probs[:, i % 2, j * P:(j + 1) * P], ident)
                        last.then_inc(turn_done, 1)

                def score(i):
                    t, br = i // BR, i % BR
                    if more and br == 2:
                        pe.wait_ge(gram_copied, b * NT + NT + t + 1)
                        if t > 0:
                            pe.wait_ge(h_added, b * NT + NT + t)
                    if i >= 2:
                        pe.wait_ge(exped, b * UNITS + i - 1)
                    elif i == 1:
                        pe.wait_ge(bank_a, b * A_READS + A_READS)
                        pe.wait_ge(bank_v, b * V_READS + V_READS)
                    else:
                        pe.wait_ge(bank_a, b * A_READS + A_READS - 3)
                        pe.wait_ge(bank_v, b * V_READS + V_READS - 3)
                    lhs = q_hi[br][:, t * P:(t + 1) * P], q_lo[br][:, t * P:(t + 1) * P]
                    for half in range(1 if br == 0 else 2):
                        at = (i % 2) * S + half * 512
                        last = product(scores[:, at:at + 512], lhs, (k_hi[br][:, half * 512:(half + 1) * 512],
                                                                     k_lo[br][:, half * 512:(half + 1) * 512]))
                    last.then_inc(scored, 1)

                def mix(i):
                    t, br = i // BR, i % BR
                    pe.wait_ge(hi_done, b * PARTS + part(i))
                    pe.wait_ge(lo_done, b * PARTS + part(i))
                    if i >= 2:
                        pe.wait_ge(o_ok, b * UNITS + i - 1)
                    elif i == 0 and tail is not None:
                        pe.wait_ge(o_ok, b * UNITS)
                    elif tail is not None:
                        pe.wait_ge(route_v, tail * 5 + 1)
                    n = (SD if br == 0 else S) // P
                    for j in range(n):
                        vals = (v0[:, j, :, :] if br == 0 else v12[:, j, br - 1, :, :]).rearrange("p h c -> p (h c)")
                        parts = [(mixed_of(i), pT_hi, vals), (mixed_of(i)[:, 0:VW], pT_lo, vals[:, 0:VW])]
                        for dst, probabilities, v in (parts[::-1] if j == n - 1 else parts):
                            last = pe.matmul(dst, probabilities[:, i % 2, j * P:(j + 1) * P], v,
                                             start=(j == 0 and v is vals), stop=(j == n - 1 and v is vals))
                    last.then_inc(pv_done, 1)

                for i in range(UNITS + 3):
                    if 0 <= i - 2 < UNITS:
                        turn(i - 2)
                    if i < UNITS:
                        score(i)
                    if i == 1 and tail is not None:
                        pe.wait_ge(x2_ok, tail * NT + NT)
                        pe.wait_ge(lo_done, (tail + 1) * PARTS)
                        route_turn()
                    if i == 2 and tail is not None:
                        pe.wait_ge(o_ok, b * UNITS)
                        route_product(tail)
                    if more:
                        if i == 1:
                            turn_gram(b + 1, 0)
                        elif i % BR == 0 and 0 < i < UNITS:
                            token(b + 1, i // BR - 1, token_psum(i // BR - 1))
                            turn_gram(b + 1, i // BR)
                        elif i == UNITS:
                            token(b + 1, NT - 1, token_psum(NT - 1))
                    if more and i == UNITS + 2:
                        turn_tokens(b + 1)
                        keep_clock(b + 1, 4)
                    if 0 <= i - 3 < UNITS:
                        mix(i - 3)

            setup()
            for t in range(NT + 1):
                if t < NT:
                    if t >= 2:
                        pe.wait_ge(gram_copied, t - 1)
                    turn_gram(0, t)
                if t > 0:
                    if t >= 3:
                        pe.wait_ge(h_added, t - 2)
                    token(0, t - 1, first_psum(t - 1))
            prologue(0, None)
            attention(0, True, None)
            prologue(1, 0)
            with pe.Fori(1, B - 1) as b:
                attention(b, True, b - 1)
                prologue(b + 1, b)
            attention(B - 1, False, B - 2)
            pe.wait_ge(x2_ok, TT - (NT - EARLY))
            pe.wait_ge(lo_done, B * PARTS)
            route_turn(range(EARLY))
            pe.wait_ge(o_ok, B * UNITS)
            route_product(B - 1, range(EARLY))
            pe.wait_ge(x2_ok, TT)
            route_turn(range(EARLY, NT))
            route_product(B, range(EARLY, NT))

        @block.vector
        def _(dve):
            def setup():
                n = [0]

                def step(ins):
                    n[0] += 1
                    ins.then_inc(setup_v, 1)

                dve.wait_ge(loaded, 64)
                for i in range(BR):
                    step(dve.tensor_scalar(gate_w[:, 3 * i:3 * i + 3], col[:, COL["gw"] + 3 * i:COL["gw"] + 3 * i + 3],
                                           col[:, COL["ln_g"] + i:COL["ln_g"] + i + 1], None, ALU.mult))
                dve.wait_ge(setup_t, 1)
                step(dve.tensor_copy(gate_mean[:], bank(0)[:, 0:9]))
                dve.wait_ge(setup_v, 4)
                step(dve.tensor_tensor(gate_w[:], gate_w[:], gate_mean[:], ALU.subtract))
                dve.wait_ge(setup_g, 8)
                for i in range(BR):
                    dve.tensor_scalar(wide[:, i, :], wide[:, i, :], col[:, COL["bv"] + i:COL["bv"] + i + 1], None, ALU.add)
                    last = dve.tensor_scalar(wide[:, 3 + i, :], wide[:, 3 + i, :],
                                             col[:, COL["ln_b"] + i:COL["ln_b"] + i + 1], None, ALU.add)
                step(last)
                step(dve.tensor_scalar(inv_temp[:], R("temp"), 0.01, None, ALU.max))
                for name in ("q_cr", "q_d"):
                    dve.tensor_scalar(W(name), W(name), SCALE, None, ALU.mult)
                    last = dve.tensor_scalar(col[:, COL["b" + name]:COL["b" + name] + 1],
                                             col[:, COL["b" + name]:COL["b" + name] + 1], SCALE, None, ALU.mult)
                step(last)
                dve.wait_ge(setup_v, 8)
                step(dve.reciprocal(inv_temp[:], inv_temp[:]))
                for i in range(BR):
                    dve.memset(bv_ext[:, i * VW + C + 3:(i + 1) * VW], 0.0)
                dve.tensor_copy(bv_ext[:, 3 * VW:3 * VW + 2 * C], R("bqk_c"))
                for i, name in enumerate(("v_cr", "v_d", "v_c")):
                    dve.tensor_reduce(v_mean[:, i:i + 1], W(name, 0, C), AX_X, ALU.add, negate=True)
                    last = dve.tensor_reduce(v_mean[:, BR + i:BR + i + 1], R("bv")[:, i * C:(i + 1) * C], AX_X, ALU.add,
                                             negate=True)
                step(last)
                dve.wait_ge(setup_v, 10)
                step(dve.tensor_scalar(v_mean[:], v_mean[:], 1.0 / C, None, ALU.mult))
                dve.wait_ge(setup_v, 11)
                for i, name in enumerate(("v_cr", "v_d", "v_c")):
                    dve.tensor_scalar(W(name, 0, C), W(name, 0, C), v_mean[:, i:i + 1], None, ALU.add)
                    dve.tensor_scalar(bv_ext[:, i * VW:i * VW + C], R("bv")[:, i * C:(i + 1) * C],
                                      v_mean[:, BR + i:BR + i + 1], None, ALU.add)
                dve.wait_ge(setup_t, 2)
                for i, name in enumerate(("v_cr", "v_d", "v_c")):
                    dve.tensor_copy(W(name, C, 3), bank(1)[:, 3 * i:3 * i + 3])
                    last = dve.tensor_copy(bv_ext[:, i * VW + C:i * VW + C + 3], bank(2)[:, 3 * i:3 * i + 3])
                step(last)
                for m in range(2):
                    last = dve.tensor_tensor(logit9[:, m, :, BR:BR + 1], bank(3)[:, 0:3].unsqueeze(2), R("gb").unsqueeze(2), ALU.add)
                step(last)
                dve.wait_ge(setup_v, 13)
                dve.tensor_copy(w_hi[:], w[:, 0:WSPLIT])
                step(dve.tensor_copy(bv_hi[:], bv_ext[0:1, :]))
                dve.wait_ge(setup_v, 14)
                dve.tensor_tensor(w_lo[:], w[:, 0:WSPLIT], w_hi[:].bitcast(F32), ALU.subtract)
                dve.tensor_tensor(bv_lo[:], bv_ext[0:1, :], bv_hi[:].bitcast(F32), ALU.subtract).then_inc(weights_ready, 1)
                dve.wait_ge(setup_g, 8)
                dve.tensor_copy(one_row[:], ones_row[:]).then_inc(weights_ready, 1)

            def hashes():
                n = [0]

                def step(ins):
                    n[0] += 1
                    ins.then_inc(hash_step, 1)
                    dve.wait_ge(hash_step, n[0])

                dve.wait_ge(tok_loaded, 48)
                step(dve.tensor_copy(xw[:], xwi[:]))

                def modulo(v, quot, quot_i):
                    step(dve.tensor_scalar(quot, v, 1.0 / VOCAB, None, ALU.mult))
                    step(dve.tensor_copy(quot_i, quot))
                    step(dve.tensor_copy(quot, quot_i))
                    step(dve.scalar_tensor_tensor(out=v, in0=quot, scalar=-float(VOCAB), in1=v,
                                                  op0=ALU.mult, op1=ALU.add))
                    step(dve.tensor_scalar(quot, v, 0.0, float(VOCAB), ALU.is_lt, ALU.mult))
                    step(dve.tensor_tensor(v, v, quot, ALU.add))
                    step(dve.tensor_scalar(quot, v, float(VOCAB), -float(VOCAB), ALU.is_ge, ALU.mult))
                    step(dve.tensor_tensor(v, v, quot, ALU.add))

                def longer(g, n):
                    step(dve.scalar_tensor_tensor(out=hashed[:, g, 0:n], in0=(hashed[:, g - 1, 0:n] if g else xw[:, 0:n]),
                                                  scalar=64.0, in1=xw[:, g + 1:g + 1 + n], op0=ALU.mult, op1=ALU.add))

                longer(0, P + 1)
                longer(1, P + 1)
                modulo(hashed[:, 0:2, :], quot[:, 0:2, :], quot_i[:, 0:2, :])
                longer(2, P)
                modulo(hashed[:, 2, 0:P], quot[:, 2, 0:P], quot_i[:, 2, 0:P])
                dve.engine_nop().then_inc(ids_ready, 1)
                dve.wait_ge(ids_turned, 1)
                for g in range(3):
                    last = dve.tensor_copy(ids[:].rearrange("p b t g -> p (b t) g")[:, :, g],
                                           turned[:, g * TT:(g + 1) * TT])
                last.then_inc(ids_ready, 1)

            def low(b, k, dst, src, hi):
                dve.wait_ge(bank_full, b * NUSE + k + 1)
                dve.wait_ge(bank_a, b * A_READS + reads("a", k))
                dve.tensor_tensor(dst, src, hi.bitcast(F32), ALU.subtract).then_inc(bank_v, 1)

            def low_bias(b, k, dst, src, bias, hi):
                dve.wait_ge(bank_full, b * NUSE + k + 1)
                dve.wait_ge(bank_a, b * A_READS + reads("a", k))
                dve.scalar_tensor_tensor(out=dst, in0=src, scalar=bias, in1=hi.bitcast(F32), op0=ALU.add,
                                         op1=ALU.subtract).then_inc(bank_v, 1)

            def token_add(s, t, src):
                dve.wait_ge(token_done, s * NT + t + 1)
                if src is not first_psum and t < NT - 1:
                    dve.wait_ge(gram_copied, s * NT + t + 2)
                dve.tensor_tensor(h[:, bass.ds((s % 2) * NT + t, 1), :], src(t).unsqueeze(1),
                                  R("proj_b").unsqueeze(1), ALU.add).then_inc(h_added, 1)

            def token_stats(s, t):
                dve.wait_ge(h_added, s * NT + t + 1)
                dve.nop(nofuse=True)
                dve.bn_stats(st1[:, t, :], h[:, bass.ds((s % 2) * NT + t, 1), :]).then_inc(ln1_stats, 1)
                dve.wait_ge(ln1_stats, s * NT + t + 1)
                dve.nop(nofuse=True)
                dve.bn_aggr(mv1[:, t, :], st1[:, t, :]).then_inc(ln1_mv, 1)

            def tokens_low(b):
                for half in range(2):
                    k = first("xT") + half
                    at = slice(2 + half * 512, 514 + half * 512)
                    low(b, k, xT_lo[:, at], bank(k), xT_hi[:, at])

            def normalise(s, half):
                dve.wait_ge(ln1_rstd, s * 2 + half + 1)
                for t in range(half * 4, half * 4 + 4):
                    dve.tensor_scalar(xn[:, t, :], h[:, bass.ds((s % 2) * NT + t, 1), :], mv1[:, t, 0:1], rstd1[:, t:t + 1],
                                      ALU.subtract, ALU.mult).then_inc(x_ready, 1)

            def prologue(b, tail):
                if tail is None:
                    tokens_low(b)
                for i in range(4):
                    if tail is not None and i == 1:
                        tile_gate_logits(tail, NT - 1)
                    if tail is not None and i == 1:
                        tile_gate(tail, NT - 2)
                    if tail is not None and i == 2:
                        tile_gate(tail, NT - 1)
                    if tail is not None and i == 3:
                        tile_h1_stats(tail, NT - 3)
                low_bias(b, first("down"), down_lo[:], bank(first("down")), col[:, COL["db"]:COL["db"] + 1], down_hi[:])
                for br, which, name in ((1, q_lo, "q_d"), (1, k_lo, "k_d"), (0, q_lo, "q_cr")):
                    for half in range(2):
                        k = first(name) + half
                        at = slice(half * 512, half * 512 + 512)
                        hi = (q_hi if which is q_lo else k_hi)[br][:, at]
                        low_bias(b, k, which[br][:, at], bank(k), col[:, COL["b" + name]:COL["b" + name] + 1], hi)
                    if tail is not None and name == "q_cr":
                        tile_h1_stats(tail, NT - 2)
                low_bias(b, first("k_cr"), k_lo[0][:], bank(first("k_cr")), col[:, COL["bk_cr"]:COL["bk_cr"] + 1],
                         k_hi[0][:])
                for i in range(2):
                    k = first("v_cr") + i
                    low(b, k, v0[:, 2 * i:2 * i + 2, 1, :], bank(k)[:, 0:2 * VW].rearrange("p (t c) -> p t c", c=VW),
                        v0[:, 2 * i:2 * i + 2, 0, :])
                for t in range(NT):
                    k = first("v_dc") + t
                    low(b, k, v12[:, t, :, 1, :], bank(k)[:, 0:2 * VW].rearrange("p (i c) -> p i c", c=VW),
                        v12[:, t, :, 0, :])
                    if t == 0:
                        dve.wait_ge(norm_g, b * 2 + 2)
                        dve.reciprocal(inv_norm[:], norm[:]).then_inc(norm_v, 1)
                        dve.wait_ge(norm_v, b * 2 + 1)
                        dve.tensor_scalar(inv_norm[:, 0:2 * NT:2], inv_norm[:, 0:2 * NT:2], inv_temp[:, 0:1], None,
                                          ALU.mult).then_inc(norm_v, 1)
                        dve.wait_ge(norm_v, b * 2 + 2)
                    if t in (1, 3):
                        half = t // 2
                        part_qk = qk_raw[:, half * 4:half * 4 + 4, :].rearrange("p t (w c) -> p (t w) c", c=C)
                        dve.tensor_tensor(part_qk, part_qk,
                                          inv_norm[:, half * 8:half * 8 + 8].unsqueeze(2).to_broadcast([P, 8, C]),
                                          ALU.mult).then_inc(qk_ready, 1)
                    if tail is not None and t == 5:
                        tile_h1_stats(tail, NT - 1)
                for which, name in ((0, "q_c"), (1, "k_c")):
                    for half in range(2):
                        k = first(name) + half
                        at = slice(half * 512, half * 512 + 512)
                        low(b, k, (k_lo if which else q_lo)[2][:, at], bank(k), (k_hi if which else q_hi)[2][:, at])

            def output(b, i):
                t, br = i // BR, i % BR
                dve.wait_ge(pv_done, b * UNITS + i + 1)
                dve.tensor_reduce(o[:, t % 4, br, :], mixed_of(i).rearrange("p (h c) -> p c h", h=2), AX_X,
                                  ALU.add).then_inc(o_ok, 1)

            def tile_stats(b, t):
                m = t % 2
                dve.wait_ge(o_ok, b * UNITS + BR * t + BR)
                for br in range(BR):
                    last = dve.bn_stats(st[:, m, br, :], o[:, t % 4, br, 0:C])
                last.then_inc(o_stats, 1)
                dve.wait_ge(o_stats, b * NT + t + 1)
                dve.nop(nofuse=True)
                for br in range(BR):
                    last = dve.bn_aggr(mv[:, m, br, :], st[:, m, br, :])
                last.then_inc(o_mv, 1)

            def tile_gate_logits(b, t):
                m, n = t % 2, b * NT + t
                dve.wait_ge(rstd_ok, n + 1)
                dve.tensor_tensor(logit9[:, m, :, 0:BR], o[:, t % 4, :, C:C + 3].rearrange("p i g -> p g i"),
                                  rstd[:, m, :].unsqueeze(1).to_broadcast([P, 3, BR]), ALU.mult).then_inc(logit_c, 1)
                dve.wait_ge(logit_c, n * 2 + 1)
                dve.tensor_reduce(logit[:, m, :], logit9[:, m, :, :], AX_X, ALU.add).then_inc(logit_c, 1)
                dve.wait_ge(logit_c, n * 2 + 2)
                dve.tensor_reduce(logit_nm[:, m:m + 1], logit[:, m, :], AX_X, ALU.max, negate=True).then_inc(logit_ok, 1)

            def tile_gate(b, t):
                m, n = t % 2, b * NT + t
                dve.wait_ge(gate_ok, n + 1)
                dve.reciprocal(gate_inv[:, m:m + 1], gate_sum[:, m:m + 1]).then_inc(gate_c, 1)
                dve.wait_ge(gate_c, n + 1)
                dve.scalar_tensor_tensor(out=gate_r[:, m, :], in0=gate_e[:, m, :], scalar=gate_inv[:, m:m + 1],
                                         in1=rstd[:, m, :], op0=ALU.mult, op1=ALU.mult).then_inc(gate_r_ok, 1)
                dve.tensor_scalar(gate[:, m, :], gate_e[:, m, :], gate_inv[:, m:m + 1], None, ALU.mult).then_inc(scale_ok, 1)
                dve.wait_ge(gate_r_ok, n + 1)
                if t >= 2:
                    dve.wait_ge(h1_ok, n - 1)
                for br in range(BR):
                    last = dve.scalar_tensor_tensor(out=u[:, m, br, :], in0=o[:, t % 4, br, 0:C],
                                                    scalar=gate_r[:, m, br:br + 1], in1=R("ln_g")[:, br * C:(br + 1) * C],
                                                    op0=ALU.mult, op1=ALU.mult)
                last.then_inc(u_ok, 1)

            def tile_h1_stats(b, t):
                m, n = t % 2, b * NT + t
                dve.wait_ge(h1_ok, n + 1)
                dve.bn_stats(st2[:, m, :], h1[:, t, :]).then_inc(st2_ok, 1)
                dve.wait_ge(st2_ok, n + 1)
                dve.nop(nofuse=True)
                dve.bn_aggr(mv2[:, m, :], st2[:, m, :]).then_inc(mv2_ok, 1)

            def last_two_tiles():
                t, m = NT - 1, (NT - 1) % 2
                dve.wait_ge(scale_ok, TT)
                dve.wait_ge(u_ok, TT)
                for br in range(BR):
                    last = dve.scalar_tensor_tensor(out=zb[:, m, br, :], in0=R("ln_b")[:, br * C:(br + 1) * C],
                                                    scalar=gate[:, m, br:br + 1], in1=u[:, m, br, :],
                                                    op0=ALU.mult, op1=ALU.add)
                last.then_inc(last_v, 1)
                dve.wait_ge(last_v, 1)
                dve.tensor_tensor(zb[:, m, 1, :], zb[:, m, 1, :], zb[:, m, 2, :], ALU.add)
                dve.tensor_tensor(zb[:, m, 0, :], zb[:, m, 0, :], h[:, ((B - 1) % 2) * NT + t, :], ALU.add).then_inc(last_v, 1)
                dve.wait_ge(h1_ok, TT - 1)
                dve.bn_stats(st2_last[:, 0, :], h1[:, t - 1, :])
                dve.wait_ge(last_v, 2)
                dve.tensor_tensor(h1[:, t, :], zb[:, m, 0, :], zb[:, m, 1, :], ALU.add).then_inc(h1_ok, 1)
                dve.wait_ge(h1_ok, TT)
                dve.bn_stats(st2_last[:, 1, :], h1[:, t, :]).then_inc(last_v, 1)
                dve.wait_ge(last_v, 3)
                dve.nop(nofuse=True)
                for i in range(2):
                    last = dve.bn_aggr(mv2_last[:, i, :], st2_last[:, i, :])
                last.then_inc(last_v, 1)
                dve.wait_ge(last_g, 2)
                for i in range(2):
                    dve.tensor_scalar(trow[:, t - 1 + i, 0:C], h1[:, t - 1 + i, :], mv2_last[:, i, 0:1],
                                      rstd2_last[:, i:i + 1], ALU.subtract, ALU.mult).then_inc(x2_ok, 1)

            def route_softmax_1(b):
                dve.wait_ge(routed, b + 1 if not isinstance(b, int) or b < B - 1 else B + 1)
                dve.tensor_tensor(r_log, mixed[:, 512:512 + NT * NE].rearrange("p (t e) -> p t e", e=NE),
                                  R("b_router").unsqueeze(1).to_broadcast([P, NT, NE]), ALU.add).then_inc(route_v, 1)
                dve.wait_ge(route_v, b * 5 + 1)
                dve.tensor_reduce(r_nm[:], r_log, AX_X, ALU.max, negate=True).then_inc(route_v, 1)
                dve.wait_ge(route_v, b * 5 + 2)
                dve.tensor_tensor(r_sub, r_log, r_nm[:].unsqueeze(2).to_broadcast([P, NT, NE]),
                                  ALU.add).then_inc(route_v, 1)

            def route_softmax_2(b, kept=False):
                dve.wait_ge(route_e, b + 1)
                dve.tensor_reduce(r_sum[:], r_exp, AX_X, ALU.add).then_inc(route_v, 1)
                dve.wait_ge(route_v, b * 5 + 4)
                dve.reciprocal(r_inv[:], r_sum[:]).then_inc(route_v, 1)
                dve.wait_ge(route_v, b * 5 + 5)
                dve.tensor_tensor(trow[:, :, C:XW], r_exp, r_inv[:].unsqueeze(2).to_broadcast([P, NT, NE]),
                                  ALU.mult).then_inc(prob_ok, 1)
                if kept:
                    dve.wait_ge(prob_kept, B - 1)
                    dve.tensor_tensor(prob_rows(b), r_exp, r_inv[:].unsqueeze(2).to_broadcast([P, NT, NE]),
                                      ALU.mult).then_inc(prob_kept, 1)

            def attention(b, more, tail):
                def maxima(i):
                    n = SD if i % BR == 0 else S
                    dve.wait_ge(scored, b * UNITS + i + 1)
                    dve.tensor_reduce(neg_max[:, i % 4:i % 4 + 1], scores[:, (i % 2) * S:(i % 2) * S + n], AX_X,
                                      ALU.max, negate=True).then_inc(maxed, 1)

                def low_part(i):
                    if i >= 2:
                        dve.wait_ge(pv_done, b * UNITS + i - 1)
                    for half in range(1 if i % BR == 0 else 2):
                        at = slice(half * 512, half * 512 + 512)
                        dve.wait_ge(hi_done, b * PARTS + part(i, half))
                        dve.tensor_tensor(pT_lo[:, i % 2, at], turned[:, at], pT_hi[:, i % 2, at].bitcast(F32),
                                          ALU.subtract).then_inc(lo_done, 1)

                for i in range(UNITS + 3):
                    if more and i == UNITS + 1:
                        normalise(b + 1, 1)
                    if 0 <= i - 2 < UNITS:
                        low_part(i - 2)
                    if i < UNITS:
                        maxima(i)
                    if i >= 4:
                        output(b, i - 4)
                    if i == 2 and tail is not None:
                        route_softmax_1(tail)
                    if i == 4 and tail is not None:
                        route_softmax_2(tail)
                    if more and i == UNITS:
                        token_add(b + 1, NT - 1, token_psum)
                        token_stats(b + 1, NT - 1)
                    if more and i == UNITS + 1:
                        tokens_low(b + 1)
                    for t in range(NT):
                        stage = i - 3 * t - 6
                        if stage == 6:
                            tile_h1_stats(b, t)
                        if stage == 0:
                            tile_stats(b, t)
                        if stage == 2:
                            tile_gate_logits(b, t)
                        if stage == 4:
                            tile_gate(b, t)
                    if more:
                        if i % BR == 0 and 0 < i < UNITS:
                            token_add(b + 1, i // BR - 1, token_psum)
                        if i % BR == 1 and 1 < i < UNITS:
                            token_stats(b + 1, i // BR - 1)
                        if i == 6 * BR:
                            normalise(b + 1, 0)
                output(b, UNITS - 1)
                tile_stats(b, NT - 1)

            hashes()
            setup()
            for t in range(NT):
                token_add(0, t, first_psum)
                token_stats(0, t)
                if t == 5:
                    normalise(0, 0)
            normalise(0, 1)
            prologue(0, None)
            attention(0, True, None)
            prologue(1, 0)
            with dve.Fori(1, B - 1) as b:
                attention(b, True, b - 1)
                prologue(b + 1, b)
            attention(B - 1, False, B - 2)
            tile_gate(B - 1, NT - 2)
            tile_gate_logits(B - 1, NT - 1)
            tile_h1_stats(B - 1, NT - 3)
            tile_gate(B - 1, NT - 1)
            last_two_tiles()
            route_softmax_1(B - 1)
            route_softmax_2(B - 1, True)

        @block.scalar
        def _(act):
            def high(b, k, dst, src, bias=0.0):
                act.wait_ge(bank_full, b * NUSE + k + 1)
                act.activation(dst, src, ACT.Identity, bias=bias).then_inc(bank_a, 1)

            def gram_copy(s, t):
                act.wait_ge(gram_turned, s * NT + t + 1)
                src, dst = spare(t)[:, 0:3 * P].rearrange("p (g t) -> p g t", t=P), gramT_of(t)
                for g0, g1, at in (((0, 2, slice(1, P)), (2, 3, slice(2, P))) if t == 0 else
                                   ((0, 1, slice(0, P)), (1, 3, slice(0, P - 1))) if t == NT - 1 else
                                   ((0, 3, slice(0, P)),)):
                    last = act.activation(dst[:, g0:g1, at], src[:, g0:g1, at], ACT.Identity)
                last.then_inc(gram_copied, 1)

            def tokens_high(b):
                for half in range(2):
                    k = first("xT") + half
                    high(b, k, xT_hi[:, 2 + half * 512:514 + half * 512], bank(k))

            def norm_squares(b, t):
                act.wait_ge(bank_a, b * A_READS + reads("a", first("qk_raw") + t // 2))
                for which in range(2):
                    last = act.activation(square[:, t, which * C:(which + 1) * C], qk_raw[:, t, which * C:(which + 1) * C],
                                          ACT.Square, accum_out=norm[:, 2 * t + which:2 * t + which + 1])
                last.then_inc(sq_ready, 1)

            def prologue(b, tail):
                if tail is None:
                    tokens_high(b)
                for i in range(4):
                    k = first("qk_raw") + i
                    high(b, k, qk_raw[:, 2 * i:2 * i + 2, :], bank(k).rearrange("p (t c) -> p t c", c=2 * C))
                    if tail is not None and i == 1:
                        tile_gate_exp(tail, NT - 1)
                    for t in range(2 * i - 2, 2 * i) if i > 0 else ():
                        norm_squares(b, t)
                high(b, first("down"), down_hi[:], bank(first("down")), col[:, COL["db"]:COL["db"] + 1])
                for br, which, name in ((1, q_hi, "q_d"), (1, k_hi, "k_d"), (0, q_hi, "q_cr")):
                    for half in range(2):
                        k = first(name) + half
                        high(b, k, which[br][:, half * 512:half * 512 + 512], bank(k),
                             col[:, COL["b" + name]:COL["b" + name] + 1])
                    for t in (6,) if name == "q_d" else (7,) if name == "k_d" else ():
                        norm_squares(b, t)
                high(b, first("k_cr"), k_hi[0][:], bank(first("k_cr")), col[:, COL["bk_cr"]:COL["bk_cr"] + 1])
                for i in range(2):
                    k = first("v_cr") + i
                    high(b, k, v0[:, 2 * i:2 * i + 2, 0, :], bank(k)[:, 0:2 * VW].rearrange("p (t c) -> p t c", c=VW))
                for t in range(NT):
                    k = first("v_dc") + t
                    high(b, k, v12[:, t, :, 0, :], bank(k)[:, 0:2 * VW].rearrange("p (i c) -> p i c", c=VW))
                for which, name in ((0, "q_c"), (1, "k_c")):
                    for half in range(2):
                        k = first(name) + half
                        high(b, k, (k_hi if which else q_hi)[2][:, half * 512:half * 512 + 512], bank(k))

            def route_copy(b, lo=0, hi=NT):
                act.wait_ge(x2_turned, b + 1)
                act.activation(x2T[:, lo * P:hi * P], turned[:, lo * P:hi * P], ACT.Identity).then_inc(x2T_ok, 1)

            def route_exp(b):
                act.wait_ge(route_v, b * 5 + 3)
                act.activation(r_exp, r_sub, ACT.Exp).then_inc(route_e, 1)

            def tile_gate_exp(b, t):
                m = t % 2
                act.wait_ge(logit_ok, b * NT + t + 1)
                act.activation(gate_e[:, m, :], logit[:, m, :], ACT.Exp, bias=logit_nm[:, m:m + 1],
                               accum_out=gate_sum[:, m:m + 1]).then_inc(gate_ok, 1)

            def attention(b, more, tail):
                def exponent(i):
                    t, br = i // BR, i % BR
                    n = SD if br == 0 else S
                    act.wait_ge(maxed, b * UNITS + i + 1)
                    if i >= 2:
                        act.wait_ge(turn_done, b * PARTS + part(i - 2))
                    act.activation(probs[:, i % 2, 0:n], scores[:, (i % 2) * S:(i % 2) * S + n], ACT.Exp,
                                   bias=neg_max[:, i % 4:i % 4 + 1],
                                   accum_out=exp_sum[:, t % 4, br:br + 1]).then_inc(exped, 1)

                def high_part(i):
                    if i >= 2:
                        act.wait_ge(pv_done, b * UNITS + i - 1)
                    for half in range(1 if i % BR == 0 else 2):
                        at = slice(half * 512, half * 512 + 512)
                        act.wait_ge(turn_done, b * PARTS + part(i, half))
                        act.activation(pT_hi[:, i % 2, at], turned[:, at], ACT.Identity).then_inc(hi_done, 1)

                for i in range(UNITS + 3):
                    if 0 <= i - 2 < UNITS:
                        high_part(i - 2)
                    if more and i == UNITS + 2:
                        tokens_high(b + 1)
                    if i < UNITS:
                        exponent(i)
                    if i == 0 and tail is not None:
                        route_copy(tail)
                    if i == 3 and tail is not None:
                        route_exp(tail)
                    for t in range(NT):
                        stage = i - 3 * t - 6
                        if stage == 3:
                            tile_gate_exp(b, t)
                    if more and (i == 1 or i % BR == 0 and 0 < i < UNITS):
                        gram_copy(b + 1, i // BR)
                tile_gate_exp(b, NT - 2)

            act.wait_ge(loaded, 64)
            act.wait_ge(weights_ready, 2)
            for t in range(NT):
                gram_copy(0, t)
            prologue(0, None)
            attention(0, True, None)
            prologue(1, 0)
            with act.Fori(1, B - 1) as b:
                attention(b, True, b - 1)
                prologue(b + 1, b)
            attention(B - 1, False, B - 2)
            tile_gate_exp(B - 1, NT - 1)
            route_copy(B - 1, 0, EARLY)
            route_copy(B, EARLY, NT)
            route_exp(B - 1)

        @block.gpsimd
        def _(pool):
            def gathers(s, t):
                if t >= 4 or not isinstance(s, int) or s > 0:
                    pool.wait_ge(gram_turned, s * NT + t - 3)
                    pool.nop(nofuse=True)
                pool.tensor_copy(ids_now[:, 3 * t:3 * t + 3],
                                 ids[:, bass.ds(s, 1), t, :].rearrange("p b g -> p (b g)")).then_inc(staged, 1)
                pool.wait_ge(staged, s * NT + t + 1)
                pool.nop(nofuse=True)
                for g in range(3):
                    pool.indirect_dma_start(gram[:, t % 4, g, :], None, emb[g],
                                            bass.IndirectOffsetOnAxis(ap=ids_now[:, 3 * t + g:3 * t + g + 1], axis=0)
                                            ).then_inc(gathered[t % 4], 16)

            def token_rstd(s, half):
                part = rstd1[:, half * 4:half * 4 + 4]
                pool.wait_ge(ln1_mv, s * NT + half * 4 + 4)
                pool.nop(nofuse=True)
                pool.tensor_scalar(part, mv1[:, half * 4:half * 4 + 4, 1], LN_EPS, None, ALU.add).then_inc(ln1_g, 1)
                pool.wait_ge(ln1_g, s * 2 + half + 1)
                pool.tensor_tensor(part, part, m_half[:, 0:4], ALU.pow).then_inc(ln1_rstd, 1)

            def prologue(b, tail):
                if tail is not None:
                    last_tiles(tail)
                pool.wait_ge(sq_ready, b * NT + NT)
                pool.tensor_tensor(norm[:], norm[:], p_half[:], ALU.pow).then_inc(norm_g, 1)
                pool.wait_ge(norm_g, b * 2 + 1)
                pool.nop(nofuse=True)
                pool.tensor_scalar(norm[:], norm[:], NORM_EPS, None, ALU.add).then_inc(norm_g, 1)
                if tail is not None:
                    last_x2(tail)

            def keep_probs(b):
                pool.wait_ge(prob_ok, b + 1)
                pool.tensor_copy(prob_rows(b), trow[:, :, C:XW]).then_inc(prob_kept, 1)

            def tile_rstd(b, t):
                m, n = t % 2, b * NT + t
                pool.wait_ge(exped, b * UNITS + BR * t + BR)
                s = exp_sum[:, t % 4, :]
                pool.tensor_tensor(sum_sq[:, m, :], s, s, ALU.mult).then_inc(rstd_g, 1)
                pool.wait_ge(rstd_g, n * 3 + 1)
                pool.nop(nofuse=True)
                pool.tensor_scalar(var_eps[:, m, :], sum_sq[:, m, :], LN_EPS, None, ALU.mult).then_inc(rstd_g, 1)
                pool.wait_ge(rstd_g, n * 3 + 2)
                pool.wait_ge(o_mv, n + 1)
                pool.tensor_tensor(var_eps[:, m, :], var_eps[:, m, :], mv[:, m, :, 1], ALU.add).then_inc(rstd_g, 1)
                pool.wait_ge(rstd_g, n * 3 + 3)
                pool.tensor_tensor(rstd[:, m, :], var_eps[:, m, :], m_half[:, 0:BR], ALU.pow).then_inc(rstd_ok, 1)

            def tile_sum(b, t):
                m, n = t % 2, b * NT + t
                k = [n * 4]

                def step(ins):
                    k[0] = k[0] + 1
                    ins.then_inc(z_g, 1)
                    pool.wait_ge(z_g, k[0])

                pool.wait_ge(scale_ok, n + 1)
                shift = R("ln_b")
                step(pool.tensor_tensor(zb[:, m, :, :], shift.rearrange("p (i c) -> p i c", c=C),
                                        gate[:, m, :].unsqueeze(2).to_broadcast([P, BR, C]), ALU.mult))
                step(pool.tensor_tensor(zb[:, m, 0, :], zb[:, m, 0, :], h[:, bass.ds((b % 2) * NT + t, 1), :], ALU.add))
                pool.wait_ge(u_ok, n + 1)
                step(pool.tensor_tensor(u[:, m, :, :], u[:, m, :, :], zb[:, m, :, :], ALU.add))
                step(pool.tensor_tensor(u[:, m, 0, :], u[:, m, 0, :], u[:, m, 1, :], ALU.add))
                if t == 0:
                    pool.wait_ge(h1_free, b + 1)
                pool.tensor_tensor(h1[:, t, :], u[:, m, 0, :], u[:, m, 2, :], ALU.add).then_inc(h1_ok, 1)

            def tile_x2(b, t):
                m, n = t % 2, b * NT + t
                pool.wait_ge(mv2_ok, n + 1)
                pool.nop(nofuse=True)
                pool.tensor_scalar(ve2[:, m:m + 1], mv2[:, m, 1:2], LN_EPS, None, ALU.add).then_inc(ve2_ok, 1)
                pool.wait_ge(ve2_ok, n + 1)
                pool.tensor_tensor(rstd2[:, m:m + 1], ve2[:, m:m + 1], m_half[:, 0:1], ALU.pow).then_inc(rstd2_ok, 1)
                if t == 0:
                    pool.wait_ge(rows_free, b + 1)
                pool.wait_ge(rstd2_ok, n + 1)
                pool.nop(nofuse=True)
                pool.tensor_scalar(trow[:, t, 0:C], h1[:, t, :], mv2[:, m, 0:1], rstd2[:, m:m + 1],
                                   ALU.subtract, ALU.mult).then_inc(x2_ok, 1)

            def last_tiles(b):
                tile_rstd(b, NT - 1)
                tile_x2(b, NT - 3)
                tile_sum(b, NT - 2)

            def last_x2(b):
                tile_sum(b, NT - 1)
                tile_x2(b, NT - 2)
                tile_x2(b, NT - 1)

            def attention(b, more, tail):
                if more:
                    for t in range(4):
                        gathers(b + 1, t)
                if tail is not None:
                    keep_probs(tail)
                for t in range(NT - 1):
                    if more and t == 6:
                        token_rstd(b + 1, 1)
                    tile_rstd(b, t)
                    if more and t == 3:
                        token_rstd(b + 1, 0)
                    if t >= 2:
                        tile_x2(b, t - 2)
                    if t >= 1:
                        tile_sum(b, t - 1)
                    if more and t < 4:
                        gathers(b + 1, t + 4)

            pool.memset(xwi[:], 0).then_inc(setup_g, 1)
            pool.memset(wide[:], 0.0).then_inc(setup_g, 1)
            pool.memset(mean_w[:], 1.0 / C).then_inc(setup_g, 1)
            pool.memset(ones_row[:], 1.0).then_inc(setup_g, 1)
            pool.memset(m_half[:], -0.5).then_inc(setup_g, 1)
            pool.memset(p_half[:], 0.5).then_inc(setup_g, 1)
            pool.memset(xT_hi[:, 0:2].bitcast(F32), 0.0)
            pool.memset(xT_lo[:, 0:2].bitcast(F32), 0.0).then_inc(setup_g, 1)
            pool.memset(gramT[:, 0, :, 0:1], 0.0)
            pool.memset(gramT[:, 0, 2, 1:2], 0.0)
            pool.memset(gramT[:, 3, 1:3, P - 1:P], 0.0).then_inc(setup_g, 1)
            pool.wait_ge(setup_g, 8)
            pool.wait_ge(ids_ready, 2)
            for t in range(NT):
                gathers(0, t)
                if t == 6:
                    token_rstd(0, 0)
            token_rstd(0, 1)
            prologue(0, None)
            attention(0, True, None)
            prologue(1, 0)
            with pool.Fori(1, B - 1) as b:
                attention(b, True, b - 1)
                prologue(b + 1, b)
            attention(B - 1, False, B - 2)
            tile_rstd(B - 1, NT - 1)
            tile_sum(B - 1, NT - 2)
            tile_x2(B - 1, NT - 3)
            pool.wait_ge(last_v, 4)
            pool.tensor_scalar(rstd2_last[:], mv2_last[:, :, 1], LN_EPS, None, ALU.add).then_inc(last_g, 1)
            pool.wait_ge(last_g, 1)
            pool.tensor_tensor(rstd2_last[:], rstd2_last[:], m_half[:, 0:2], ALU.pow).then_inc(last_g, 1)

        first_part.__exit__(None, None, None)
        attn.close()
        experts(nc, ctx, con, prob, scores, turned, mixed, table, cand_bits, w_up, b_up, w_down, out)


def experts(nc, ctx, con, prob, scores, turned, mixed, table, cand_bits, w_up, b_up, w_down, out):
    CT = TT // CHUNKS
    RW = P + 2

    def sb(name, shape, dt=F32):
        return ctx.enter_context(nc.sbuf_tensor(name, shape, dt))

    def sem(name):
        return ctx.enter_context(nc.semaphore(name))

    def K(name):
        return con[:, CON[name][0]:CON[name][1]]

    ident = K("ident")

    same_twice = sb("same_twice", [P, P])
    bits_i = sb("bits_i", [P, BITS + 1], I32)
    bits_f = sb("bits_f", [P, BITS + 1])
    probT = sb("probT", [P, CT * P])
    odd = sb("odd", [P, CT * P - SPLIT])
    below = sb("below", [P, CT * P], BF16)
    below_a = sb("below_a", [P, CT * P - SPLIT], BF16)
    count = sb("count", [P, 1])
    count_a = sb("count_a", [P, 1])
    cand = sb("cand", [P, 1], I32)
    cand_next = sb("cand_next", [P, 1], I32)
    drop = sb("drop", [P, 1], I32)
    thr_row = sb("thr_row", [NE, P])
    thr = sb("thr", [P, NE])
    ones_bf = sb("ones_bf", [P, P], BF16)
    upto_bf = sb("upto_bf", [P, P], BF16)
    after_bf = sb("after_bf", [P, P], BF16)
    below_bf = sb("below_bf", [P, P], BF16)
    slot_bf = sb("slot_bf", [P, TOPK], BF16)
    over = sb("over", [P, TT, NE], BF16)
    tie = sb("tie", [P, TT, NE], BF16)
    tie_in = sb("tie_in", [P, TT, NE], BF16)
    n_over = sb("n_over", [P, NE])
    room = sb("room", [P, NE])
    tie_tile = sb("tie_tile", [P, NE, TT + 1])
    keep = sb("keep", [P, NE, TT + 1])
    tie_before = sb("tie_before", [P, NE, TT + 1])
    tie_rank = sb("tie_rank", [P, TT, NE])
    chosen = sb("chosen", [P, TT + 1, NE], BF16)
    ranks = sb("ranks", [TT, NE, RW], BF16)
    before = sb("before", [TT, NE])
    reached = sb("reached", [TT, NE, TOPK], BF16)
    less = sb("less", [P, NE * HALVES, P], BF16)
    n_less = sb("n_less", [P, NE * HALVES])
    tile_no = sb("tile_no", [P, NE * HALVES])
    slot_f = sb("slot_f", [P, NE * HALVES])
    slots = sb("slots", [P, NE * HALVES], I32)
    EB = GROUP
    g_ids = sb("g_ids", [P, EB * HALVES], I32)
    s_ids = sb("s_ids", [P, EB * HALVES], I32)
    bup = sb("bup", [FP, NG * FC])
    wu = sb("wu", [P, EB, DFF])
    wd = sb("wd", [FP, EB, FC, C])
    xg = sb("xg", [P, EB, HALVES, XW])
    xT = sb("xT", [P, 2, TOPK])
    hid = sb("hid", [FP, 2, FC, TOPK])
    yw = sb("yw", [P, EB, HALVES, C])

    bits_in = sem("bits_in")
    twice_ok = sem("twice_ok")
    prob_turned = sem("prob_turned")
    prob_copied = sem("prob_copied")
    made = sem("made")
    made_g = sem("made_g")
    odd_ok = sem("odd_ok")
    counted = sem("counted")
    counted_a = sem("counted_a")
    totalled = sem("totalled")
    cand_c = sem("cand_c")
    drop_ok = sem("drop_ok")
    cand_ok = sem("cand_ok")
    thr_v = sem("thr_v")
    thr_t = sem("thr_t")
    masks = sem("masks")
    sums_t = sem("sums_t")
    pick_v = sem("pick_v")
    chosen_ok = sem("chosen_ok")
    rank_t = sem("rank_t")
    rank_a = sem("rank_a")
    before_t = sem("before_t")
    before_v = sem("before_v")
    reached_ok = sem("reached_ok")
    row_t = sem("row_t")
    row_v = sem("row_v")
    row_a = sem("row_a")
    slots_v = sem("slots_v")
    slots_ok = sem("slots_ok")
    g_staged = sem("g_staged")
    s_staged = sem("s_staged")
    bup_in = sem("bup_in")
    w_in = [sem(f"w_in{j}") for j in range(EB)]
    x_in = [sem(f"x_in{j}") for j in range(EB)]
    xt_t = sem("xt_t")
    xt_v = sem("xt_v")
    up_t = sem("up_t")
    hid_a = sem("hid_a")
    down_t = sem("down_t")
    y_v = sem("y_v")
    added = sem("added")
    ones_set = sem("ones_set")

    rows_out = out.rearrange("b s c -> (b s) c")

    def wave(e):
        return e // EB + 1

    def slot_bank(k):
        k = k % 8
        return (scores[:, k * 512:(k + 1) * 512] if k < 4 else turned[:, (k - 4) * 512:(k - 3) * 512] if k < 6
                else mixed[:, (k - 6) * 512:(k - 5) * 512])

    row_banks = [(half, e0, min(3, NE - e0)) for e0 in range(0, NE, 3) for half in range(HALVES)]

    block = ctx.enter_context(nc.Block())

    @block.sync
    def _(sp):
        sp.dma_start(bits_i[:], cand_bits[0]).then_inc(bits_in, 16)
        sp.dma_start(bits_f[:], cand_bits[1]).then_inc(bits_in, 16)
        sp.dma_start(bup[:], b_up.rearrange("p g c -> p (g c)")).then_inc(bup_in, 16)

        def load(g, j):
            sp.dma_start(wu[:, j, :], w_up[bass.ds(g, 1), :, :].rearrange("g h f -> (g h) f")).then_inc(w_in[j], 16)
            sp.dma_start(wd[:, j, :, :], w_down[bass.ds(g * GROUP + j, 1), :, :].rearrange("e (c p) h -> p (e c) h", p=FP)
                         ).then_inc(w_in[j], 16)

        for j in range(EB):
            load(0, j)
        with sp.Fori(0, NG - 1) as g:
            for j in range(EB):
                sp.wait_ge(down_t, g * GROUP + j + 1)
                load(g + 1, j)

    @block.tensor
    def _(pe):
        for u in range(CT):
            last = pe.transpose(scores[:, u * P:(u + 1) * P], prob[:, u * CHUNKS:(u + 1) * CHUNKS, :].rearrange("p c e -> p (c e)"), ident)
            if u % 4 == 3:
                last.then_inc(prob_turned, 1)
        pe.wait_ge(twice_ok, 1)
        def total(k):
            pe.wait_ge(counted_a, k + 1)
            pe.matmul(turned[:, 0:1], K("same"), count_a[:], start=True, stop=False)
            pe.wait_ge(counted, k + 1)
            pe.matmul(turned[:, 0:1], same_twice[:], count[:], start=False, stop=True).then_inc(totalled, 1)

        with pe.Fori(0, (BITS - 1) // STEP) as g:
            for j in range(STEP):
                total(g * STEP + j)
        for k in range((BITS - 1) // STEP * STEP, BITS - 1):
            total(k)
        pe.wait_ge(counted, BITS)
        pe.matmul(turned[:, 0:1], K("same"), count[:], start=True, stop=True).then_inc(totalled, 1)
        pe.wait_ge(thr_v, 1)
        pe.transpose(turned[:, 512:512 + NE], thr_row[:], ident[0:NE, 0:NE]).then_inc(thr_t, 1)
        pe.wait_ge(made, 4)
        pe.wait_ge(made_g, 1)
        pe.wait_ge(masks, 1)
        for q in range(4):
            last = pe.matmul(turned[:, 0:512], ones_bf[:], over[:, q * 16:(q + 1) * 16, :], start=(q == 0), stop=(q == 3))
        last.then_inc(sums_t, 1)
        pe.wait_ge(masks, 2)
        pe.wait_ge(prob_copied, 4)
        for q in range(4):
            last = pe.matmul(scores[:, q * 512:(q + 1) * 512], ones_bf[:], tie[:, q * 16:(q + 1) * 16, :],
                             start=True, stop=True)
        last.then_inc(sums_t, 1)
        pe.wait_ge(pick_v, 1)
        for q in range(4):
            last = pe.matmul(slot_bank(4 + q), upto_bf[:], tie[:, q * 16:(q + 1) * 16, :], start=True, stop=True)
        last.then_inc(sums_t, 1)
        pe.wait_ge(chosen_ok, 1)
        for e in range(NE):
            dst = slot_bank(e // 4)[0:TT, (e % 4) * P:(e % 4 + 1) * P]
            pe.matmul(dst, chosen[:, 1:TT + 1, e], upto_bf[:], start=True, stop=False)
            last = pe.matmul(dst, chosen[:, 0:TT, e], after_bf[:], start=False, stop=True)
            if e % 4 == 3:
                last.then_inc(rank_t, 1)
        pe.wait_ge(rank_a, 8)
        pe.matmul(scores[0:TT, 0:NE], below_bf[0:TT, 0:TT], ranks[:, :, P - 1], start=True, stop=True).then_inc(before_t, 1)
        pe.wait_ge(before_v, 1)
        for n, (half, e0, m) in enumerate(row_banks):
            pe.wait_ge(reached_ok, min(e0 + m, NE))
            if n >= 8:
                pe.wait_ge((row_v, row_a)[half], (n - 8) // 2 + 1)
            for i in range(m):
                last = pe.matmul(slot_bank(n)[:, i * RW:(i + 1) * RW], reached[:, e0 + i, half * P:(half + 1) * P],
                                 ranks[:, e0 + i, :], start=True, stop=True)
            last.then_inc(row_t, 1)
        pe.wait_ge(row_v, len(row_banks) // 2)
        pe.wait_ge(row_a, len(row_banks) // 2)

        def turn(e, j):
            pe.wait_ge(x_in[j % EB], wave(e) * 32)
            if not isinstance(e, int) or e >= 2:
                pe.wait_ge(xt_v, e - 1)
            for half in range(HALVES):
                last = pe.transpose(scores[:, (j % 2) * 512 + half * P:(j % 2) * 512 + (half + 1) * P],
                                    xg[:, j % EB, half, 0:C], ident)
            last.then_inc(xt_t, 1)

        def up_bank(j):
            return scores[:, 1024:2048] if j % 2 == 0 else turned[:]

        def up(e, j):
            pe.wait_ge(w_in[j % EB], wave(e) * 32)
            pe.wait_ge(xt_v, e + 1)
            if not isinstance(e, int) or e >= 2:
                pe.wait_ge(hid_a, e - 1)
            for c in range(FC):
                n = FP if c < FC - 1 else FP - 1
                last = pe.matmul(up_bank(j)[0:n, c * TOPK:(c + 1) * TOPK], wu[:, j % EB, c * FP:c * FP + n],
                                 xT[:, j % 2, :], start=True, stop=True)
            last.then_inc(up_t, 1)

        def down(e, j):
            pe.wait_ge(hid_a, e + 1)
            if not isinstance(e, int) or e >= 2:
                pe.wait_ge(y_v, e - 1)
            for half in range(HALVES):
                for c in range(FC):
                    last = pe.matmul(mixed[:, (j % 2) * 512 + half * C:(j % 2) * 512 + (half + 1) * C],
                                     hid[:, j % 2, c, half * P:(half + 1) * P], wd[:, j % EB, c, :],
                                     start=(c == 0), stop=(c == FC - 1))
            last.then_inc(down_t, 1)

        pe.wait_ge(ones_set, 2)
        turn(0, 0)
        up(0, 0)
        turn(1, 1)

        def group(first_e):
            for j in range(EB):
                up(first_e + j + 1, j + 1)
                down(first_e + j, j)
                turn(first_e + j + 2, j + 2)

        group(0)
        with pe.Fori(1, NG - 1) as g:
            group(g * GROUP)
        for j in range(EB):
            e = NE - GROUP + j
            if e + 1 < NE:
                up(e + 1, j + 1)
            down(e, j)
            if e + 2 < NE:
                turn(e + 2, j + 2)

    @block.vector
    def _(dve):
        dve.memset(cand[:], 1 << (BITS - 1)).then_inc(cand_ok, 1)
        dve.wait_ge(bits_in, 32)
        dve.wait_ge(prob_copied, 4)
        dve.tensor_scalar(odd[:].bitcast(I32), probT[:, SPLIT:].bitcast(I32), 1, None, ALU.bitwise_or
                          ).then_inc(odd_ok, 1)

        def try_bit(k, tokens, limit):
            dve.wait_ge(cand_ok, k + 1)
            dve.tensor_scalar(below[:, 0:tokens], probT[:, 0:tokens], cand[:].bitcast(F32), None, ALU.is_lt, ALU.add,
                              accum_out=count[:]).then_inc(counted, 1)
            dve.tensor_tensor(cand_next[:], cand[:], bits_i[:, bass.ds(k + 1, 1)], ALU.bitwise_or).then_inc(cand_c, 1)
            dve.wait_ge(totalled, k + 1)
            dve.scalar_tensor_tensor(out=drop[:], in0=turned[:, 0:1], scalar=float(limit), in1=bits_f[:, bass.ds(k, 1)],
                                     op0=ALU.is_gt, op1=ALU.mult).then_inc(drop_ok, 1)
            dve.wait_ge(drop_ok, k + 1)
            dve.wait_ge(cand_c, k + 1)
            dve.tensor_tensor(cand[:], cand_next[:], drop[:], ALU.bitwise_xor).then_inc(cand_ok, 1)

        def try_half(k):
            try_bit(k, SPLIT, 2 * (TOK - TOPK) - CHUNKS * (CT * P - SPLIT))

        with dve.Fori(0, (BITS - 1) // STEP) as g:
            for j in range(STEP):
                try_half(g * STEP + j)
        for k in range((BITS - 1) // STEP * STEP, BITS - 1):
            try_half(k)
        try_bit(BITS - 1, CT * P, TOK - TOPK)
        dve.wait_ge(cand_ok, BITS + 1)
        dve.wait_ge(made_g, 1)
        dve.tensor_scalar(thr_row[:], thr_row[:], cand[0:NE, :].bitcast(F32), None, ALU.add).then_inc(thr_v, 1)
        dve.wait_ge(thr_t, 1)
        dve.tensor_copy(thr[:], turned[:, 512:512 + NE]).then_inc(thr_v, 1)
        dve.wait_ge(thr_v, 2)
        everywhere = thr[:].unsqueeze(1).to_broadcast([P, CT, NE])
        for mask, op in ((over, ALU.is_gt), (tie, ALU.is_equal)):
            for c in range(CHUNKS):
                last = dve.tensor_tensor(mask[:, c * CT:(c + 1) * CT, :], prob[:, c:TT:CHUNKS, :], everywhere, op)
            last.then_inc(masks, 1)
        dve.wait_ge(sums_t, 1)
        dve.tensor_reduce(n_over[:], turned[:, 0:512].rearrange("p (t e) -> p e t", e=NE), AX_X, ALU.add).then_inc(pick_v, 1)
        dve.wait_ge(sums_t, 2)
        for q in range(4):
            last = dve.tensor_copy(tie_tile[:, :, 1 + q * 16:17 + q * 16],
                                   scores[:, q * 512:(q + 1) * 512].rearrange("p (t e) -> p e t", e=NE))
        last.then_inc(pick_v, 1)
        dve.wait_ge(pick_v, 2)
        dve.tensor_scalar(room[:], n_over[:], -1.0, float(TOPK), ALU.mult, ALU.add)
        dve.tensor_tensor_scan(tie_before[:].rearrange("p e t -> p (e t)"), keep[:].rearrange("p e t -> p (e t)"),
                               tie_tile[:].rearrange("p e t -> p (e t)"), 0.0, ALU.mult, ALU.add).then_inc(pick_v, 1)
        dve.wait_ge(pick_v, 3)
        dve.wait_ge(sums_t, 3)
        for n, part in enumerate((turned, mixed)):
            last = dve.tensor_tensor(tie_rank[:, n * 32:(n + 1) * 32, :], part[:].rearrange("p (t e) -> p t e", e=NE),
                                     tie_before[:].rearrange("p e t -> p t e")[:, n * 32:(n + 1) * 32, :], ALU.add)
        last.then_inc(pick_v, 1)
        dve.wait_ge(pick_v, 4)
        dve.tensor_tensor(tie_in[:], tie_rank[:], room[:].unsqueeze(1).to_broadcast([P, TT, NE]),
                          ALU.is_le).then_inc(pick_v, 1)
        dve.wait_ge(pick_v, 5)
        dve.tensor_tensor(tie_in[:], tie_in[:], tie[:], ALU.mult).then_inc(pick_v, 1)
        dve.wait_ge(pick_v, 6)
        dve.tensor_tensor(chosen[:, 1:TT + 1, :], tie_in[:], over[:], ALU.add).then_inc(chosen_ok, 1)
        dve.wait_ge(before_t, 1)
        dve.tensor_copy(before[:], scores[0:TT, 0:NE]).then_inc(before_v, 1)
        dve.wait_ge(before_v, 1)
        for e in range(NE):
            dve.tensor_scalar(reached[:, e, :], slot_bf[0:TT, :], before[:, e:e + 1], None, ALU.is_gt).then_inc(reached_ok, 1)
        for n, (half, e0, m) in enumerate(row_banks):
            if half == 0:
                dve.wait_ge(row_t, n + 1)
                for i in range(m):
                    k = (e0 + i) * HALVES + half
                    dve.tensor_scalar(less[:, k, :], slot_bank(n)[:, i * RW:i * RW + P],
                                      K("slotcol")[:, half:half + 1], None, ALU.is_lt, ALU.add, accum_out=n_less[:, k:k + 1])
                at = slice(e0 * HALVES + half, (e0 + m - 1) * HALVES + half + 1, HALVES)
                dve.tensor_copy(tile_no[:, at], slot_bank(n)[:, 0:m * RW].rearrange("p (i r) -> p i r", r=RW)[:, :, P]
                                ).then_inc(row_v, 1)
        dve.wait_ge(row_v, len(row_banks) // 2)
        dve.wait_ge(row_a, len(row_banks) // 2)
        second = n_less[:].rearrange("p (e h) -> p e h", h=HALVES)[:, :, 1]
        dve.tensor_scalar(second, second, 0.5, P / 2.0, ALU.mult, ALU.add)
        dve.tensor_scalar(slot_f[:], tile_no[:], float(P), -float(P), ALU.mult, ALU.add).then_inc(slots_v, 1)
        dve.wait_ge(slots_v, 1)
        dve.tensor_tensor(slots[:], slot_f[:], n_less[:], ALU.add).then_inc(slots_ok, 1)

        def copy_x(e, j):
            dve.wait_ge(xt_t, e + 1)
            if not isinstance(e, int) or e >= 2:
                dve.wait_ge(up_t, e - 1)
            dve.tensor_copy(xT[:, j % 2, :], scores[:, (j % 2) * 512:(j % 2) * 512 + TOPK]).then_inc(xt_v, 1)

        def weigh(e, j):
            dve.wait_ge(down_t, e + 1)
            if not isinstance(e, int) or e >= EB:
                dve.wait_ge(added, (e - (EB - 1)) * 32)
            for half in range(HALVES):
                last = dve.tensor_scalar(yw[:, j % EB, half, :],
                                         mixed[:, (j % 2) * 512 + half * C:(j % 2) * 512 + (half + 1) * C],
                                         xg[:, j % EB, half, bass.ds(C + e, 1)], None, ALU.mult)
            last.then_inc(y_v, 1)

        copy_x(0, 0)
        copy_x(1, 1)
        for j in range(EB):
            weigh(j, j)
            copy_x(j + 2, j + 2)
        with dve.Fori(1, NG - 1) as g:
            for j in range(EB):
                weigh(g * GROUP + j, j)
                copy_x(g * GROUP + j + 2, j + 2)
        for j in range(EB):
            e = NE - GROUP + j
            weigh(e, j)
            if e + 2 < NE:
                copy_x(e + 2, j + 2)

    @block.scalar
    def _(act):
        act.activation(same_twice[:], K("same"), ACT.Identity, scale=2.0).then_inc(twice_ok, 1)
        for q in range(4):
            act.wait_ge(prob_turned, q + 1)
            act.activation(probT[:, q * 512:(q + 1) * 512], scores[:, q * 512:(q + 1) * 512],
                           ACT.Identity).then_inc(prob_copied, 1)
        act.wait_ge(odd_ok, 1)
        with act.Fori(0, BITS - 1) as k:
            act.wait_ge(cand_ok, k + 1)
            act.activation(below_a[:], odd[:], ACT.Sign, bias=cand[:].bitcast(F32), scale=-1.0,
                           accum_out=count_a[:]).then_inc(counted_a, 1)
        act.activation(upto_bf[:], K("upto"), ACT.Identity).then_inc(made, 1)
        act.activation(after_bf[:], K("after"), ACT.Identity).then_inc(made, 1)
        act.activation(below_bf[:], K("below"), ACT.Identity).then_inc(made, 1)
        act.activation(slot_bf[:], K("slot"), ACT.Identity).then_inc(made, 1)
        act.wait_ge(made_g, 1)
        for q in range(8):
            act.wait_ge(rank_t, q + 1)
            act.activation(ranks[:, 4 * q:4 * q + 4, 0:P], slot_bank(q)[0:TT, :].rearrange("p (e t) -> p e t", t=P),
                           ACT.Identity).then_inc(rank_a, 1)

        for n, (half, e0, m) in enumerate(row_banks):
            if half == 1:
                act.wait_ge(row_t, n + 1)
                for i in range(m):
                    k = (e0 + i) * HALVES + half
                    act.activation(less[:, k, :], slot_bank(n)[:, i * RW:i * RW + P], ACT.Sign,
                                   bias=K("slotmid")[:, half:half + 1], scale=-1.0, accum_out=n_less[:, k:k + 1])
                at = slice(e0 * HALVES + half, (e0 + m - 1) * HALVES + half + 1, HALVES)
                act.activation(tile_no[:, at], slot_bank(n)[:, 0:m * RW].rearrange("p (i r) -> p i r", r=RW)[:, :, P],
                               ACT.Identity).then_inc(row_a, 1)

        def silu(g, e, j):
            act.wait_ge(up_t, e + 1)
            if not isinstance(e, int) or e >= 2:
                act.wait_ge(down_t, e - 1)
            if not isinstance(e, int):
                act.nop(nofuse=True)
            src = scores[:, 1024:2048] if j % 2 == 0 else turned[:]
            for c in range(FC):
                n = FP if c < FC - 1 else FP - 1
                last = act.activation(hid[0:n, j % 2, c, :], src[0:n, c * TOPK:(c + 1) * TOPK], ACT.Silu,
                                      bias=bup[0:n, bass.ds(g * FC + c, 1)])
            last.then_inc(hid_a, 1)

        act.wait_ge(bup_in, 16)
        act.wait_ge(ones_set, 2)
        for j in range(EB):
            silu(0, j, j)
        with act.Fori(1, NG) as g:
            for j in range(EB):
                silu(g, g * GROUP + j, j)

    @block.gpsimd
    def _(pool):
        pool.memset(ones_bf[:], 1.0)
        pool.memset(thr_row[:], 0.0)
        pool.memset(tie_tile[:, :, 0:1], 0.0)
        pool.memset(keep[:, :, 1:TT + 1], 1.0)
        pool.memset(keep[:, :, 0:1], 0.0)
        pool.memset(chosen[:, 0:1, :], 0.0)
        pool.memset(ranks[:, :, P:P + 1], 1.0)
        pool.memset(ranks[:, :, P + 1:RW], 0.0).then_inc(made_g, 1)
        pool.wait_ge(made_g, 1)
        for j in range(2):
            pool.memset(hid[96:FP, j, FC - 1, :], 1.0).then_inc(ones_set, 1)

        def stage(to, e, j, done):
            pool.tensor_copy(to[:, j * HALVES:(j + 1) * HALVES], slots[:, bass.ds(e * HALVES, HALVES)]).then_inc(done, 1)
            pool.wait_ge(done, e + 1)
            pool.nop(nofuse=True)

        def gather(e, j):
            j = j % EB
            if not isinstance(e, int) or e >= EB:
                pool.wait_ge(y_v, e - (EB - 1))
                pool.nop(nofuse=True)
            stage(g_ids, e, j, g_staged)
            for half in range(HALVES):
                at = j * HALVES + half
                pool.indirect_dma_start(xg[:, j, half, :], None, table,
                                        bass.IndirectOffsetOnAxis(ap=g_ids[:, at:at + 1], axis=0)
                                        ).then_inc(x_in[j], 16)

        def scatter(e, j):
            if not isinstance(e, int) or e >= 1:
                pool.wait_ge(added, e * 32)
                pool.nop(nofuse=True)
            stage(s_ids, e, j, s_staged)
            pool.wait_ge(y_v, e + 1)
            pool.nop(nofuse=True)
            for half in range(HALVES):
                at = j * HALVES + half
                pool.indirect_dma_start(rows_out, bass.IndirectOffsetOnAxis(ap=s_ids[:, at:at + 1], axis=0),
                                        yw[:, j, half, :], None, compute_op=ALU.add).then_inc(added, 16)

        def group(first_e, ahead=EB):
            for j in range(EB):
                if j < ahead:
                    gather(first_e + j + 3, j + 3)
                scatter(first_e + j, j)

        pool.wait_ge(ones_set, 2)
        pool.wait_ge(slots_ok, 1)
        for j in range(3):
            gather(j, j)
        group(0)
        with pool.Fori(1, NG - 1) as g:
            group(g * GROUP)
        group(NE - GROUP, 1)
        pool.wait_ge(added, NE * 32)


def kernel(**inputs):
    import numpy as np
    import concourse.bacc as bacc
    from concourse.bass_utils import run_bass_kernel_spmd

    g = {k: np.ascontiguousarray(v) for k, v in inputs.items()}

    def a(name):
        return g["L0_attn_" + name]

    zero3 = np.zeros((C, VW - C), np.float32)
    parts = [a("dw").transpose(1, 2, 0).reshape(C, 3 * C), a("wq_cr").T, a("wk_cr").T, a("wq_d").T, a("wk_d").T,
             a("wq_c").T, a("wk_c").T]
    for br in ("cr", "d", "c"):
        parts += [a(f"wv_{br}").T, zero3]
    parts += [g["L0_tok_proj_w"].reshape(C, 3, C).transpose(2, 1, 0).reshape(C, 3 * C)]
    parts += [a(f"wv_{br}") for br in ("cr", "d", "c")]
    parts += [g["L0_ffn_W_router"]]
    weights = np.ascontiguousarray(np.concatenate(parts, axis=1))
    gw = a("gw").reshape(3, 3, C).transpose(2, 1, 0).reshape(C, 9)
    cols = np.ascontiguousarray(np.concatenate(
        [np.stack([a("db"), a("bq_cr"), a("bk_cr"), a("bq_d"), a("bk_d")] + [a(f"ln_{n}_g") for n in ("cr", "d", "c")]
                  + [a(f"ln_{n}_b") for n in ("cr", "d", "c")] + [a(f"bv_{n}") for n in ("cr", "d", "c")], axis=1), gw],
        axis=1))
    rows1 = np.concatenate([g["L0_tok_proj_b"], a("bq_c"), a("bk_c")] + [a(f"bv_{n}") for n in ("cr", "d", "c")]
                           + [a(f"ln_{n}_g") for n in ("cr", "d", "c")] + [a(f"ln_{n}_b") for n in ("cr", "d", "c")]
                           + [g["L0_ffn_b_router"], a("gb"), a("temp").reshape(1)])
    rows = np.ascontiguousarray(np.broadcast_to(rows1[None, :], (P, NROW)))
    i = np.arange(P)
    consts = np.ascontiguousarray(np.concatenate([
        np.eye(P), i[:, None] <= i[None, :], i[:, None] > i[None, :], i[:, None] < i[None, :],
        (i[:, None] % NE) == (i[None, :] % NE), np.broadcast_to(np.arange(1, TOPK + 1), (P, TOPK)),
        i[:, None] + 1 + P * np.arange(HALVES)[None, :], i[:, None] + 0.5 + P * np.arange(HALVES)[None, :]], axis=1).astype(np.float32))
    bits = np.concatenate([1 << np.arange(BITS - 1, -1, -1), [0]])
    bits_i = np.ascontiguousarray(np.broadcast_to(bits.astype(np.int32), (P, BITS + 1)))
    bits_f = np.ascontiguousarray(np.broadcast_to(bits.astype(np.float32), (P, BITS + 1)))
    w_down = np.ascontiguousarray(np.concatenate([g["L0_ffn_W_down"], g["L0_ffn_b_down"][:, None, :]], axis=1))
    b_up = np.ascontiguousarray(np.concatenate([g["L0_ffn_b_up"], np.zeros((NG, 1), np.float32)], axis=1)
                                .reshape(NG, FC, FP).transpose(2, 0, 1))
    arrays = dict(x_tok=g["x"], emb_2=g["L0_tok_emb_2"], emb_3=g["L0_tok_emb_3"], emb_4=g["L0_tok_emb_4"],
                  weights=weights, cols=cols, rows=rows, consts=consts, bits_i=bits_i, bits_f=bits_f, w_up=g["L0_ffn_W_up"], b_up=b_up, w_down=w_down)
    nc = bacc.Bacc("TRN2", target_bir_lowering=False, num_devices=1)
    ap = {n: nc.dram_tensor(f"in_{n}", v.shape, mybir.dt.from_np(v.dtype), kind="ExternalInput").ap()
          for n, v in arrays.items()}
    out = nc.dram_tensor("out_h", (B, S, C), F32, kind="ExternalOutput").ap()
    build_program(nc, ap["x_tok"], (ap["emb_2"], ap["emb_3"], ap["emb_4"]), ap["weights"], ap["cols"], ap["rows"],
                  ap["consts"], (ap["bits_i"], ap["bits_f"]), ap["w_up"], ap["b_up"], ap["w_down"], out)
    r = run_bass_kernel_spmd(nc, [{f"in_{n}": v for n, v in arrays.items()}], core_ids=[0])
    return r.results[0]["out_h"]
```
